# Optimizing a Trainium2 kernel written in Bass

```python
import numpy as np
import jax
import jax.numpy as jnp

def _softmax(x, axis=-1):
    return jax.nn.softmax(x, axis=axis)

def _gelu(x):
    return jax.nn.gelu(x, approximate=True)

def _silu(x):
    return jax.nn.silu(x)

def _sigmoid(x):
    return jax.nn.sigmoid(x)

def _layernorm(x, axis=-1, eps=1e-05):
    m = jnp.mean(x, axis=axis, keepdims=True)
    v = jnp.var(x, axis=axis, keepdims=True)
    return (x - m) / jnp.sqrt(v + eps)

def _scatter_add(tgt, idx, src, axis=0):
    return tgt.at[idx].add(src)

def _segment_sum(src, seg, n):
    return jax.ops.segment_sum(src, seg, n)
kernel_name = 'mk_cond_seq_d4_seqx_r4_8f9353'

def setup_inputs(seed: int=0):
    np.random.seed(seed)
    _w = jnp.asarray

    def _rec_inputs():
        import jax
        import jax.numpy as jnp
        _rk = jax.random.key(seed)
        x = 7.22e-05 + 1 * jax.random.normal(jax.random.fold_in(_rk, 1), (8, 512, 256), jnp.float32)
        _lenS = 512 - jax.random.randint(jax.random.fold_in(_rk, 7), (8,), 0, max(1, 512 // 4) + 1, jnp.int32)
        _lenS2 = 512 - jax.random.randint(jax.random.fold_in(_rk, 8), (8,), 0, max(1, 512 // 4) + 1, jnp.int32)
        cond_2048 = 0.00782532 + 1.00527 * jax.random.normal(jax.random.fold_in(_rk, 11), (8, 512), jnp.float32)
        itok_S_0_1023 = jax.random.randint(jax.random.fold_in(_rk, 14), (512,), 0, 256, jnp.int32)
        _validS = jnp.arange(512)[None, :] < _lenS[:, None]
        _validS2 = jnp.arange(512)[None, :] < _lenS2[:, None]
        _causal = jnp.tril(jnp.ones((512, 512), dtype=bool))
        mask_BxSx1_fk1 = jnp.where(jnp.ones((8, 512, 1), dtype=bool), 1.0, 0.0).astype(jnp.float32)
        mask_BxS_ff1 = jnp.where(jnp.ones((8, 512), dtype=bool), 1.0, 0.0).astype(jnp.float32)
        return (x, cond_2048, itok_S_0_1023, mask_BxSx1_fk1, mask_BxS_ff1)
    x, cond_2048, itok_S_0_1023, mask_BxSx1_fk1, mask_BxS_ff1 = _rec_inputs()

    def _L0_cond_setup():
        import jax, jax.numpy as jnp
        import numpy as np
        B, T, D, H, TE = (4, 512, 256, 8, 512)
        EPS = 1e-05

        def _ln(x, w, b):
            m = jnp.mean(x, axis=-1, keepdims=True)
            v = jnp.mean((x - m) ** 2, axis=-1, keepdims=True)
            return (x - m) * jax.lax.rsqrt(v + EPS) * w + b
        key = jax.random.key(seed)
        ks = jax.random.split(key, 16)
        s = 0.02
        inp = {'x': jax.random.normal(ks[0], (B, T, D), jnp.float32), 'emb': jax.random.normal(ks[1], (B, TE), jnp.float32), 'src_mask': (jax.random.uniform(ks[2], (B, T, 1)) > 0.2).astype(jnp.float32), 'num_head': H, 'ln_w': jnp.ones((D,), jnp.float32), 'ln_b': jnp.zeros((D,), jnp.float32), 'Wq': jax.random.normal(ks[3], (D, D), jnp.float32) * s, 'bq': jnp.zeros((D,), jnp.float32), 'Wk': jax.random.normal(ks[4], (D, D), jnp.float32) * s, 'bk': jnp.zeros((D,), jnp.float32), 'Wv': jax.random.normal(ks[5], (D, D), jnp.float32) * s, 'bv': jnp.zeros((D,), jnp.float32), 'W_emb': jax.random.normal(ks[6], (TE, 2 * D), jnp.float32) * s, 'b_emb': jnp.zeros((2 * D,), jnp.float32), 'ln2_w': jnp.ones((D,), jnp.float32), 'ln2_b': jnp.zeros((D,), jnp.float32), 'W_out': jax.random.normal(ks[7], (D, D), jnp.float32) * s, 'b_out': jnp.zeros((D,), jnp.float32)}
        return inp
    _L0_cond_all = _L0_cond_setup()
    _L0_cond_in = {k: v for k, v in _L0_cond_all.items() if k in ('ln_w', 'ln_b', 'Wq', 'bq', 'Wk', 'bk', 'Wv', 'bv', 'W_emb', 'b_emb', 'ln2_w', 'ln2_b', 'W_out', 'b_out')}
    del _L0_cond_all

    def _L1_cond_setup():
        import jax, jax.numpy as jnp
        import numpy as np
        D = 256
        DI = 512
        N = 16
        DT_RANK = 64
        D_CONV = 4
        EPS = 1e-05

        def _layernorm(x, g, b):
            mu = jnp.mean(x, axis=-1, keepdims=True)
            var = jnp.mean((x - mu) ** 2, axis=-1, keepdims=True)
            return (x - mu) * jax.lax.rsqrt(var + EPS) * g + b

        def _mamba(xn, in_proj_w, conv_w, conv_b, x_proj_w, dt_proj_w, dt_proj_b, A_log, D_param, out_proj_w):
            b, sl, _ = xn.shape
            xz = jnp.einsum('bsd,ed->bse', xn, in_proj_w)
            x_in, z = jnp.split(xz, 2, axis=-1)
            xt = jnp.transpose(x_in, (0, 2, 1))
            u = jax.lax.conv_general_dilated(xt, conv_w[:, None, :], (1,), [(D_CONV - 1, 0)], feature_group_count=DI, dimension_numbers=('NCH', 'OIH', 'NCH')) + conv_b[None, :, None]
            u = jax.nn.silu(jnp.transpose(u, (0, 2, 1)))
            x_dbl = jnp.einsum('bsd,ed->bse', u, x_proj_w)
            dt_r, B, C = jnp.split(x_dbl, [DT_RANK, DT_RANK + N], axis=-1)
            dt = jax.nn.softplus(jnp.einsum('bsr,dr->bsd', dt_r, dt_proj_w) + dt_proj_b)
            A = -jnp.exp(A_log)

            def step(h, inp):
                dt_t, B_t, C_t, u_t = inp
                dA = jnp.exp(dt_t[:, :, None] * A)
                h = h * dA + (dt_t * u_t)[:, :, None] * B_t[:, None, :]
                y = jnp.einsum('bdn,bn->bd', h, C_t)
                return (h, y)
            seq = (jnp.transpose(dt, (1, 0, 2)), jnp.transpose(B, (1, 0, 2)), jnp.transpose(C, (1, 0, 2)), jnp.transpose(u, (1, 0, 2)))
            h0 = jnp.zeros((b, DI, N), xn.dtype)
            _, ys = jax.lax.scan(step, h0, seq)
            y = jnp.transpose(ys, (1, 0, 2)) + u * D_param
            y = y * jax.nn.silu(z)
            return jnp.einsum('bsd,ed->bse', y, out_proj_w)
        key = jax.random.key(seed)
        ks = jax.random.split(key, 16)
        s = lambda fan: 1.0 / np.sqrt(fan)
        inp = {'x': jax.random.normal(ks[0], (2, 512, D), jnp.float32), 'c': jax.random.normal(ks[1], (2, 2 * D), jnp.float32), 'ln_g': jnp.ones((D,), jnp.float32), 'ln_b': jnp.zeros((D,), jnp.float32), 'ada_w': jax.random.normal(ks[2], (3 * D, 2 * D), jnp.float32) * s(2 * D), 'ada_b': jnp.zeros((3 * D,), jnp.float32), 'in_proj_w': jax.random.normal(ks[3], (2 * DI, D), jnp.float32) * s(D), 'conv_w': jax.random.normal(ks[4], (DI, D_CONV), jnp.float32) * s(D_CONV), 'conv_b': jnp.zeros((DI,), jnp.float32), 'x_proj_w': jax.random.normal(ks[5], (DT_RANK + 2 * N, DI), jnp.float32) * s(DI), 'dt_proj_w': jax.random.normal(ks[6], (DI, DT_RANK), jnp.float32) * s(DT_RANK), 'dt_proj_b': jax.random.uniform(ks[7], (DI,), jnp.float32, -4.0, -2.0), 'A_log': jnp.tile(jnp.log(jnp.arange(1, N + 1, dtype=jnp.float32)), (DI, 1)), 'D_param': jnp.ones((DI,), jnp.float32), 'out_proj_w': jax.random.normal(ks[8], (D, DI), jnp.float32) * s(DI)}
        return inp
    _L1_cond_all = _L1_cond_setup()
    _L1_cond_in = {k: v for k, v in _L1_cond_all.items() if k in ('ln_g', 'ln_b', 'ada_w', 'ada_b', 'in_proj_w', 'conv_w', 'conv_b', 'x_proj_w', 'dt_proj_w', 'dt_proj_b', 'A_log', 'D_param', 'out_proj_w')}
    del _L1_cond_all

    def _L2_cond_setup():
        import jax, jax.numpy as jnp
        import numpy as np
        B, T, D, H, TE = (8, 256, 256, 16, 512)
        LN_EPS = 1e-05

        def layer_norm(x, w, b):
            m = jnp.mean(x, axis=-1, keepdims=True)
            v = jnp.var(x, axis=-1, keepdims=True)
            return (x - m) / jnp.sqrt(v + LN_EPS) * w + b
        key = jax.random.key(seed)
        ks = jax.random.split(key, 8)
        s = lambda k, sh: jax.random.normal(k, sh, jnp.float32) * 0.02
        return dict(x=jax.random.normal(ks[0], (B, T, D), jnp.float32), emb=jax.random.normal(ks[1], (B, TE), jnp.float32), src_mask=jnp.ones((B, T), jnp.float32), norm_w=jnp.ones((D,), jnp.float32), norm_b=jnp.zeros((D,), jnp.float32), q_w=s(ks[2], (D, D)), q_b=jnp.zeros((D,), jnp.float32), k_w=s(ks[3], (D, D)), k_b=jnp.zeros((D,), jnp.float32), v_w=s(ks[4], (D, D)), v_b=jnp.zeros((D,), jnp.float32), emb_w=s(ks[5], (TE, 2 * D)), emb_b=jnp.zeros((2 * D,), jnp.float32), sb_norm_w=jnp.ones((D,), jnp.float32), sb_norm_b=jnp.zeros((D,), jnp.float32), out_w=s(ks[6], (D, D)), out_b=jnp.zeros((D,), jnp.float32))
    _L2_cond_all = _L2_cond_setup()
    _L2_cond_in = {k: v for k, v in _L2_cond_all.items() if k in ('norm_w', 'norm_b', 'q_w', 'q_b', 'k_w', 'k_b', 'v_w', 'v_b', 'emb_w', 'emb_b', 'sb_norm_w', 'sb_norm_b', 'out_w', 'out_b')}
    del _L2_cond_all

    def _L3_cond_setup():
        import jax, jax.numpy as jnp
        import numpy as np
        B_SZ, S, D = (4, 256, 256)
        DI, DS, DTR, DC = (512, 16, 64, 4)
        EPS = 1e-05

        def _layernorm(x, g, b):
            m = jnp.mean(x, axis=-1, keepdims=True)
            v = jnp.var(x, axis=-1, keepdims=True)
            return (x - m) * jax.lax.rsqrt(v + EPS) * g + b

        def _mamba(h, W_in, conv_w, conv_b, W_xp, W_dt, b_dt, A_log, D_param, W_out):
            bsz = h.shape[0]
            xz = h @ W_in
            xm, z = jnp.split(xz, 2, axis=-1)
            xc = jnp.transpose(xm, (0, 2, 1))
            xc = jax.lax.conv_general_dilated(xc, conv_w, (1,), [(DC - 1, 0)], feature_group_count=DI, dimension_numbers=('NCH', 'OIH', 'NCH'))
            xc = xc + conv_b[None, :, None]
            xm = jax.nn.silu(jnp.transpose(xc, (0, 2, 1)))
            xdbl = xm @ W_xp
            dtr, Bm, Cm = jnp.split(xdbl, [DTR, DTR + DS], axis=-1)
            dt = jax.nn.softplus(dtr @ W_dt + b_dt)
            A = -jnp.exp(A_log)

            def step(hst, inp):
                dt_t, B_t, C_t, x_t = inp
                dA = jnp.exp(dt_t[:, :, None] * A)
                hst = hst * dA + (dt_t * x_t)[:, :, None] * B_t[:, None, :]
                y = jnp.einsum('bds,bs->bd', hst, C_t)
                return (hst, y)
            inputs = (jnp.transpose(dt, (1, 0, 2)), jnp.transpose(Bm, (1, 0, 2)), jnp.transpose(Cm, (1, 0, 2)), jnp.transpose(xm, (1, 0, 2)))
            h0 = jnp.zeros((bsz, DI, DS), dt.dtype)
            _, ys = jax.lax.scan(step, h0, inputs)
            y = jnp.transpose(ys, (1, 0, 2)) + xm * D_param
            y = y * jax.nn.silu(z)
            return y @ W_out
        key = jax.random.key(seed)
        ks = jax.random.split(key, 12)

        def w(k, shape, scale=0.02):
            return jax.random.normal(k, shape, jnp.float32) * scale
        x = jax.random.normal(ks[0], (B_SZ, S, D), jnp.float32)
        c = jax.random.normal(ks[1], (B_SZ, 2 * D), jnp.float32)
        W_ada = w(ks[2], (2 * D, 3 * D))
        b_ada = jnp.zeros((3 * D,), jnp.float32)
        gamma = jnp.ones((D,), jnp.float32)
        beta = jnp.zeros((D,), jnp.float32)
        W_in = w(ks[3], (D, 2 * DI))
        conv_w = w(ks[4], (DI, 1, DC), 0.1)
        conv_b = jnp.zeros((DI,), jnp.float32)
        W_xp = w(ks[5], (DI, DTR + 2 * DS))
        W_dt = w(ks[6], (DTR, DI))
        b_dt = jnp.full((DI,), jnp.log(jnp.expm1(jnp.float32(0.01))), jnp.float32)
        A_log = jnp.log(jnp.broadcast_to(jnp.arange(1, DS + 1, dtype=jnp.float32), (DI, DS)))
        D_param = jnp.ones((DI,), jnp.float32)
        W_out = w(ks[7], (DI, D))
        perm = jax.random.permutation(ks[8], S)
        inv_perm = jnp.argsort(perm)
        return dict(x=x, c=c, W_ada=W_ada, b_ada=b_ada, gamma=gamma, beta=beta, W_in=W_in, conv_w=conv_w, conv_b=conv_b, W_xp=W_xp, W_dt=W_dt, b_dt=b_dt, A_log=A_log, D_param=D_param, W_out=W_out, perm=perm, inv_perm=inv_perm)
    _L3_cond_all = _L3_cond_setup()
    _L3_cond_in = {k: v for k, v in _L3_cond_all.items() if k in ('W_ada', 'b_ada', 'gamma', 'beta', 'W_in', 'conv_w', 'conv_b', 'W_xp', 'W_dt', 'b_dt', 'A_log', 'D_param', 'W_out')}
    del _L3_cond_all
    return {'x': x, 'cond_2048': cond_2048, 'itok_S_0_1023': itok_S_0_1023, 'mask_BxSx1_fk1': mask_BxSx1_fk1, 'mask_BxS_ff1': mask_BxS_ff1, 'L0_cond_ln_w': _L0_cond_in['ln_w'], 'L0_cond_ln_b': _L0_cond_in['ln_b'], 'L0_cond_Wq': _L0_cond_in['Wq'], 'L0_cond_bq': _L0_cond_in['bq'], 'L0_cond_Wk': _L0_cond_in['Wk'], 'L0_cond_bk': _L0_cond_in['bk'], 'L0_cond_Wv': _L0_cond_in['Wv'], 'L0_cond_bv': _L0_cond_in['bv'], 'L0_cond_W_emb': _L0_cond_in['W_emb'], 'L0_cond_b_emb': _L0_cond_in['b_emb'], 'L0_cond_ln2_w': _L0_cond_in['ln2_w'], 'L0_cond_ln2_b': _L0_cond_in['ln2_b'], 'L0_cond_W_out': _L0_cond_in['W_out'], 'L0_cond_b_out': _L0_cond_in['b_out'], 'L1_cond_ln_g': _L1_cond_in['ln_g'], 'L1_cond_ln_b': _L1_cond_in['ln_b'], 'L1_cond_ada_w': _L1_cond_in['ada_w'], 'L1_cond_ada_b': _L1_cond_in['ada_b'], 'L1_cond_in_proj_w': _L1_cond_in['in_proj_w'], 'L1_cond_conv_w': _L1_cond_in['conv_w'], 'L1_cond_conv_b': _L1_cond_in['conv_b'], 'L1_cond_x_proj_w': _L1_cond_in['x_proj_w'], 'L1_cond_dt_proj_w': _L1_cond_in['dt_proj_w'], 'L1_cond_dt_proj_b': _L1_cond_in['dt_proj_b'], 'L1_cond_A_log': _L1_cond_in['A_log'], 'L1_cond_D_param': _L1_cond_in['D_param'], 'L1_cond_out_proj_w': _L1_cond_in['out_proj_w'], 'L2_cond_norm_w': _L2_cond_in['norm_w'], 'L2_cond_norm_b': _L2_cond_in['norm_b'], 'L2_cond_q_w': _L2_cond_in['q_w'], 'L2_cond_q_b': _L2_cond_in['q_b'], 'L2_cond_k_w': _L2_cond_in['k_w'], 'L2_cond_k_b': _L2_cond_in['k_b'], 'L2_cond_v_w': _L2_cond_in['v_w'], 'L2_cond_v_b': _L2_cond_in['v_b'], 'L2_cond_emb_w': _L2_cond_in['emb_w'], 'L2_cond_emb_b': _L2_cond_in['emb_b'], 'L2_cond_sb_norm_w': _L2_cond_in['sb_norm_w'], 'L2_cond_sb_norm_b': _L2_cond_in['sb_norm_b'], 'L2_cond_out_w': _L2_cond_in['out_w'], 'L2_cond_out_b': _L2_cond_in['out_b'], 'L3_cond_W_ada': _L3_cond_in['W_ada'], 'L3_cond_b_ada': _L3_cond_in['b_ada'], 'L3_cond_gamma': _L3_cond_in['gamma'], 'L3_cond_beta': _L3_cond_in['beta'], 'L3_cond_W_in': _L3_cond_in['W_in'], 'L3_cond_conv_w': _L3_cond_in['conv_w'], 'L3_cond_conv_b': _L3_cond_in['conv_b'], 'L3_cond_W_xp': _L3_cond_in['W_xp'], 'L3_cond_W_dt': _L3_cond_in['W_dt'], 'L3_cond_b_dt': _L3_cond_in['b_dt'], 'L3_cond_A_log': _L3_cond_in['A_log'], 'L3_cond_D_param': _L3_cond_in['D_param'], 'L3_cond_W_out': _L3_cond_in['W_out']}

def reference(x, cond_2048, itok_S_0_1023, mask_BxSx1_fk1, mask_BxS_ff1, L0_cond_ln_w, L0_cond_ln_b, L0_cond_Wq, L0_cond_bq, L0_cond_Wk, L0_cond_bk, L0_cond_Wv, L0_cond_bv, L0_cond_W_emb, L0_cond_b_emb, L0_cond_ln2_w, L0_cond_ln2_b, L0_cond_W_out, L0_cond_b_out, L1_cond_ln_g, L1_cond_ln_b, L1_cond_ada_w, L1_cond_ada_b, L1_cond_in_proj_w, L1_cond_conv_w, L1_cond_conv_b, L1_cond_x_proj_w, L1_cond_dt_proj_w, L1_cond_dt_proj_b, L1_cond_A_log, L1_cond_D_param, L1_cond_out_proj_w, L2_cond_norm_w, L2_cond_norm_b, L2_cond_q_w, L2_cond_q_b, L2_cond_k_w, L2_cond_k_b, L2_cond_v_w, L2_cond_v_b, L2_cond_emb_w, L2_cond_emb_b, L2_cond_sb_norm_w, L2_cond_sb_norm_b, L2_cond_out_w, L2_cond_out_b, L3_cond_W_ada, L3_cond_b_ada, L3_cond_gamma, L3_cond_beta, L3_cond_W_in, L3_cond_conv_w, L3_cond_conv_b, L3_cond_W_xp, L3_cond_W_dt, L3_cond_b_dt, L3_cond_A_log, L3_cond_D_param, L3_cond_W_out):
    import jax
    import jax.numpy as jnp

    def _L0_cond_ref(x, emb, src_mask, num_head, ln_w, ln_b, Wq, bq, Wk, bk, Wv, bv, W_emb, b_emb, ln2_w, ln2_b, W_out, b_out):
        import jax, jax.numpy as jnp
        import numpy as np
        B, T, D, H, TE = (4, 512, 256, 8, 512)
        EPS = 1e-05

        def _ln(x, w, b):
            m = jnp.mean(x, axis=-1, keepdims=True)
            v = jnp.mean((x - m) ** 2, axis=-1, keepdims=True)
            return (x - m) * jax.lax.rsqrt(v + EPS) * w + b
        b, t, d = x.shape
        h = num_head
        dh = d // h
        xn = _ln(x, ln_w, ln_b)
        q = xn @ Wq + bq
        k = xn @ Wk + bk + (1.0 - src_mask) * -1000000.0
        q = jax.nn.softmax(q.reshape(b, t, h, dh), axis=-1)
        k = jax.nn.softmax(k.reshape(b, t, h, dh), axis=1)
        v = ((xn @ Wv + bv) * src_mask).reshape(b, t, h, dh)
        att = jnp.einsum('bnhd,bnhl->bhdl', k, v)
        y = jnp.einsum('bnhd,bhdl->bnhl', q, att).reshape(b, t, d)
        emb_out = (jax.nn.silu(emb) @ W_emb + b_emb)[:, None, :]
        scale, shift = jnp.split(emb_out, 2, axis=2)
        hh = _ln(y, ln2_w, ln2_b) * (1.0 + scale) + shift
        hh = jax.nn.silu(hh) @ W_out + b_out
        return x + hh

    def _L1_cond_ref(x, c, ln_g, ln_b, ada_w, ada_b, in_proj_w, conv_w, conv_b, x_proj_w, dt_proj_w, dt_proj_b, A_log, D_param, out_proj_w):
        import jax, jax.numpy as jnp
        import numpy as np
        D = 256
        DI = 512
        N = 16
        DT_RANK = 64
        D_CONV = 4
        EPS = 1e-05

        def _layernorm(x, g, b):
            mu = jnp.mean(x, axis=-1, keepdims=True)
            var = jnp.mean((x - mu) ** 2, axis=-1, keepdims=True)
            return (x - mu) * jax.lax.rsqrt(var + EPS) * g + b

        def _mamba(xn, in_proj_w, conv_w, conv_b, x_proj_w, dt_proj_w, dt_proj_b, A_log, D_param, out_proj_w):
            b, sl, _ = xn.shape
            xz = jnp.einsum('bsd,ed->bse', xn, in_proj_w)
            x_in, z = jnp.split(xz, 2, axis=-1)
            xt = jnp.transpose(x_in, (0, 2, 1))
            u = jax.lax.conv_general_dilated(xt, conv_w[:, None, :], (1,), [(D_CONV - 1, 0)], feature_group_count=DI, dimension_numbers=('NCH', 'OIH', 'NCH')) + conv_b[None, :, None]
            u = jax.nn.silu(jnp.transpose(u, (0, 2, 1)))
            x_dbl = jnp.einsum('bsd,ed->bse', u, x_proj_w)
            dt_r, B, C = jnp.split(x_dbl, [DT_RANK, DT_RANK + N], axis=-1)
            dt = jax.nn.softplus(jnp.einsum('bsr,dr->bsd', dt_r, dt_proj_w) + dt_proj_b)
            A = -jnp.exp(A_log)

            def step(h, inp):
                dt_t, B_t, C_t, u_t = inp
                dA = jnp.exp(dt_t[:, :, None] * A)
                h = h * dA + (dt_t * u_t)[:, :, None] * B_t[:, None, :]
                y = jnp.einsum('bdn,bn->bd', h, C_t)
                return (h, y)
            seq = (jnp.transpose(dt, (1, 0, 2)), jnp.transpose(B, (1, 0, 2)), jnp.transpose(C, (1, 0, 2)), jnp.transpose(u, (1, 0, 2)))
            h0 = jnp.zeros((b, DI, N), xn.dtype)
            _, ys = jax.lax.scan(step, h0, seq)
            y = jnp.transpose(ys, (1, 0, 2)) + u * D_param
            y = y * jax.nn.silu(z)
            return jnp.einsum('bsd,ed->bse', y, out_proj_w)
        ada = jnp.einsum('bc,ec->be', jax.nn.silu(c), ada_w) + ada_b
        shift, scale, gate = jnp.split(ada, 3, axis=1)
        xn = _layernorm(x, ln_g, ln_b)
        xn = xn * (1.0 + scale[:, None, :]) + shift[:, None, :]
        x_ssm = _mamba(xn, in_proj_w, conv_w, conv_b, x_proj_w, dt_proj_w, dt_proj_b, A_log, D_param, out_proj_w)
        return x + gate[:, None, :] * x_ssm

    def _L2_cond_ref(x, emb, src_mask, norm_w, norm_b, q_w, q_b, k_w, k_b, v_w, v_b, emb_w, emb_b, sb_norm_w, sb_norm_b, out_w, out_b):
        import jax, jax.numpy as jnp
        import numpy as np
        B, T, D, H, TE = (8, 256, 256, 16, 512)
        LN_EPS = 1e-05

        def layer_norm(x, w, b):
            m = jnp.mean(x, axis=-1, keepdims=True)
            v = jnp.var(x, axis=-1, keepdims=True)
            return (x - m) / jnp.sqrt(v + LN_EPS) * w + b
        Bx, Tx, Dx = x.shape
        xn = layer_norm(x, norm_w, norm_b)
        q = (xn @ q_w + q_b).reshape(Bx, Tx, H, -1)
        k = (xn @ k_w + k_b).reshape(Bx, Tx, H, -1)
        att = jnp.einsum('bnhl,bmhl->bnmh', q, k)
        mask = src_mask.reshape(Bx, 1, Tx, 1)
        att = att + (1.0 - mask) * -1000000.0
        att = jax.nn.softmax(att, axis=2)
        v = ((xn @ v_w + v_b) * src_mask[:, :, None]).reshape(Bx, Tx, H, -1)
        y = jnp.einsum('bnmh,bmhl->bnhl', att, v).reshape(Bx, Tx, Dx)
        e = jax.nn.silu(emb) @ emb_w + emb_b
        scale, shift = jnp.split(e[:, None, :], 2, axis=2)
        h = layer_norm(y, sb_norm_w, sb_norm_b) * (1.0 + scale) + shift
        h = jax.nn.silu(h) @ out_w + out_b
        return x + h

    def _L3_cond_ref(x, c, W_ada, b_ada, gamma, beta, W_in, conv_w, conv_b, W_xp, W_dt, b_dt, A_log, D_param, W_out, perm, inv_perm):
        import jax, jax.numpy as jnp
        import numpy as np
        B_SZ, S, D = (4, 256, 256)
        DI, DS, DTR, DC = (512, 16, 64, 4)
        EPS = 1e-05

        def _layernorm(x, g, b):
            m = jnp.mean(x, axis=-1, keepdims=True)
            v = jnp.var(x, axis=-1, keepdims=True)
            return (x - m) * jax.lax.rsqrt(v + EPS) * g + b

        def _mamba(h, W_in, conv_w, conv_b, W_xp, W_dt, b_dt, A_log, D_param, W_out):
            bsz = h.shape[0]
            xz = h @ W_in
            xm, z = jnp.split(xz, 2, axis=-1)
            xc = jnp.transpose(xm, (0, 2, 1))
            xc = jax.lax.conv_general_dilated(xc, conv_w, (1,), [(DC - 1, 0)], feature_group_count=DI, dimension_numbers=('NCH', 'OIH', 'NCH'))
            xc = xc + conv_b[None, :, None]
            xm = jax.nn.silu(jnp.transpose(xc, (0, 2, 1)))
            xdbl = xm @ W_xp
            dtr, Bm, Cm = jnp.split(xdbl, [DTR, DTR + DS], axis=-1)
            dt = jax.nn.softplus(dtr @ W_dt + b_dt)
            A = -jnp.exp(A_log)

            def step(hst, inp):
                dt_t, B_t, C_t, x_t = inp
                dA = jnp.exp(dt_t[:, :, None] * A)
                hst = hst * dA + (dt_t * x_t)[:, :, None] * B_t[:, None, :]
                y = jnp.einsum('bds,bs->bd', hst, C_t)
                return (hst, y)
            inputs = (jnp.transpose(dt, (1, 0, 2)), jnp.transpose(Bm, (1, 0, 2)), jnp.transpose(Cm, (1, 0, 2)), jnp.transpose(xm, (1, 0, 2)))
            h0 = jnp.zeros((bsz, DI, DS), dt.dtype)
            _, ys = jax.lax.scan(step, h0, inputs)
            y = jnp.transpose(ys, (1, 0, 2)) + xm * D_param
            y = y * jax.nn.silu(z)
            return y @ W_out
        mod = jax.nn.silu(c) @ W_ada + b_ada
        shift, scale, gate = jnp.split(mod, 3, axis=1)
        h = _layernorm(x, gamma, beta)
        h = h * (1.0 + scale[:, None, :]) + shift[:, None, :]
        h = h[:, perm]
        y = _mamba(h, W_in, conv_w, conv_b, W_xp, W_dt, b_dt, A_log, D_param, W_out)
        y = y[:, inv_perm]
        return x + gate[:, None, :] * y
    x = _L0_cond_ref(x, cond_2048, mask_BxSx1_fk1, 8, L0_cond_ln_w, L0_cond_ln_b, L0_cond_Wq, L0_cond_bq, L0_cond_Wk, L0_cond_bk, L0_cond_Wv, L0_cond_bv, L0_cond_W_emb, L0_cond_b_emb, L0_cond_ln2_w, L0_cond_ln2_b, L0_cond_W_out, L0_cond_b_out)
    x = _L1_cond_ref(x, cond_2048, L1_cond_ln_g, L1_cond_ln_b, L1_cond_ada_w, L1_cond_ada_b, L1_cond_in_proj_w, L1_cond_conv_w, L1_cond_conv_b, L1_cond_x_proj_w, L1_cond_dt_proj_w, L1_cond_dt_proj_b, L1_cond_A_log, L1_cond_D_param, L1_cond_out_proj_w)
    x = _L2_cond_ref(x, cond_2048, mask_BxS_ff1, L2_cond_norm_w, L2_cond_norm_b, L2_cond_q_w, L2_cond_q_b, L2_cond_k_w, L2_cond_k_b, L2_cond_v_w, L2_cond_v_b, L2_cond_emb_w, L2_cond_emb_b, L2_cond_sb_norm_w, L2_cond_sb_norm_b, L2_cond_out_w, L2_cond_out_b)
    x = _L3_cond_ref(x, cond_2048, L3_cond_W_ada, L3_cond_b_ada, L3_cond_gamma, L3_cond_beta, L3_cond_W_in, L3_cond_conv_w, L3_cond_conv_b, L3_cond_W_xp, L3_cond_W_dt, L3_cond_b_dt, L3_cond_A_log, L3_cond_D_param, L3_cond_W_out, itok_S_0_1023, itok_S_0_1023)
    return x

_drawn_inputs = setup_inputs


def setup_inputs(seed=0):
    import zlib

    import numpy as np

    out = dict(_drawn_inputs(seed))
    spreads = {'L0_cond_ln_w': (1.0, 0.2),
     'L0_cond_ln_b': (0.0, 0.1),
     'L0_cond_bq': (0.0, 0.1),
     'L0_cond_bk': (0.0, 0.1),
     'L0_cond_bv': (0.0, 0.1),
     'L0_cond_b_emb': (0.0, 0.1),
     'L0_cond_ln2_w': (1.0, 0.2),
     'L0_cond_ln2_b': (0.0, 0.1),
     'L0_cond_b_out': (0.0, 0.1),
     'L1_cond_ln_g': (1.0, 0.2),
     'L1_cond_ln_b': (0.0, 0.1),
     'L1_cond_ada_b': (0.0, 0.1),
     'L1_cond_conv_b': (0.0, 0.1),
     'L1_cond_D_param': (1.0, 0.2),
     'L2_cond_norm_w': (1.0, 0.2),
     'L2_cond_norm_b': (0.0, 0.1),
     'L2_cond_q_b': (0.0, 0.1),
     'L2_cond_k_b': (0.0, 0.1),
     'L2_cond_v_b': (0.0, 0.1),
     'L2_cond_emb_b': (0.0, 0.1),
     'L2_cond_sb_norm_w': (1.0, 0.2),
     'L2_cond_sb_norm_b': (0.0, 0.1),
     'L2_cond_out_b': (0.0, 0.1),
     'L3_cond_b_ada': (0.0, 0.1),
     'L3_cond_gamma': (1.0, 0.2),
     'L3_cond_beta': (0.0, 0.1),
     'L3_cond_conv_b': (0.0, 0.1),
     'L3_cond_b_dt': (-4.600166320800781, 0.2),
     'L3_cond_D_param': (1.0, 0.2)}
    factors = {}
    for name, (base, spread) in spreads.items():
        noise = np.random.default_rng([zlib.crc32(name.encode()), seed]).standard_normal(out[name].shape)
        drawn = base * np.exp(spread * noise) if base else spread * noise
        out[name] = jnp.asarray(drawn.astype(out[name].dtype))
    for name, factor in factors.items():
        out[name] = (out[name] * factor).astype(out[name].dtype)
    return out
```

```python
from contextlib import ExitStack

import numpy as np

import concourse.bass as bass
from concourse import mybir

F32 = mybir.dt.float32
I32 = mybir.dt.int32
ALU = mybir.AluOpType
ACT = mybir.ActivationFunctionType
AX = mybir.AxisListType

P = 128
B, T, D = 8, 512, 256
TB = T // P
DH = D // P
TE = 512
KE = TE // P
H0 = 8
W0 = D // H0
H2 = 16
W2 = D // H2
DI = 512
JB = DI // P
N = 16
R = 64
XD = R + 2 * N
TAPS = 4
EPS = 1e-5
MASKED = 1000000.0

VEC_LAYOUT = {}
_at = 0
for _name, _n in (
    [("L0_ln_w", DH), ("L0_ln_b", DH), ("L0_ln2_w", DH), ("L0_ln2_b", DH), ("L0_scale_b", DH), ("L0_shift_b", DH),
     ("L2_ln_w", DH), ("L2_ln_b", DH), ("L2_ln2_w", DH), ("L2_ln2_b", DH), ("L2_scale_b", DH), ("L2_shift_b", DH),
     ("L2_q_bias", 4), ("L2_k_bias", 4)]
    + [(f"L{l}_{n}", c) for l in (1, 3) for n, c in (
        ("ln_w", DH), ("ln_b", DH), ("shift_b", DH), ("scale_b", DH), ("conv_b", JB), ("dt_b", JB),
        ("D", JB), ("conv_w", JB * TAPS), ("A_log", JB * N))]
):
    VEC_LAYOUT[_name] = (_at, _n)
    _at += _n
NVEC = _at
ROWS = ["L0_bq", "L0_bk", "L0_bv", "L0_b_out", "L2_bv", "L2_b_out", "L1_gate_b", "L3_gate_b"]
COND_AT = {"L0": 0, "L2": 2 * D, "L1": 4 * D, "L3": 7 * D}
COND_W = 10 * D
STYLE = ("L0", "L1", "L2", "L3")


def vec(tile, name):
    a, n = VEC_LAYOUT[name]
    return tile[:, a:a + n]


class Chain:

    def __init__(self, eng, sem, per, b):
        self.eng, self.sem, self.per, self.base, self.n = eng, sem, per, b * per, 0

    def link(self, ins):
        ins.then_inc(self.sem, 1)
        self.n += 1
        self.eng.wait_ge(self.sem, self.base + self.n)

    def end(self):
        assert self.n == self.per, (self.n, self.per)


class Semaphores:

    def __init__(self, nc, ctx):
        self.nc, self.ctx, self.all = nc, ctx, []

    def __call__(self, name):
        self.all.append(self.ctx.enter_context(self.nc.semaphore(name)))
        return self.all[-1]

    def clear(self, name):
        with self.nc.Block(name) as block:
            @block.sync
            def _(sp):
                for s in self.all:
                    sp.sem_clear(s)


def setup_block(nc, io, keep):
    with ExitStack() as ctx:
        sb = lambda name, shape: ctx.enter_context(nc.sbuf_tensor(name, shape, F32))
        sems = Semaphores(nc, ctx)
        sem = lambda name: sems(name)
        cond_w = sb("su_cond_w", [P, KE, COND_W])
        cond_t = sb("su_cond_t", [P, KE, B])
        silu_c = sb("su_silu_c", [P, KE, B])
        raw = sb("su_raw", [P, 4, 2 * DH, B])
        one_b = sb("su_one_b", [1, B])
        gates = sb("su_gates", [B, 2, D])
        bias2 = sb("su_bias2", [P, 4, 2 * DH, B])
        ps = ctx.enter_context(nc.psum_tensor("su_ps", [P, 4, 2 * DH * B], F32))
        ps_gate = ctx.enter_context(nc.psum_tensor("su_ps_gate", [P, 2, D], F32))
        vecs, rows, ident, ones, eps, coef = (keep[k] for k in ("vecs", "rows", "ident", "ones", "eps", "coef"))
        loaded, weights_in, filled, diag_done = sem("su_loaded"), sem("su_weights_in"), sem("su_filled"), sem("su_diag")
        silu_done, mm_done, gate_mm, gate_out, stored, steps = (
            sem("su_silu"), sem("su_mm"), sem("su_gate_mm"), sem("su_gate_out"), sem("su_stored"), sem("su_steps"))

        with nc.Block("setup") as block:
            @block.sync
            def _(sp):
                sp.dma_start(cond_t[:], io["cond_t"]).then_inc(loaded, 16)
                sp.dma_start(vecs[:], io["vecs"]).then_inc(loaded, 16)
                sp.dma_start(rows[:], io["rows"]).then_inc(loaded, 16)
                sp.dma_start(cond_w[:], io["cond_w"]).then_inc(weights_in, 16)
                sp.wait_ge(gate_out, 1)
                sp.dma_start(io["gates"].rearrange("l b d -> b l d"), gates[:]).then_inc(stored, 16)
                sp.wait_ge(stored, 16)

            @block.gpsimd
            def _(pool):
                pool.memset(ident[:], 0.0).then_inc(filled, 1)
                pool.memset(ones[:], 1.0).then_inc(filled, 1)
                pool.memset(eps[:], EPS).then_inc(filled, 1)
                pool.memset(one_b[:], 1.0).then_inc(filled, 1)
                pool.wait_ge(filled, 4)
                pool.affine_select(out=ident[:], in_=ident[:], compare_op=ALU.not_equal, fill=1.0, base=0,
                                   pattern=[[-1, P]], channel_multiplier=1).then_inc(diag_done, 1)

            @block.scalar
            def _(act):
                act.wait_ge(loaded, 48)
                act.activation(silu_c[:], cond_t[:], ACT.Silu).then_inc(silu_done, 1)

            @block.tensor
            def _(pe):
                pe.wait_ge(silu_done, 1)
                pe.wait_ge(weights_in, 16)
                pe.wait_ge(filled, 4)
                for l, name in enumerate(STYLE):
                    for part in range(2 * DH):
                        first = part if name in ("L0", "L2") else (part + DH) % (2 * DH)
                        c = COND_AT[name] + first * P
                        for k in range(KE):
                            last = pe.matmul(ps[:, l, part * B:(part + 1) * B], cond_w[:, k, c:c + P], silu_c[:, k, :],
                                             start=(k == 0), stop=(k == KE - 1))
                last.then_inc(mm_done, 1)
                for l, name in enumerate(("L1", "L3")):
                    c = COND_AT[name] + 2 * D
                    for k in range(KE):
                        pe.matmul(ps_gate[0:B, l, :], silu_c[:, k, :], cond_w[:, k, c:c + D], start=(k == 0), stop=False)
                    r = ROWS.index(name + "_gate_b")
                    last = pe.matmul(ps_gate[0:B, l, :], one_b[:], rows[:, r * D:(r + 1) * D], start=False, stop=True)
                last.then_inc(gate_mm, 1)

            @block.vector
            def _(dve):
                chain = Chain(dve, steps, 12, 0)
                dve.wait_ge(loaded, 48)
                dve.wait_ge(mm_done, 1)
                for l, name in enumerate(STYLE):
                    two = "2" if name in ("L0", "L2") else ""
                    bias = vecs[:, VEC_LAYOUT[name + "_scale_b"][0]:VEC_LAYOUT[name + "_scale_b"][0] + DH]
                    sbias = vecs[:, VEC_LAYOUT[name + "_shift_b"][0]:VEC_LAYOUT[name + "_shift_b"][0] + DH]
                    w, bb = vec(vecs, f"{name}_ln{two}_w"), vec(vecs, f"{name}_ln{two}_b")
                    v = ps[:, l, :].rearrange("p (q b) -> p q b", b=B)
                    for h in range(DH):
                        last = dve.tensor_scalar(raw[:, l, h, :], v[:, h, :], bias[:, h:h + 1], 1.0, ALU.add, ALU.add)
                    chain.link(last)
                    for h in range(DH):
                        dve.tensor_scalar(raw[:, l, DH + h, :], v[:, DH + h, :], sbias[:, h:h + 1], None, ALU.add)
                        dve.tensor_scalar(coef[:, l, 0, h, :], raw[:, l, h, :], w[:, h:h + 1], None, ALU.mult)
                        last = dve.tensor_scalar(bias2[:, l, h, :], raw[:, l, h, :], bb[:, h:h + 1], None, ALU.mult)
                    chain.link(last)
                    for h in range(DH):
                        last = dve.tensor_tensor(coef[:, l, 1, h, :], bias2[:, l, h, :], raw[:, l, DH + h, :], ALU.add)
                    chain.link(last)
                chain.end()
                dve.wait_ge(gate_mm, 1)
                dve.tensor_copy(gates[:], ps_gate[0:B, :, :]).then_inc(gate_out, 1)
        sems.clear("setup_clear")


def linear_attention(nc, io, keep):
    with ExitStack() as ctx:
        sb = lambda name, shape: ctx.enter_context(nc.sbuf_tensor("l0_" + name, shape, F32))
        sems = Semaphores(nc, ctx)
        sem = lambda name: sems("l0_" + name)
        pb = lambda name: ctx.enter_context(nc.psum_tensor("l0_" + name, [P, 2, T], F32))
        vecs, rows, ident, ones, eps, coef = (keep[k] for k in ("vecs", "rows", "ident", "ones", "eps", "coef"))
        w = sb("w", [P, DH, 4 * D])
        wq, wk, wv, wo = (w[:, :, i * D:(i + 1) * D] for i in range(4))
        mask_t = sb("mask_t", [P, B, TB])
        mask_row = sb("mask_row", [1, 2, T])
        mask_add = sb("mask_add", [1, 2, T])
        heads = sb("heads", [P, P])
        x_in = sb("x_in", [P, 2, TB, D])
        xn = sb("xn", [P, TB, D])
        xnT = sb("xnT", [P, DH, T])
        stats, moments, rstd = sb("stats", [P, TB, 6]), sb("moments", [P, TB, 2]), sb("rstd", [P, TB])
        stats2, moments2, rstd2 = sb("stats2", [P, TB, 6]), sb("moments2", [P, TB, 2]), sb("rstd2", [P, TB])
        q = sb("q", [P, TB * D])
        q_max, q_sum = sb("q_max", [P, TB * H0]), sb("q_sum", [P, TB * H0])
        k_exp = sb("k_exp", [P, DH, T])
        k_max, k_sum = sb("k_max", [P, DH]), sb("k_sum", [P, DH])
        k_tok = sb("k_tok", [P, TB, D])
        v = sb("v", [P, TB, D])
        qT = sb("qT", [P, DH, T])
        att = sb("att", [P, DH, P])
        yn = sb("yn", [P, TB, D])
        hT = sb("hT", [P, DH, T])
        res = sb("res", [P, 2, TB, D])
        ps_t, ps_q, ps_k, ps_v = pb("ps_t"), pb("ps_q"), pb("ps_k"), pb("ps_v")

        w_in, x_ld, mask_ld, heads_ok, stored = sem("w_in"), [sem("x_ld_even"), sem("x_ld_odd")], [sem("mask_ld_even"), sem("mask_ld_odd")], sem("heads_ok"), [sem("stored_even"), sem("stored_odd")]
        moments_ok, rstd_ok, xn_ok, xn_tr, xnT_ok, madd_ok = (
            sem("moments"), sem("rstd"), sem("xn"), sem("xn_tr"), sem("xnT"), sem("madd"))
        q_mm, k_mm, v_mm, q_sub, q_exp, q_ok, kmax_ok, kexp_ok, k_tr, ktok_ok, v_ok, rks_ok = (
            sem("q_mm"), sem("k_mm"), sem("v_mm"), sem("q_sub"), sem("q_exp"), sem("q_ok"), sem("kmax"), sem("kexp"),
            sem("k_tr"), sem("ktok"), sem("v_ok"), sem("rks"))
        att_mm, att_ok, q_tr, qT_ok, y_mm, m2_ok, rstd2_ok, yn_ok, yn_tr, hT_ok, o_mm, res_ok, a_steps, v_steps = (
            sem("att_mm"), sem("att_ok"), sem("q_tr"), sem("qT_ok"), sem("y_mm"), sem("m2"), sem("rstd2"), sem("yn"),
            sem("yn_tr"), sem("hT"), sem("o_mm"), sem("res"), sem("a_steps"), sem("v_steps"))

        def row(name):
            r = ROWS.index(name)
            return rows[:, r * D:(r + 1) * D]

        passed_v, res_free = sem("passed_v"), sem("res_free")

        with nc.Block("layer0") as block:
            @block.sync
            def _(sp):
                sp.dma_start(w[:], io["L0_w"]).then_inc(w_in, 16)
                sp.dma_start(mask_t[:], io["mask_t"]).then_inc(w_in, 16)
                with sp.Fori(0, B // 2) as pair:
                    for p in range(2):
                        b = pair * 2 + p
                        sp.wait_ge(res_ok, b + 1)
                        sp.dma_start(x_in[:, p, :, :], io["x"][bass.ds(b * T, T), :].rearrange("(k p) d -> p k d", p=P)).then_inc(x_ld[p], 16)
                        sp.dma_start(mask_row[:, p, :], io["mask_k"][bass.ds(b, 1), :]).then_inc(mask_ld[p], 16)
                for s in stored:
                    sp.wait_ge(s, 16 * (B // 2))

            @block.gpsimd
            def _(pool):
                pool.sem_inc(res_free, 2)
                pool.memset(heads[:], 0.0).then_inc(heads_ok, 1)
                pool.wait_ge(heads_ok, 1)
                for h in range(P // W0):
                    last = pool.memset(heads[h * W0:(h + 1) * W0, h * W0:(h + 1) * W0], 1.0)
                last.then_inc(heads_ok, 1)
                with pool.Fori(0, B // 2) as pair:
                    for p in range(2):
                        b = pair * 2 + p
                        pool.wait_ge(res_ok, b + 3)
                        pool.dma_start(io["x1"][bass.ds(b * T, T), :].rearrange("(k p) d -> p k d", p=P), res[:, p, :, :]).then_inc(stored[p], 16)
                        pool.wait_ge(stored[p], pair * 16 + 16)
                        pool.sem_inc(res_free, 1)

            @block.vector
            def _(dve):
                dve.sem_inc(res_ok, 2)
                dve.wait_ge(heads_ok, 2)
                with dve.Fori(0, B // 2) as pair:
                    for p in range(2):
                        b = pair * 2 + p
                        chain = Chain(dve, v_steps, 6, b)
                        dve.wait_ge(mask_ld[p], pair * 16 + 16)
                        dve.tensor_scalar(mask_add[:, p, :], mask_row[:, p, :], 1.0, MASKED, ALU.subtract, ALU.mult).then_inc(madd_ok, 1)
                        dve.wait_ge(x_ld[p], pair * 16 + 16)
                        for t in range(TB):
                            last = dve.bn_stats(stats[:, t, :], x_in[:, p, t, :])
                        chain.link(last)
                        dve.sem_inc(passed_v, 1)
                        for t in range(TB):
                            last = dve.bn_aggr(moments[:, t, :], stats[:, t, :])
                        last.then_inc(moments_ok, 1)
                        dve.wait_ge(rstd_ok, b + 1)
                        for t in range(TB):
                            last = dve.tensor_scalar(xn[:, t, :], x_in[:, p, t, :], moments[:, t, 0:1], rstd[:, t:t + 1],
                                                     ALU.subtract, ALU.mult)
                        last.then_inc(xn_ok, 1)
                        dve.wait_ge(q_mm, b + 1)
                        qv = ps_q[:].rearrange("p a (g c) -> p (a g) c", c=W0)
                        q3 = q[:].rearrange("p (g c) -> p g c", c=W0)
                        chain.link(dve.tensor_reduce(q_max[:], qv, AX.X, ALU.max))
                        dve.tensor_tensor(q3, qv, q_max[:].unsqueeze(2).to_broadcast([P, TB * H0, W0]), ALU.subtract).then_inc(q_sub, 1)
                        dve.wait_ge(k_mm, b + 1)
                        for h in range(DH):
                            last = dve.tensor_reduce(k_max[:, h:h + 1], ps_k[:, h, :], AX.X, ALU.max, negate=True)
                        last.then_inc(kmax_ok, 1)
                        dve.wait_ge(q_exp, b + 1)
                        chain.link(dve.tensor_reduce(q_sum[:], q3, AX.X, ALU.add))
                        chain.link(dve.reciprocal(q_sum[:], q_sum[:]))
                        dve.tensor_tensor(q3, q3, q_sum[:].unsqueeze(2).to_broadcast([P, TB * H0, W0]), ALU.mult).then_inc(q_ok, 1)
                        dve.wait_ge(kexp_ok, b + 1)
                        chain.link(dve.reciprocal(k_sum[:], k_sum[:]))
                        dve.wait_ge(att_mm, b + 1)
                        for h in range(DH):
                            last = dve.scalar_tensor_tensor(att[:, h, :], ps_q[:, h, 0:P], k_sum[:, h:h + 1], heads[:], ALU.mult, ALU.mult)
                        last.then_inc(att_ok, 1)
                        dve.wait_ge(y_mm, b + 1)
                        yv = ps_v[:].rearrange("p a (k d) -> p (a k) d", d=D)
                        for t in range(TB):
                            last = dve.bn_stats(stats2[:, t, :], yv[:, t, :])
                        chain.link(last)
                        dve.sem_inc(passed_v, 1)
                        for t in range(TB):
                            last = dve.bn_aggr(moments2[:, t, :], stats2[:, t, :])
                        last.then_inc(m2_ok, 1)
                        dve.wait_ge(rstd2_ok, b + 1)
                        for t in range(TB):
                            last = dve.tensor_scalar(yn[:, t, :], yv[:, t, :], moments2[:, t, 0:1], rstd2[:, t:t + 1],
                                                     ALU.subtract, ALU.mult)
                        last.then_inc(yn_ok, 1)
                        dve.wait_ge(o_mm, b + 1)
                        dve.wait_ge(res_free, b + 1)
                        dve.tensor_tensor(res[:, p, :, :].rearrange("p k d -> p (k d)"), ps_k[:].rearrange("p a c -> p (a c)"),
                                          x_in[:, p, :, :].rearrange("p k d -> p (k d)"), ALU.add).then_inc(res_ok, 1)
                        chain.end()

            @block.scalar
            def _(act):
                act.sem_inc(hT_ok, 1)
                act.wait_ge(w_in, 32)
                with act.Fori(0, B // 2) as pair:
                    for p in range(2):
                        b = pair * 2 + p
                        chain = Chain(act, a_steps, 2, b)
                        act.wait_ge(moments_ok, b + 1)
                        chain.link(act.activation(rstd[:], moments[:, :, 1], ACT.Ln, bias=eps[:]))
                        act.activation(rstd[:], rstd[:], ACT.Exp, scale=-0.5).then_inc(rstd_ok, 1)
                        act.wait_ge(xn_tr, b + 1)
                        for h in range(DH):
                            last = act.activation(xnT[:, h, :], ps_t[:, h, :], ACT.Identity, scale=vec(vecs, "L0_ln_w")[:, h:h + 1],
                                                  bias=vec(vecs, "L0_ln_b")[:, h:h + 1])
                        last.then_inc(xnT_ok, 1)
                        act.wait_ge(q_sub, b + 1)
                        act.activation(q[:], q[:], ACT.Exp).then_inc(q_exp, 1)
                        act.wait_ge(kmax_ok, b + 1)
                        for h in range(DH):
                            last = act.activation(k_exp[:, h, :], ps_k[:, h, :], ACT.Exp, bias=k_max[:, h:h + 1], accum_out=k_sum[:, h:h + 1])
                        last.then_inc(kexp_ok, 1)
                        act.wait_ge(v_mm, b + 1)
                        vv = ps_v[:].rearrange("p a (k d) -> p (a k) d", d=D)
                        for t in range(TB):
                            last = act.activation(v[:, t, :], vv[:, t, :], ACT.Copy, scale=mask_t[:, bass.ds(b, 1), t])
                        last.then_inc(v_ok, 1)
                        act.wait_ge(k_tr, b + 1)
                        act.activation(k_tok[:].rearrange("p k d -> p (k d)"), ps_t[:].rearrange("p a c -> p (a c)"), ACT.Copy).then_inc(ktok_ok, 1)
                        act.wait_ge(q_tr, b + 1)
                        act.activation(qT[:], ps_t[:], ACT.Copy).then_inc(qT_ok, 1)
                        act.wait_ge(m2_ok, b + 1)
                        chain.link(act.activation(rstd2[:], moments2[:, :, 1], ACT.Ln, bias=eps[:]))
                        act.activation(rstd2[:], rstd2[:], ACT.Exp, scale=-0.5).then_inc(rstd2_ok, 1)
                        act.wait_ge(yn_tr, b + 1)
                        for h in range(DH):
                            last = act.activation(hT[:, h, :], ps_t[:, h, :], ACT.Silu, scale=coef[:, 0, 0, h, bass.ds(b, 1)],
                                                  bias=coef[:, 0, 1, h, bass.ds(b, 1)])
                        last.then_inc(hT_ok, 1)
                        chain.end()

            @block.tensor
            def _(pe):
                pe.wait_ge(w_in, 32)
                with pe.Fori(0, B // 2) as pair:
                    for p in range(2):
                        b = pair * 2 + p

                        def transposed(src):
                            for h in range(DH):
                                for t in range(TB):
                                    last = pe.transpose(ps_t[:, h, t * P:(t + 1) * P], src[:, t, h * P:(h + 1) * P], ident[:])
                            return last

                        pe.wait_ge(xn_ok, b + 1)
                        pe.wait_ge(hT_ok, b + 1)
                        transposed(xn).then_inc(xn_tr, 1)
                        pe.wait_ge(xnT_ok, b + 1)
                        qv = ps_q[:].rearrange("p a (k d) -> p (a k) d", d=D)
                        vv = ps_v[:].rearrange("p a (k d) -> p (a k) d", d=D)
                        ov = ps_k[:].rearrange("p a (k d) -> p (a k) d", d=D)

                        def project(dst, src, weight, bias):
                            for t in range(TB):
                                for k in range(DH):
                                    pe.matmul(dst[:, t, :], src[:, k, t * P:(t + 1) * P], weight[:, k, :], start=(k == 0), stop=False)
                                last = pe.matmul(dst[:, t, :], ones[0:1, 0:P], bias, start=False, stop=True)
                            return last

                        project(qv, xnT, wq, row("L0_bq")).then_inc(q_mm, 1)
                        pe.wait_ge(madd_ok, b + 1)
                        pe.wait_ge(res_ok, b + 2)
                        for h in range(DH):
                            for k in range(DH):
                                pe.matmul(ps_k[:, h, :], wk[:, k, h * P:(h + 1) * P], xnT[:, k, :], start=(k == 0), stop=False)
                            pe.matmul(ps_k[:, h, :], row("L0_bk")[:, h * P:(h + 1) * P], ones[0:1, :], start=False, stop=False)
                            last = pe.matmul(ps_k[:, h, :], ones[0:1, 0:P], mask_add[:, p, :], start=False, stop=True)
                        last.then_inc(k_mm, 1)
                        project(vv, xnT, wv, row("L0_bv")).then_inc(v_mm, 1)
                        pe.wait_ge(kexp_ok, b + 1)
                        for t in range(TB):
                            for h in range(DH):
                                last = pe.transpose(ps_t[:].rearrange("p a (k d) -> p (a k) d", d=D)[:, t, h * P:(h + 1) * P],
                                                    k_exp[:, h, t * P:(t + 1) * P], ident[:])
                        last.then_inc(k_tr, 1)
                        pe.wait_ge(ktok_ok, b + 1)
                        pe.wait_ge(v_ok, b + 1)
                        pe.wait_ge(q_sub, b + 1)
                        for h in range(DH):
                            for t in range(TB):
                                last = pe.matmul(ps_q[:, h, 0:P], k_tok[:, t, h * P:(h + 1) * P], v[:, t, h * P:(h + 1) * P],
                                                 start=(t == 0), stop=(t == TB - 1))
                        last.then_inc(att_mm, 1)
                        pe.wait_ge(q_ok, b + 1)
                        transposed(q[:].rearrange("p (k d) -> p k d", d=D)).then_inc(q_tr, 1)
                        pe.wait_ge(qT_ok, b + 1)
                        pe.wait_ge(att_ok, b + 1)
                        for t in range(TB):
                            for h in range(DH):
                                last = pe.matmul(vv[:, t, h * P:(h + 1) * P], qT[:, h, t * P:(t + 1) * P], att[:, h, :], start=True, stop=True)
                        last.then_inc(y_mm, 1)
                        pe.wait_ge(yn_ok, b + 1)
                        transposed(yn).then_inc(yn_tr, 1)
                        pe.wait_ge(hT_ok, b + 2)
                        project(ov, hT, wo, row("L0_b_out")).then_inc(o_mm, 1)
        sems.clear("layer0_clear")


UNITS = N * JB
DA_RING, DBU_RING, H_RING, HC_RING = 4, 3, 4, 4
CREDIT = 8
C_GROUP = 4
C_LOADS = N // C_GROUP
OUT_PARTS = TB // 2
PREP_V = 1 + JB * (TAPS - 1)


def dbu_slot(s):
    return s % DBU_RING


def dbu_back(s):
    if s >= DBU_RING:
        return DBU_RING
    return next(d for d in range(1, UNITS + 1) if d > s and dbu_slot(s - d + UNITS) == dbu_slot(s))


def mamba(nc, io, keep, layer, src, dst, gathered):
    pre = f"l{layer}_"
    L = f"L{layer}"
    li = STYLE.index(L)
    with ExitStack() as ctx:
        sb = lambda name, shape, dt=F32: ctx.enter_context(nc.sbuf_tensor(pre + name, shape, dt))
        sems = Semaphores(nc, ctx)
        sem = lambda name: sems(pre + name)
        vecs, ident, eps, coef = (keep[k] for k in ("vecs", "ident", "eps", "coef"))
        w_in, w_x, w_dt, w_out = sb("w_in", [P, DH, 2 * DI]), sb("w_x", [P, JB, XD]), sb("w_dt", [R, DI]), sb("w_out", [P, JB, D])
        gate = sb("gate", [P, B, D])
        a_neg = sb("a_neg", [P, JB * N])
        x_in = sb("x_in", [P, TB, D])
        stats, moments, rstd = sb("stats", [P, TB, 6]), sb("moments", [P, TB, 2]), sb("rstd", [P, TB])
        modT = sb("modT", [P, DH, T])
        conv_in = sb("conv_in", [P, JB, T + TAPS - 1])
        work = sb("work", [P, JB, T])
        u = sb("u", [P, 2, JB, T])
        z = sb("z", [P, 2, JB, T])
        x_dbl = sb("x_dbl", [XD, 2, T])
        dt_in = conv_in[:, :, TAPS - 1:]
        dt = sb("dt", [P, 2, JB, T])
        duT = sb("duT", [P, 2, TB, DI])
        b_tok = sb("b_tok", [P, 2, TB, N])
        c_all = sb("c_all", [P, 2, C_GROUP, T])
        dub = sb("dub", [P, 2, TB, DI])
        dA = sb("dA", [P, DA_RING, T])
        h = sb("h", [P, H_RING, T])
        hc = sb("hc", [P, HC_RING, T])
        y = sb("y", [P, JB, T])
        og = sb("og", [P, 2, 2, D])
        res = sb("res", [P, TB, D])
        x_loads = TB if gathered else 1
        res_steps = 1 if gathered else OUT_PARTS
        idx = idx_x = y_rows = None
        if gathered:
            idx = sb("idx", [P, TB], I32)
            idx_x = sb("idx_x", [P, TB], I32)
            y_rows = sb("y_rows", [P, TB, D])
        ps_y = ctx.enter_context(nc.psum_tensor(pre + "ps_y", [P, JB, T], F32))
        ps_dbu = ctx.enter_context(nc.psum_tensor(pre + "ps_dbu", [P, DBU_RING, T], F32))
        misc = ctx.enter_context(nc.psum_tensor(pre + "misc", [P, T], F32))

        w_ld, a_exp_ok, pad_ok, x_ld, idx_ld, idx_ok = sem("w_ld"), sem("a_exp"), sem("pad"), sem("x_ld"), sem("idx_ld"), sem("idx_ok")
        mom_ok, rstd_ok, xn_ok, xn_tr, mod_ok = sem("mom"), sem("rstd"), sem("xn"), sem("xn_tr"), sem("mod")
        in_mm, xc_ok, conv_ok, z_ok, u_ok, xd_mm, xd_ok, b_tr, b_ok = (
            sem("in_mm"), sem("xc"), sem("conv"), sem("z"), sem("u"), sem("xd_mm"), sem("xd"), sem("b_tr"), sem("b"))
        dt_mm, dti_ok, clip_ok, ln_ok, dt_ok, du_ok, duT_tr, duT_ok = (
            sem("dt_mm"), sem("dti"), sem("clip"), sem("ln"), sem("dt"), sem("du"), sem("duT_tr"), sem("duT"))
        c_st, c_ld = sem("c_st"), [sem("c_ld0"), sem("c_ld1")]
        dub_ok, da_ok, dbu_ok, scan_ok, hc_ok, sum_ok = (
            sem("dub"), sem("da"), sem("dbu"), sem("scan"), sem("hc"), sem("sum"))
        y_ok, yg_ok, out_mm, og_ok, res_ld, res_ok, stored, y_st, yr_ld = (
            sem("y"), sem("yg"), sem("out_mm"), sem("og"), sem("res_ld"), sem("res"), sem("stored"), sem("y_st"), sem("yr_ld"))
        prep_v, prep_a, a_ok = sem("prep_v"), sem("prep_a"), sem("a_ok")

        def rows_of(ap, b):
            return ap[bass.ds(b * T, T), :].rearrange("(k p) d -> p k d", p=P)

        y_dram = (io["y_even"], io["y_odd"])

        def first(b):
            return isinstance(b, int) and b == 0

        def early(b):
            return isinstance(b, int) and b < 2

        def batches(eng, body):
            body(0, 0, False, True)
            with eng.Fori(0, (B - 2) // 2) as pair:
                body(pair * 2 + 1, 1, True, True)
                body(pair * 2 + 2, 0, True, True)
            body(B - 1, (B - 1) % 2, True, False)

        passed_v, passed_p = sem("passed_v"), sem("passed_p")

        with nc.Block(f"layer{layer}") as block:
            @block.sync
            def _(sp):
                for tile, name in ((w_in, "w_in"), (w_x, "w_x"), (w_dt, "w_dt"), (w_out, "w_out")):
                    sp.dma_start(tile[:], io[f"{L}_{name}"]).then_inc(w_ld, 16)
                sp.dma_start(gate[:].rearrange("p b d -> p (b d)"),
                             io["gates"][(0 if layer == 1 else 1):(1 if layer == 1 else 2), :, :].rearrange("l b d -> l (b d)").to_broadcast([P, B * D])).then_inc(w_ld, 16)
                if gathered:
                    sp.dma_start(idx_x[:], io["idx"]).then_inc(idx_ld, 16)
                    sp.dma_start(idx[:], io["idx"]).then_inc(idx_ld, 16)

                def load_x(b):
                    if not gathered:
                        if not first(b):
                            sp.wait_ge(xn_tr, b * DH)
                        sp.dma_start(x_in[:], rows_of(src, b)).then_inc(x_ld, 16)

                def c_out(b, p):
                    sp.wait_ge(xd_ok, b + 1)
                    sp.dma_start(io["c_rows"][p, :, :], x_dbl[R + N:XD, p, :]).then_inc(c_st, 16)

                def c_load(b, p, g):
                    if not (g < 2 and first(b)):
                        sp.wait_ge(hc_ok, b * UNITS + (g - 1) * C_GROUP * JB + CREDIT)
                    sp.dma_start(c_all[:, g % 2, :, :].rearrange("p n t -> p (n t)"),
                                 io["c_rows"][p, g * C_GROUP:(g + 1) * C_GROUP, :].rearrange("(o n) t -> o (n t)", o=1).to_broadcast([P, C_GROUP * T])
                                 ).then_inc(c_ld[g % 2], 16)

                def res_load(b):
                    sp.wait_ge(stored, b * 16 + 16)
                    sp.dma_start(res[:], rows_of(src, b)).then_inc(res_ld, 16)

                def out(b):
                    sp.wait_ge(res_ok, b * res_steps + res_steps + CREDIT)
                    sp.dma_start(rows_of(dst, b), res[:]).then_inc(stored, 16)

                def body(b, p, has_post, has_prep):
                    if has_prep:
                        load_x(b + 1)
                    if has_post:
                        res_load(b - 1)
                        if gathered:
                            for tp in range(OUT_PARTS):
                                y_store(b - 1, 1 - p, tp)
                    c_load(b, p, 2)
                    if has_post:
                        out(b - 1)
                    c_load(b, p, 3)
                    if has_prep:
                        c_out(b + 1, 1 - p)
                        sp.wait_ge(c_st, b * 16 + 32)
                        c_load(b + 1, 1 - p, 0)
                        c_load(b + 1, 1 - p, 1)

                def y_store(b, p, tp):
                    sp.wait_ge(og_ok, b * OUT_PARTS + tp + 1)
                    sp.dma_start(y_dram[p][tp * 2 * P:(tp + 1) * 2 * P, :].rearrange("(k p) d -> p k d", p=P), og[:, tp, :, :]).then_inc(y_st, 16)

                sp.sem_inc(stored, 16)
                sp.sem_inc(y_st, 16)
                load_x(0)
                c_out(0, 0)
                sp.wait_ge(c_st, 16)
                c_load(0, 0, 0)
                c_load(0, 0, 1)
                batches(sp, body)
                res_load(B - 1)
                if gathered:
                    for tp in range(OUT_PARTS):
                        y_store(B - 1, (B - 1) % 2, tp)
                out(B - 1)
                sp.wait_ge(stored, 16 * B + 16)

            @block.scalar
            def _(act):
                act.activation(a_neg[:], vec(vecs, L + "_A_log"), ACT.Exp).then_inc(a_exp_ok, 1)
                act.wait_ge(a_ok, 1)

                def ln_rstd(b):
                    chain = Chain(act, prep_a, 2, b)
                    act.wait_ge(mom_ok, b + 1)
                    chain.link(act.activation(rstd[:], moments[:, :, 1], ACT.Ln, bias=eps[:]))
                    act.activation(rstd[:], rstd[:], ACT.Exp, scale=-0.5).then_inc(rstd_ok, 1)
                    return chain

                def mod(b, half):
                    act.wait_ge(xn_tr, b * DH + half + 1)
                    act.activation(modT[:, half, :], misc[:], ACT.Identity, scale=coef[:, li, 0, half, bass.ds(b, 1)],
                                   bias=coef[:, li, 1, half, bass.ds(b, 1)]).then_inc(mod_ok, 1)

                def x_part(b, j):
                    act.wait_ge(in_mm, b * 2 * JB + j + 1)
                    act.activation(conv_in[:, j, TAPS - 1:], misc[:], ACT.Copy).then_inc(xc_ok, 1)

                def z_part(b, p, j):
                    act.wait_ge(in_mm, b * 2 * JB + JB + j + 1)
                    if j == 0:
                        if not early(b):
                            act.wait_ge(yg_ok, b * JB - JB)
                    act.activation(z[:, p, j, :], misc[:], ACT.Copy).then_inc(z_ok, 1)

                def silus(b, p):
                    act.wait_ge(conv_ok, b * JB + JB)
                    act.activation(u[:, p, :, :], work[:], ACT.Silu).then_inc(u_ok, 1)
                    act.wait_ge(z_ok, b * JB + JB)
                    act.activation(z[:, p, :, :], z[:, p, :, :], ACT.Silu).then_inc(u_ok, 1)

                def xd(b, p):
                    act.wait_ge(xd_mm, b + 1)
                    if not early(b):
                        act.wait_ge(c_st, b * 16 - 16)
                    act.activation(x_dbl[:, p, :], misc[0:XD, :], ACT.Copy).then_inc(xd_ok, 1)

                def dt_raw(b, j):
                    act.wait_ge(dt_mm, b * JB + j + 1)
                    act.activation(dt_in[:, j, :], misc[:], ACT.Identity, bias=vec(vecs, L + "_dt_b")[:, j:j + 1]).then_inc(dti_ok, 1)

                def softplus(b):
                    act.wait_ge(clip_ok, b + 1)
                    act.activation(work[:], work[:], ACT.Exp).then_inc(prep_a, 1)
                    act.wait_ge(prep_a, b * 2 + 2)
                    act.activation(work[:], work[:], ACT.Ln, bias=1.0).then_inc(ln_ok, 1)

                def du_tok(b, p, t):
                    act.wait_ge(duT_tr, b * TB + t + 1)
                    act.activation(duT[:, p, t, :], misc[:], ACT.Copy).then_inc(duT_ok, 1)

                def prep_step(s, b, p):
                    if s == 8: ln_rstd(b)
                    if s in (13, 15): mod(b, (s - 13) // 2)
                    if s in (18, 20, 22, 24): x_part(b, (s - 18) // 2)
                    if s in (26, 28, 30, 32): z_part(b, p, (s - 26) // 2)
                    if s == 33: silus(b, p)
                    if s == 36: xd(b, p)
                    if s in (41, 43, 45, 47): dt_raw(b, (s - 41) // 2)
                    if s == 50: softplus(b)
                    if s in (55, 57, 59, 61): du_tok(b, p, (s - 55) // 2)

                def body(b, p, has_post, has_prep):
                    for n in range(N):
                        if n == 0:
                            act.wait_ge(duT_ok, b * TB + TB)
                            act.wait_ge(b_ok, b + 1)
                        act.wait_ge(dbu_ok, b * UNITS + (n - 1) * JB + CREDIT)
                        for t in range(TB):
                            last = act.activation(dub[:, n % 2, t, :], duT[:, p, t, :], ACT.Copy, scale=b_tok[:, p, t, n:n + 1])
                        last.then_inc(dub_ok, 1)
                        for j in range(JB):
                            s = n * JB + j
                            if s == 0:
                                act.wait_ge(dt_ok, b + 1)
                            act.wait_ge(scan_ok, b * UNITS + s + 1 - DA_RING + CREDIT)
                            act.activation(dA[:, s % DA_RING, :], dt[:, p, j, :], ACT.Exp, scale=a_neg[:, j * N + n:j * N + n + 1]).then_inc(da_ok, 1)
                            if has_prep:
                                prep_step(s, b + 1, 1 - p)

                for s in range(UNITS):
                    prep_step(s, 0, 0)
                batches(act, body)

            @block.vector
            def _(dve):
                dve.memset(conv_in[:, :, 0:TAPS - 1], 0.0).then_inc(pad_ok, 1)
                dve.sem_inc(scan_ok, CREDIT)
                dve.wait_ge(pad_ok, 1)
                dve.wait_ge(w_ld, 16 * 5)
                dve.wait_ge(a_exp_ok, 1)
                dve.tensor_scalar(a_neg[:], a_neg[:], -1.0, None, ALU.mult).then_inc(a_ok, 1)

                def ln_stats(b):
                    dve.wait_ge(x_ld, (b + 1) * 16 * x_loads)
                    for t in range(TB):
                        last = dve.bn_stats(stats[:, t, :], x_in[:, t, :])
                    last.then_inc(prep_v, 1)
                    dve.wait_ge(prep_v, b * PREP_V + 1)
                    dve.sem_inc(passed_v, 1)
                    for t in range(TB):
                        last = dve.bn_aggr(moments[:, t, :], stats[:, t, :])
                    last.then_inc(mom_ok, 1)

                def ln_apply(b):
                    dve.wait_ge(rstd_ok, b + 1)
                    for t in range(TB):
                        last = dve.tensor_scalar(x_in[:, t, :], x_in[:, t, :], moments[:, t, 0:1], rstd[:, t:t + 1], ALU.subtract, ALU.mult)
                    last.then_inc(xn_ok, 1)

                def conv(b, j):
                    dve.wait_ge(xc_ok, b * JB + j + 1)
                    if j == 0 and not first(b):
                        dve.wait_ge(dt_ok, b)
                    wcol = VEC_LAYOUT[L + "_conv_w"][0] + j * TAPS
                    dve.tensor_scalar(work[:, j, :], conv_in[:, j, 0:T], vecs[:, wcol:wcol + 1],
                                      vec(vecs, L + "_conv_b")[:, j:j + 1], ALU.mult, ALU.add).then_inc(prep_v, 1)
                    for k in range(1, TAPS):
                        dve.wait_ge(prep_v, b * PREP_V + 1 + j * (TAPS - 1) + k)
                        last = dve.scalar_tensor_tensor(work[:, j, :], conv_in[:, j, k:k + T], vecs[:, wcol + k:wcol + k + 1], work[:, j, :],
                                                        ALU.mult, ALU.add)
                        last.then_inc(prep_v if k < TAPS - 1 else conv_ok, 1)

                def b_copy(b, p):
                    dve.wait_ge(b_tr, b + 1)
                    dve.tensor_copy(b_tok[:, p, :, :], misc[:, 0:TB * XD].rearrange("p (t c) -> p t c", c=XD)[:, :, R:R + N]).then_inc(b_ok, 1)

                def clip(b):
                    dve.wait_ge(dti_ok, b * JB + JB)
                    dve.wait_ge(u_ok, b * 2 + 1)
                    dve.tensor_scalar(work[:], dt_in, 30.0, None, ALU.min).then_inc(clip_ok, 1)

                def dt_du(b, p):
                    dve.wait_ge(ln_ok, b + 1)
                    dve.tensor_tensor(dt[:, p, :, :], dt_in, work[:], ALU.max).then_inc(dt_ok, 1)
                    dve.wait_ge(dt_ok, b + 1)
                    dve.tensor_tensor(dt_in, dt[:, p, :, :], u[:, p, :, :], ALU.mult).then_inc(du_ok, 1)

                def y_skip(b, p):
                    for j in range(JB):
                        dve.wait_ge(sum_ok, b * UNITS + UNITS - JB + j + 1 + CREDIT)
                        if j == 0:
                            dve.wait_ge(out_mm, b * OUT_PARTS + 1)
                        dve.scalar_tensor_tensor(y[:, j, :], u[:, p, j, :], vec(vecs, L + "_D")[:, j:j + 1], ps_y[:, j, :], ALU.mult, ALU.add).then_inc(y_ok, 1)

                def out_gate(b, tp):
                    dve.wait_ge(out_mm, b * OUT_PARTS + tp + 2)
                    if gathered:
                        dve.wait_ge(y_st, b * OUT_PARTS * 16 + 16)
                    else:
                        dve.wait_ge(res_ok, b * OUT_PARTS + CREDIT)
                    dve.tensor_tensor(og[:, tp, :, :], misc[:].rearrange("p (k d) -> p k d", d=D),
                                      gate[:, bass.ds(b, 1), :].to_broadcast([P, 2, D]), ALU.mult).then_inc(og_ok, 1)

                def prep_step(s, b, p):
                    if s == 6: ln_stats(b)
                    if s == 10: ln_apply(b)
                    if s in (19, 21, 23, 25): conv(b, (s - 19) // 2)
                    if s == 39: b_copy(b, p)
                    if s == 49: clip(b)
                    if s == 52: dt_du(b, p)

                def post_step(s, b, p):
                    if s == 0: y_skip(b, p)
                    if s in (7, 11): out_gate(b, (s - 7) // 4)

                def body(b, p, has_post, has_prep):
                    for s in range(UNITS):
                        if has_post:
                            post_step(s, b - 1, 1 - p)
                        dve.wait_ge(da_ok, b * UNITS + s + 1)
                        dve.wait_ge(dbu_ok, b * UNITS + s + 1 + CREDIT)
                        dve.wait_ge(hc_ok, b * UNITS + s + 1 - H_RING + CREDIT)
                        dve.tensor_tensor_scan(h[:, s % H_RING, :], dA[:, s % DA_RING, :], ps_dbu[:, dbu_slot(s), :],
                                               0.0, ALU.mult, ALU.add).then_inc(scan_ok, 1)
                        if has_prep:
                            prep_step(s, b + 1, 1 - p)

                for s in range(UNITS):
                    prep_step(s, 0, 0)
                batches(dve, body)
                for s in range(12):
                    post_step(s, B - 1, (B - 1) % 2)

            @block.gpsimd
            def _(pool):
                pool.sem_inc(hc_ok, CREDIT)
                pool.sem_inc(res_ok, CREDIT)
                if gathered:
                    pool.wait_ge(idx_ld, 32)

                def gather_x(b):
                    if not first(b):
                        pool.wait_ge(xn_tr, b * DH)
                        pool.sem_inc(passed_p, 1)
                        pool.tensor_scalar(idx_x[:], idx_x[:], float(T), None, ALU.add).then_inc(idx_ok, 1)
                        pool.wait_ge(idx_ok, b)
                        pool.sem_inc(passed_p, 1)
                    for t in range(TB):
                        pool.indirect_dma_start(x_in[:, t, :], None, src[:, :], bass.IndirectOffsetOnAxis(ap=idx_x[:, t:t + 1], axis=0)).then_inc(x_ld, 16)

                def silu_gate(b, p):
                    pool.wait_ge(u_ok, b * 2 + 2)
                    for j in range(JB):
                        pool.wait_ge(y_ok, b * JB + j + 1)
                        pool.tensor_tensor(y[:, j, :], y[:, j, :], z[:, p, j, :], ALU.mult).then_inc(yg_ok, 1)

                def residual(b, tp):
                    pool.wait_ge(og_ok, b * OUT_PARTS + tp + 1)
                    if tp == 0:
                        pool.wait_ge(res_ld, b * 16 + 16)
                    pool.tensor_tensor(res[:, 2 * tp:2 * tp + 2, :], res[:, 2 * tp:2 * tp + 2, :], og[:, tp, :, :], ALU.add).then_inc(res_ok, 1)

                def gather_y(b, p):
                    pool.wait_ge(y_st, b * OUT_PARTS * 16 + OUT_PARTS * 16 + 16)
                    pool.wait_ge(res_ok, b + CREDIT)
                    pool.sem_inc(passed_p, 1)
                    for t in range(TB):
                        pool.indirect_dma_start(y_rows[:, t, :], None, y_dram[p], bass.IndirectOffsetOnAxis(ap=idx[:, t:t + 1], axis=0)).then_inc(yr_ld, 16)

                def residual_rows(b):
                    pool.wait_ge(yr_ld, (b + 1) * 16 * TB)
                    pool.wait_ge(res_ld, b * 16 + 16)
                    pool.tensor_tensor(res[:], res[:], y_rows[:], ALU.add).then_inc(res_ok, 1)

                def body(b, p, has_post, has_prep):
                    for s in range(UNITS):
                        if gathered and has_prep and s == 0: gather_x(b + 1)
                        if gathered and has_post and s == 18: gather_y(b - 1, 1 - p)
                        if gathered and has_post and s == 26: residual_rows(b - 1)
                        if has_post:
                            if s == 2: silu_gate(b - 1, 1 - p)
                            if not gathered and s in (9, 13): residual(b - 1, (s - 9) // 4)
                        n, j = s // JB, s % JB
                        if s % (C_GROUP * JB) == 0:
                            g = n // C_GROUP
                            pool.wait_ge(c_ld[g % 2], b * 32 + (g // 2) * 16 + 16)
                        pool.wait_ge(scan_ok, b * UNITS + s + 1 + CREDIT)
                        pool.wait_ge(sum_ok, b * UNITS + s + 1 - HC_RING + CREDIT)
                        pool.tensor_tensor(hc[:, s % HC_RING, :], h[:, s % H_RING, :], c_all[:, (n // C_GROUP) % 2, n % C_GROUP, :], ALU.mult).then_inc(hc_ok, 1)

                if gathered:
                    gather_x(0)
                batches(pool, body)
                silu_gate(B - 1, (B - 1) % 2)
                if gathered:
                    gather_y(B - 1, (B - 1) % 2)
                    residual_rows(B - 1)
                else:
                    for tp in range(OUT_PARTS):
                        residual(B - 1, tp)

            @block.tensor
            def _(pe):
                pe.wait_ge(w_ld, 16 * 5)
                pe.sem_inc(dbu_ok, CREDIT)
                pe.sem_inc(sum_ok, CREDIT)
                pe.sem_inc(out_mm, 1)

                def xn_half(b, half, after_post):
                    pe.wait_ge(xn_ok, b + 1)
                    if half:
                        pe.wait_ge(mod_ok, b * DH + 1)
                    elif after_post:
                        pe.wait_ge(og_ok, b * OUT_PARTS - OUT_PARTS)
                    elif not first(b):
                        pe.wait_ge(duT_ok, b * TB)
                    for t in range(TB):
                        last = pe.transpose(misc[:, t * P:(t + 1) * P], x_in[:, t, half * P:(half + 1) * P], ident[:])
                    last.then_inc(xn_tr, 1)

                def in_proj(b, e):
                    if e == 0:
                        pe.wait_ge(mod_ok, b * DH + DH)
                    elif e <= JB:
                        pe.wait_ge(xc_ok, b * JB + e)
                    else:
                        pe.wait_ge(z_ok, b * JB + e - JB)
                    for k in range(DH):
                        last = pe.matmul(misc[:], w_in[:, k, e * P:(e + 1) * P], modT[:, k, :], start=(k == 0), stop=(k == DH - 1))
                    last.then_inc(in_mm, 1)

                def x_proj(b, p):
                    pe.wait_ge(u_ok, b * 2 + 1)
                    pe.wait_ge(z_ok, b * JB + JB)
                    for k in range(JB):
                        last = pe.matmul(misc[0:XD, :], w_x[:, k, :], u[:, p, k, :], start=(k == 0), stop=(k == JB - 1))
                    last.then_inc(xd_mm, 1)

                def b_turn(b, p):
                    pe.wait_ge(xd_ok, b + 1)
                    for t in range(TB):
                        last = pe.transpose(misc[:, t * XD:(t + 1) * XD], x_dbl[:, p, t * P:(t + 1) * P], ident[0:XD, 0:XD])
                    last.then_inc(b_tr, 1)

                def dt_proj(b, p, j):
                    if j == 0:
                        pe.wait_ge(b_ok, b + 1)
                    else:
                        pe.wait_ge(dti_ok, b * JB + j)
                    pe.matmul(misc[:], w_dt[:, j * P:(j + 1) * P], x_dbl[0:R, p, :], start=True, stop=True).then_inc(dt_mm, 1)

                def du_turn(b, t):
                    pe.wait_ge(du_ok, b + 1)
                    if t == 0:
                        pe.wait_ge(dti_ok, b * JB + JB)
                    else:
                        pe.wait_ge(duT_ok, b * TB + t)
                    for j in range(JB):
                        last = pe.transpose(misc[:, j * P:(j + 1) * P], dt_in[:, j, t * P:(t + 1) * P], ident[:])
                    last.then_inc(duT_tr, 1)

                def out_proj(b, tp):
                    pe.wait_ge(yg_ok, b * JB + JB)
                    if tp == 0:
                        if not (isinstance(b, int) and b == B - 1):
                            pe.wait_ge(duT_ok, b * TB + 2 * TB)
                    else:
                        pe.wait_ge(og_ok, b * OUT_PARTS + tp)
                    for i in range(2):
                        t = 2 * tp + i
                        for k in range(JB):
                            last = pe.matmul(misc[:, i * D:(i + 1) * D], y[:, k, t * P:(t + 1) * P], w_out[:, k, :], start=(k == 0), stop=(k == JB - 1))
                    last.then_inc(out_mm, 1)

                def prep_step(s, b, p, after_post):
                    if s in (12, 14): xn_half(b, (s - 12) // 2, after_post)
                    if s in (17, 19, 21, 23): in_proj(b, (s - 17) // 2)
                    if s in (25, 27, 29, 31): in_proj(b, JB + (s - 25) // 2)
                    if s == 35: x_proj(b, p)
                    if s == 38: b_turn(b, p)
                    if s in (40, 42, 44, 46): dt_proj(b, p, (s - 40) // 2)
                    if s in (54, 56, 58, 60): du_turn(b, (s - 54) // 2)

                def add_unit(b, s, has_post):
                    n, j = s // JB, s % JB
                    if n == 0 and has_post:
                        pe.wait_ge(y_ok, b * JB - JB + j + 1)
                    pe.wait_ge(hc_ok, b * UNITS + s + 1 + CREDIT)
                    pe.matmul(ps_y[:, j, :], ident[:], hc[:, s % HC_RING, :], start=(n == 0), stop=(n == N - 1), skip_group_check=True).then_inc(sum_ok, 1)

                LAG = 3

                def body(b, p, has_post, has_prep):
                    for s in range(UNITS):
                        n, j = s // JB, s % JB
                        if j == 0:
                            pe.wait_ge(dub_ok, b * N + n + 1)
                        pe.wait_ge(scan_ok, b * UNITS + s + 1 - dbu_back(s) + CREDIT)
                        for t in range(TB):
                            last = pe.transpose(ps_dbu[:, dbu_slot(s), t * P:(t + 1) * P], dub[:, n % 2, t, j * P:(j + 1) * P], ident[:])
                        last.then_inc(dbu_ok, 1)
                        if s >= LAG:
                            add_unit(b, s - LAG, has_post)
                        if has_post and s in (6, 10):
                            out_proj(b - 1, (s - 6) // 4)
                        if has_prep:
                            prep_step(s, b + 1, 1 - p, has_post)
                    for s in range(UNITS - LAG, UNITS):
                        add_unit(b, s, has_post)

                for s in range(UNITS):
                    prep_step(s, 0, 0, False)
                batches(pe, body)
                for tp in range(OUT_PARTS):
                    out_proj(B - 1, tp)
        sems.clear(f"layer{layer}_clear")


SLOT = 32
MASK_ROW, MAX_ROW = W2, W2 + 1
GROUPS = H2 * SLOT // P
PAIRS = H2 // 2
S_LEAD = 2
RING = 3


def score_order():
    order = []
    for g in range(-S_LEAD, GROUPS):
        for half in range(2):
            for t in range(TB):
                if g >= 0:
                    order.append(("exp", 2 * g + half, t))
                if g + S_LEAD < GROUPS:
                    order.append(("max", 2 * (g + S_LEAD) + half, t))
    return order


def softmax_attention(nc, io, keep):
    with ExitStack() as ctx:
        sb = lambda name, shape: ctx.enter_context(nc.sbuf_tensor("l2_" + name, shape, F32))
        sems = Semaphores(nc, ctx)
        sem = lambda name: sems("l2_" + name)
        vecs, rows, ident, ones, eps, coef = (keep[k] for k in ("vecs", "rows", "ident", "ones", "eps", "coef"))
        QK = H2 * SLOT
        w = sb("w", [P, DH, 2 * QK + 2 * D])
        wq, wk, wv, wo = w[:, :, 0:QK], w[:, :, QK:2 * QK], w[:, :, 2 * QK:2 * QK + D], w[:, :, 2 * QK + D:]
        mask_t = sb("mask_t", [P, B, TB])
        mask_row, mask_add = sb("mask_row", [1, 2, T]), sb("mask_add", [1, 2, T])
        mask_slot = sb("mask_slot", [1, P])
        x_in = sb("x_in", [P, 2, TB, D])
        xn = sb("xn", [P, TB, D])
        xnT = sb("xnT", [P, DH, T])
        stats, moments, rstd = sb("stats", [P, TB, 6]), sb("moments", [P, TB, 2]), sb("rstd", [P, TB])
        qT, kT = sb("qT", [P, GROUPS, T]), sb("kT", [P, GROUPS, T])
        v = sb("v", [P, TB, H2, W2 + 1])
        q_max = sb("q_max", [P, GROUPS, TB, P])
        probs = sb("probs", [P, 2, 2, TB, T])
        inv_sum = sb("inv_sum", [P, 2, TB])
        y = sb("y", [P, TB, D])
        hT = sb("hT", [P, DH, T])
        res = sb("res", [P, 2, TB, D])
        ring = ctx.enter_context(nc.psum_tensor("l2_ring", [P, RING, 2, T], F32))
        ps_y = ctx.enter_context(nc.psum_tensor("l2_ps_y", [P, T], F32))
        misc = ctx.enter_context(nc.psum_tensor("l2_misc", [P, T], F32))

        w_ld, x_ld, mask_ld, fill_ok, slot_ok, stored, madd_ok = (
            sem("w_ld"), [sem("x_ld_even"), sem("x_ld_odd")], [sem("mask_ld_even"), sem("mask_ld_odd")], sem("fill"), sem("slot"), [sem("stored_even"), sem("stored_odd")], sem("madd"))
        mom_ok, rstd_ok, xn_ok, xn_tr, xnT_ok, q_mm, q_ok, k_mm, k_ok, v_mm, v_ok = (
            sem("mom"), sem("rstd"), sem("xn"), sem("xn_tr"), sem("xnT"), sem("q_mm"), sem("q"), sem("k_mm"), sem("k"), sem("v_mm"), sem("v"))
        s_mm, smax_ok, max_tr, qmax_ok, st_mm, exp_ok, pv_ok, y_ok = (
            sem("s_mm"), sem("smax"), sem("max_tr"), sem("qmax"), sem("st_mm"), sem("exp"), sem("pv"), sem("y"))
        m2_ok, rstd2_ok, yn_ok, yn_tr, hT_ok, o_mm, res_ok, a_steps, v_steps = (
            sem("m2"), sem("rstd2"), sem("yn"), sem("yn_tr"), sem("hT"), sem("o_mm"), sem("res"), sem("a_steps"), sem("v_steps"))
        order = score_order()
        OUT = TB // 2

        def row(name):
            r = ROWS.index(name)
            return rows[:, r * D:(r + 1) * D]

        def y_bank(pair):
            return ps_y[:, 0:2 * TB * (W2 + 1)].rearrange("p (h t c) -> p h t c", h=2, c=W2 + 1)

        passed_v, res_free = sem("passed_v"), sem("res_free")

        with nc.Block("layer2") as block:
            @block.sync
            def _(sp):
                sp.dma_start(w[:], io["L2_w"]).then_inc(w_ld, 16)
                sp.dma_start(mask_t[:], io["mask2_t"]).then_inc(w_ld, 16)
                with sp.Fori(0, B // 2) as two:
                    for p in range(2):
                        b = two * 2 + p
                        sp.wait_ge(res_ok, (b + 1) * OUT)
                        sp.dma_start(x_in[:, p, :, :], io["x2"][bass.ds(b * T, T), :].rearrange("(k p) d -> p k d", p=P)).then_inc(x_ld[p], 16)
                        sp.dma_start(mask_row[:, p, :], io["mask2_k"][bass.ds(b, 1), :]).then_inc(mask_ld[p], 16)
                for s in stored:
                    sp.wait_ge(s, 16 * (B // 2))

            @block.gpsimd
            def _(pool):
                pool.sem_inc(res_free, 2)
                pool.memset(mask_slot[:], 0.0).then_inc(slot_ok, 1)
                pool.memset(q_max[:], 0.0).then_inc(fill_ok, 1)
                pool.memset(v[:, :, :, W2], 1.0).then_inc(fill_ok, 1)
                pool.wait_ge(slot_ok, 1)
                pool.memset(mask_slot[:].rearrange("o (h s) -> o h s", s=SLOT)[:, :, MASK_ROW], 1.0).then_inc(fill_ok, 1)
                with pool.Fori(0, B // 2) as two:
                    for p in range(2):
                        b = two * 2 + p
                        pool.wait_ge(res_ok, (b + 3) * OUT)
                        pool.dma_start(io["x3"][bass.ds(b * T, T), :].rearrange("(k p) d -> p k d", p=P), res[:, p, :, :]).then_inc(stored[p], 16)
                        pool.wait_ge(stored[p], two * 16 + 16)
                        pool.sem_inc(res_free, 1)

            @block.vector
            def _(dve):
                dve.sem_inc(res_ok, 2 * OUT)
                dve.sem_inc(smax_ok, RING)
                dve.sem_inc(y_ok, 1)
                dve.wait_ge(fill_ok, 3)
                with dve.Fori(0, B // 2) as two:
                    for p in range(2):
                        b = two * 2 + p
                        chain = Chain(dve, v_steps, 2 + PAIRS, b)
                        dve.wait_ge(mask_ld[p], two * 16 + 16)
                        dve.tensor_scalar(mask_add[:, p, :], mask_row[:, p, :], 1.0, MASKED, ALU.subtract, ALU.mult).then_inc(madd_ok, 1)
                        dve.wait_ge(x_ld[p], two * 16 + 16)
                        for t in range(TB):
                            last = dve.bn_stats(stats[:, t, :], x_in[:, p, t, :])
                        chain.link(last)
                        dve.sem_inc(passed_v, 1)
                        for t in range(TB):
                            last = dve.bn_aggr(moments[:, t, :], stats[:, t, :])
                        last.then_inc(mom_ok, 1)
                        dve.wait_ge(rstd_ok, b + 1)
                        for t in range(TB):
                            last = dve.tensor_scalar(xn[:, t, :], x_in[:, p, t, :], moments[:, t, 0:1], rstd[:, t:t + 1], ALU.subtract, ALU.mult)
                        last.then_inc(xn_ok, 1)

                        def put_max(g):
                            dve.wait_ge(max_tr, b * GROUPS + g + 1)
                            dve.tensor_tensor(qT[:, g, :], qT[:, g, :], misc[:], ALU.add).then_inc(qmax_ok, 1)

                        def quotient(pair):
                            dve.wait_ge(pv_ok, b * PAIRS + pair + 1)
                            yb = y_bank(pair)
                            chain.link(dve.reciprocal(inv_sum[:], yb[:, :, :, W2]))
                            for i in range(2):
                                c = (2 * pair + i) * W2
                                last = dve.tensor_tensor(y[:, :, c:c + W2], yb[:, i, :, 0:W2],
                                                         inv_sum[:, i, :].unsqueeze(2).to_broadcast([P, TB, W2]), ALU.mult)
                            last.then_inc(y_ok, 1)

                        used = 0
                        for kind, pair, t in order:
                            n = used
                            used += 1
                            g = pair // 2
                            if kind == "exp":
                                if t == 0 and pair % 2 == 0 and g + 1 < GROUPS:
                                    if g == 0:
                                        put_max(0)
                                    put_max(g + 1)
                                if t == 2 and pair >= 1:
                                    quotient(pair - 1)
                                continue
                            dve.wait_ge(s_mm, b * PAIRS * TB + pair * TB + t + 1)
                            c = (pair % 2) * 2 * SLOT + MAX_ROW
                            dve.tensor_reduce(q_max[:, g, t, c:c + SLOT + 1:SLOT], ring[:, n % RING, :, :], AX.X, ALU.max).then_inc(smax_ok, 1)
                        quotient(PAIRS - 1)
                        dve.wait_ge(y_ok, (b + 1) * PAIRS + 1)
                        for t in range(TB):
                            last = dve.bn_stats(stats[:, t, :], y[:, t, :])
                        chain.link(last)
                        dve.sem_inc(passed_v, 1)
                        for t in range(TB):
                            last = dve.bn_aggr(moments[:, t, :], stats[:, t, :])
                        last.then_inc(m2_ok, 1)
                        dve.wait_ge(rstd2_ok, b + 1)
                        for t in range(TB):
                            last = dve.tensor_scalar(xn[:, t, :], y[:, t, :], moments[:, t, 0:1], rstd[:, t:t + 1], ALU.subtract, ALU.mult)
                        last.then_inc(yn_ok, 1)
                        dve.wait_ge(res_free, b + 1)
                        for t in range(OUT):
                            dve.wait_ge(o_mm, b * OUT + t + 1)
                            dve.tensor_tensor(res[:, p, 2 * t:2 * t + 2, :], misc[:].rearrange("p (k d) -> p k d", d=D),
                                              x_in[:, p, 2 * t:2 * t + 2, :], ALU.add).then_inc(res_ok, 1)
                        chain.end()

            @block.scalar
            def _(act):
                act.wait_ge(w_ld, 32)
                act.wait_ge(fill_ok, 3)
                act.sem_inc(exp_ok, RING)
                with act.Fori(0, B // 2) as two:
                    for p in range(2):
                        b = two * 2 + p
                        chain = Chain(act, a_steps, 2, b)
                        act.wait_ge(mom_ok, b + 1)
                        chain.link(act.activation(rstd[:], moments[:, :, 1], ACT.Ln, bias=eps[:]))
                        act.activation(rstd[:], rstd[:], ACT.Exp, scale=-0.5).then_inc(rstd_ok, 1)
                        for h in range(DH):
                            act.wait_ge(xn_tr, b * DH + h + 1)
                            act.activation(xnT[:, h, :], misc[:], ACT.Identity, scale=vec(vecs, "L2_ln_w")[:, h:h + 1],
                                           bias=vec(vecs, "L2_ln_b")[:, h:h + 1]).then_inc(xnT_ok, 1)
                        for mm, ok, dst, bias in ((q_mm, q_ok, qT, "L2_q_bias"), (k_mm, k_ok, kT, "L2_k_bias")):
                            for g in range(GROUPS):
                                act.wait_ge(mm, b * GROUPS + g + 1)
                                act.activation(dst[:, g, :], misc[:], ACT.Identity, bias=vec(vecs, bias)[:, g:g + 1]).then_inc(ok, 1)
                        for t in range(TB):
                            act.wait_ge(v_mm, b * OUT + t // 2 + 1)
                            act.activation(v[:, t, :, 0:W2], misc[:, (t % 2) * D:(t % 2 + 1) * D].rearrange("p (h c) -> p h c", c=W2), ACT.Copy,
                                           scale=mask_t[:, bass.ds(b, 1), t]).then_inc(v_ok, 1)
                        used = 0
                        for kind, pair, t in order:
                            n = used
                            used += 1
                            if kind == "max":
                                continue
                            act.wait_ge(st_mm, b * PAIRS * TB + pair * TB + t + 1)
                            if t == 0:
                                act.wait_ge(pv_ok, b * PAIRS + pair - 1) if pair >= 2 else None
                            act.activation(probs[:, pair % 2, :, t, :], ring[:, n % RING, :, :], ACT.Exp).then_inc(exp_ok, 1)
                        act.wait_ge(m2_ok, b + 1)
                        chain.link(act.activation(rstd[:], moments[:, :, 1], ACT.Ln, bias=eps[:]))
                        act.activation(rstd[:], rstd[:], ACT.Exp, scale=-0.5).then_inc(rstd2_ok, 1)
                        for h in range(DH):
                            act.wait_ge(yn_tr, b * DH + h + 1)
                            act.activation(hT[:, h, :], misc[:], ACT.Silu, scale=coef[:, 2, 0, h, bass.ds(b, 1)],
                                           bias=coef[:, 2, 1, h, bass.ds(b, 1)]).then_inc(hT_ok, 1)
                        chain.end()

            @block.tensor
            def _(pe):
                pe.wait_ge(w_ld, 32)
                pe.wait_ge(fill_ok, 3)
                with pe.Fori(0, B // 2) as two:
                    for p in range(2):
                        b = two * 2 + p
                        pe.wait_ge(xn_ok, b + 1)
                        pe.wait_ge(res_ok, (b + 2) * OUT)
                        for h in range(DH):
                            if h:
                                pe.wait_ge(xnT_ok, b * DH + h)
                            for t in range(TB):
                                last = pe.transpose(misc[:, t * P:(t + 1) * P], xn[:, t, h * P:(h + 1) * P], ident[:])
                            last.then_inc(xn_tr, 1)
                        pe.wait_ge(xnT_ok, b * DH + DH)
                        for g in range(GROUPS):
                            if g:
                                pe.wait_ge(q_ok, b * GROUPS + g)
                            for k in range(DH):
                                last = pe.matmul(misc[:], wq[:, k, g * P:(g + 1) * P], xnT[:, k, :], start=(k == 0), stop=(k == DH - 1))
                            last.then_inc(q_mm, 1)
                        pe.wait_ge(q_ok, b * GROUPS + GROUPS)
                        pe.wait_ge(madd_ok, b + 1)
                        for g in range(GROUPS):
                            if g:
                                pe.wait_ge(k_ok, b * GROUPS + g)
                            for k in range(DH):
                                pe.matmul(misc[:], wk[:, k, g * P:(g + 1) * P], xnT[:, k, :], start=(k == 0), stop=False)
                            pe.matmul(misc[:], mask_slot[:], mask_add[:, p, :], start=False, stop=True).then_inc(k_mm, 1)
                        pe.wait_ge(k_ok, b * GROUPS + GROUPS)
                        for t in range(TB):
                            if t == 2:
                                pe.wait_ge(v_ok, b * TB + 2)
                            o = misc[:, (t % 2) * D:(t % 2 + 1) * D]
                            for k in range(DH):
                                pe.matmul(o, xnT[:, k, t * P:(t + 1) * P], wv[:, k, :], start=(k == 0), stop=False)
                            last = pe.matmul(o, ones[0:1, 0:P], row("L2_bv"), start=False, stop=True)
                            if t % 2:
                                last.then_inc(v_mm, 1)
                        pe.wait_ge(v_ok, b * TB + TB)

                        def max_rows(g):
                            pe.wait_ge(smax_ok, b * PAIRS * TB + (g + 1) * 2 * TB + RING)
                            if g:
                                pe.wait_ge(qmax_ok, b * GROUPS + g)
                            for t in range(TB):
                                last = pe.transpose(misc[:, t * P:(t + 1) * P], q_max[:, g, t, :], ident[:])
                            last.then_inc(max_tr, 1)

                        def times_v(pair):
                            pe.wait_ge(exp_ok, b * PAIRS * TB + (pair + 1) * TB + RING)
                            pe.wait_ge(y_ok, b * PAIRS + pair + 1)
                            yb = y_bank(pair)
                            for i in range(2):
                                for t in range(TB):
                                    for m in range(TB):
                                        last = pe.matmul(yb[:, i, t, :], probs[:, pair % 2, i, m, t * P:(t + 1) * P], v[:, m, 2 * pair + i, :],
                                                         start=(m == 0), stop=(m == TB - 1))
                            last.then_inc(pv_ok, 1)

                        done = {"max": 0, "exp": 0}
                        for n, (kind, pair, t) in enumerate(order):
                            g = pair // 2
                            if kind == "exp" and t == 0 and pair % 2 == 0:
                                if g == 0:
                                    max_rows(0)
                                if g + 1 < GROUPS:
                                    max_rows(g + 1)
                                pe.wait_ge(qmax_ok, b * GROUPS + g + 1)
                            if kind == "exp" and t == 0 and pair >= 1:
                                times_v(pair - 1)
                            if n >= RING:
                                was, wpair, wt = order[n - RING]
                                pe.wait_ge(smax_ok if was == "max" else exp_ok, b * PAIRS * TB + wpair * TB + wt + 1 + RING)
                            else:
                                pe.wait_ge(exp_ok, b * PAIRS * TB + RING)
                            for i in range(2):
                                r = (2 * (pair % 2) + i) * SLOT
                                if kind == "max":
                                    last = pe.matmul(ring[:, n % RING, i, :], qT[r:r + MAX_ROW, g, t * P:(t + 1) * P], kT[r:r + MAX_ROW, g, :], start=True, stop=True)
                                else:
                                    last = pe.matmul(ring[:, n % RING, i, :], kT[r:r + MAX_ROW + 1, g, t * P:(t + 1) * P], qT[r:r + MAX_ROW + 1, g, :], start=True, stop=True)
                            last.then_inc(s_mm if kind == "max" else st_mm, 1)
                        times_v(PAIRS - 1)
                        pe.wait_ge(yn_ok, b + 1)
                        for h in range(DH):
                            if h:
                                pe.wait_ge(hT_ok, b * DH + h)
                            for t in range(TB):
                                last = pe.transpose(misc[:, t * P:(t + 1) * P], xn[:, t, h * P:(h + 1) * P], ident[:])
                            last.then_inc(yn_tr, 1)
                        pe.wait_ge(hT_ok, b * DH + DH)
                        for t in range(TB):
                            if t == 2:
                                pe.wait_ge(res_ok, (b + 2) * OUT + 1)
                            o = misc[:, (t % 2) * D:(t % 2 + 1) * D]
                            for k in range(DH):
                                pe.matmul(o, hT[:, k, t * P:(t + 1) * P], wo[:, k, :], start=(k == 0), stop=False)
                            last = pe.matmul(o, ones[0:1, 0:P], row("L2_b_out"), start=False, stop=True)
                            if t % 2:
                                last.then_inc(o_mm, 1)
        sems.clear("layer2_clear")


def build(nc, io):
    with ExitStack() as ctx:
        sb = lambda name, shape: ctx.enter_context(nc.sbuf_tensor(name, shape, F32))
        keep = {
            "vecs": sb("vecs", [P, NVEC]),
            "rows": sb("rows", [1, len(ROWS) * D]),
            "ident": sb("ident", [P, P]),
            "ones": sb("ones", [1, T]),
            "eps": sb("eps", [P, 1]),
            "coef": sb("coef", [P, 4, 2, DH, B]),
        }
        setup_block(nc, io, keep)
        linear_attention(nc, io, keep)
        mamba(nc, io, keep, 1, io["x1"], io["x2"], False)
        softmax_attention(nc, io, keep)
        mamba(nc, io, keep, 3, io["x3"], io["out"], True)


def _halves(a, n):
    return np.ascontiguousarray(np.asarray(a).reshape(n, P).T)


def _blocks(a):
    a = np.asarray(a)
    return np.ascontiguousarray(a.reshape(-1, P, a.shape[1]).transpose(1, 0, 2))


def _layout(i):
    f = {k: np.asarray(v) for k, v in i.items()}
    vecs = np.zeros((P, NVEC), np.float32)

    def put(name, a):
        c, n = VEC_LAYOUT[name]
        vecs[:, c:c + n] = a

    for l, ln, ln2, eb in (("L0", "ln", "ln2", "b_emb"), ("L2", "norm", "sb_norm", "emb_b")):
        put(l + "_ln_w", _halves(f[f"{l}_cond_{ln}_w"], DH))
        put(l + "_ln_b", _halves(f[f"{l}_cond_{ln}_b"], DH))
        put(l + "_ln2_w", _halves(f[f"{l}_cond_{ln2}_w"], DH))
        put(l + "_ln2_b", _halves(f[f"{l}_cond_{ln2}_b"], DH))
        put(l + "_scale_b", _halves(f[f"{l}_cond_{eb}"][:D], DH))
        put(l + "_shift_b", _halves(f[f"{l}_cond_{eb}"][D:], DH))
    for name, at, one in (("q", W2, 1.0), ("k", W2 + 1, -1.0)):
        slots = np.zeros((H2, 32), np.float32)
        slots[:, 0:W2] = f[f"L2_cond_{name}_b"].reshape(H2, W2)
        slots[:, at] = one
        put(f"L2_{name}_bias", _halves(slots.reshape(-1), 4))
    m = {1: ("ln_g", "ln_b", "ada_b", "dt_proj_b"), 3: ("gamma", "beta", "b_ada", "b_dt")}
    for l, (g, bb, ab, db) in m.items():
        c = f"L{l}_cond_"
        put(f"L{l}_ln_w", _halves(f[c + g], DH))
        put(f"L{l}_ln_b", _halves(f[c + bb], DH))
        put(f"L{l}_shift_b", _halves(f[c + ab][:D], DH))
        put(f"L{l}_scale_b", _halves(f[c + ab][D:2 * D], DH))
        put(f"L{l}_conv_b", _halves(f[c + "conv_b"], JB))
        put(f"L{l}_dt_b", _halves(f[c + db], JB))
        put(f"L{l}_D", _halves(f[c + "D_param"], JB))
        put(f"L{l}_conv_w", _blocks(f[c + "conv_w"].reshape(DI, TAPS)).reshape(P, JB * TAPS))
        put(f"L{l}_A_log", _blocks(f[c + "A_log"]).reshape(P, JB * N))
    rows = np.concatenate([f["L0_cond_bq"], f["L0_cond_bk"], f["L0_cond_bv"], f["L0_cond_b_out"], f["L2_cond_v_b"],
                           f["L2_cond_out_b"], f["L1_cond_ada_b"][2 * D:], f["L3_cond_b_ada"][2 * D:]])[None, :]
    cond_w = np.concatenate([f["L0_cond_W_emb"], f["L2_cond_emb_w"], f["L1_cond_ada_w"].T, f["L3_cond_W_ada"]], axis=1)
    out = {
        "x": f["x"].reshape(B * T, D),
        "cond_t": _blocks(f["cond_2048"].T),
        "cond_w": _blocks(cond_w),
        "vecs": vecs,
        "rows": rows,
        "mask_k": f["mask_BxSx1_fk1"].reshape(B, T),
        "mask_t": np.ascontiguousarray(f["mask_BxSx1_fk1"].reshape(B, TB, P).transpose(2, 0, 1)),
        "L0_w": _blocks(np.concatenate([f["L0_cond_Wq"], f["L0_cond_Wk"], f["L0_cond_Wv"], f["L0_cond_W_out"]], axis=1)),
    }
    slotted = []
    for name in ("q", "k"):
        s = np.zeros((D, H2, 32), np.float32)
        s[:, :, 0:W2] = f[f"L2_cond_{name}_w"].reshape(D, H2, W2)
        slotted.append(s.reshape(D, H2 * 32))
    out["L2_w"] = _blocks(np.concatenate(slotted + [f["L2_cond_v_w"], f["L2_cond_out_w"]], axis=1))
    out["mask2_k"] = f["mask_BxS_ff1"]
    out["mask2_t"] = np.ascontiguousarray(f["mask_BxS_ff1"].reshape(B, TB, P).transpose(2, 0, 1))
    for l, names, t in (("L1", ("in_proj_w", "x_proj_w", "dt_proj_w", "out_proj_w"), True), ("L3", ("W_in", "W_xp", "W_dt", "W_out"), False)):
        w = [f[f"{l}_cond_{n}"] for n in names]
        w = [a.T for a in w] if t else w
        out[l + "_w_in"], out[l + "_w_x"], out[l + "_w_dt"], out[l + "_w_out"] = _blocks(w[0]), _blocks(w[1]), w[2], _blocks(w[3])
    out["idx"] = np.ascontiguousarray(f["itok_S_0_1023"].reshape(TB, P).T)
    return {k: np.ascontiguousarray(v) for k, v in out.items()}


def kernel(**inputs):
    import concourse.bacc as _bacc
    from concourse.bass_utils import run_bass_kernel_spmd as _run

    nc = _bacc.Bacc("TRN2", target_bir_lowering=False, num_devices=1)
    arrays, io = {}, {}
    for name, a in _layout(inputs).items():
        arrays[f"in_{name}"] = a
        io[name] = nc.dram_tensor(f"in_{name}", a.shape, mybir.dt.from_np(a.dtype), kind="ExternalInput").ap()
    io["out"] = nc.dram_tensor("out_0_dram", (B * T, D), F32, kind="ExternalOutput").ap()
    for name in ("x1", "x2", "x3"):
        io[name] = nc.dram_tensor(name + "_dram", (B * T, D), F32).ap()
    for name in ("y_even", "y_odd"):
        io[name] = nc.dram_tensor(name + "_dram", (T, D), F32).ap()
    io["gates"] = nc.dram_tensor("gates_dram", (2, B, D), F32).ap()
    io["c_rows"] = nc.dram_tensor("c_rows_dram", (2, N, T), F32).ap()
    build(nc, io)
    r = _run(nc, [arrays], core_ids=[0])
    return r.results[0]["out_0_dram"].reshape(B, T, D)
```

```python
from contextlib import ExitStack

import numpy as np

import concourse.bass as bass
from concourse import mybir

F32 = mybir.dt.float32
I32 = mybir.dt.int32
BF16 = mybir.dt.bfloat16
ALU = mybir.AluOpType
ACT = mybir.ActivationFunctionType
AX = mybir.AxisListType

P = 128
B, T, D = 8, 512, 256
TB = T // P
DH = D // P
TE = 512
KE = TE // P
H0 = 8
W0 = D // H0
H2 = 16
W2 = D // H2
DI = 512
JB = DI // P
N = 16
R = 64
XD = R + 2 * N
TAPS = 4
EPS = 1e-5
MASKED = 1000000.0

VEC_LAYOUT = {}
_at = 0
for _name, _n in (
    [("L0_ln_w", DH), ("L0_ln_b", DH), ("L0_ln2_w", DH), ("L0_ln2_b", DH), ("L0_scale_b", DH), ("L0_shift_b", DH),
     ("L2_ln_w", DH), ("L2_ln_b", DH), ("L2_ln2_w", DH), ("L2_ln2_b", DH), ("L2_scale_b", DH), ("L2_shift_b", DH),
     ("L2_q_bias", DH), ("L2_k_bias", DH)]
    + [(f"L{l}_{n}", c) for l in (1, 3) for n, c in (
        ("ln_w", DH), ("ln_b", DH), ("shift_b", DH), ("scale_b", DH), ("conv_b", JB), ("dt_b", JB),
        ("D", JB), ("conv_w", JB * TAPS), ("A_log", JB * N))]
):
    VEC_LAYOUT[_name] = (_at, _n)
    _at += _n
NVEC = _at
ROWS = ["L0_bq", "L0_bk", "L0_bv", "L0_b_out", "L2_bv", "L2_b_out", "L1_gate_b", "L3_gate_b"]
COND_AT = {"L0": 0, "L2": 2 * D, "L1": 4 * D, "L3": 7 * D}
COND_W = 10 * D
STYLE = ("L0", "L1", "L2", "L3")


def vec(tile, name):
    a, n = VEC_LAYOUT[name]
    return tile[:, a:a + n]


class Chain:

    def __init__(self, eng, sem, per, b):
        self.eng, self.sem, self.per, self.base, self.n = eng, sem, per, b * per, 0

    def link(self, ins):
        ins.then_inc(self.sem, 1)
        self.n += 1
        self.eng.wait_ge(self.sem, self.base + self.n)

    def end(self):
        assert self.n == self.per, (self.n, self.per)


class Semaphores:

    def __init__(self, nc, ctx):
        self.nc, self.ctx, self.all = nc, ctx, []

    def __call__(self, name):
        self.all.append(self.ctx.enter_context(self.nc.semaphore(name)))
        return self.all[-1]

    def clear(self, name):
        with self.nc.Block(name) as block:
            @block.sync
            def _(sp):
                for s in self.all:
                    sp.sem_clear(s)


def setup_block(nc, io, keep):
    with ExitStack() as ctx:
        sb = lambda name, shape: ctx.enter_context(nc.sbuf_tensor(name, shape, F32))
        sems = Semaphores(nc, ctx)
        sem = lambda name: sems(name)
        cond_w = sb("su_cond_w", [P, KE, COND_W])
        cond_t = sb("su_cond_t", [P, KE, B])
        silu_c = sb("su_silu_c", [P, KE, B])
        raw = sb("su_raw", [P, 4, 2 * DH, B])
        one_b = sb("su_one_b", [1, B])
        gates = sb("su_gates", [B, 2, D])
        bias2 = sb("su_bias2", [P, 4, 2 * DH, B])
        ps = ctx.enter_context(nc.psum_tensor("su_ps", [P, 4, 2 * DH * B], F32))
        ps_gate = ctx.enter_context(nc.psum_tensor("su_ps_gate", [P, 2, D], F32))
        vecs, rows, ident, ones, eps, coef = (keep[k] for k in ("vecs", "rows", "ident", "ones", "eps", "coef"))
        loaded, weights_in, filled, diag_done = sem("su_loaded"), sem("su_weights_in"), sem("su_filled"), sem("su_diag")
        silu_done, mm_done, gate_mm, gate_out, stored, steps = (
            sem("su_silu"), sem("su_mm"), sem("su_gate_mm"), sem("su_gate_out"), sem("su_stored"), sem("su_steps"))

        with nc.Block("setup") as block:
            @block.sync
            def _(sp):
                sp.dma_start(cond_t[:], io["cond_t"]).then_inc(loaded, 16)
                sp.dma_start(vecs[:], io["vecs"]).then_inc(loaded, 16)
                sp.dma_start(rows[:], io["rows"]).then_inc(loaded, 16)
                sp.dma_start(cond_w[:], io["cond_w"]).then_inc(weights_in, 16)
                sp.wait_ge(gate_out, 1)
                sp.dma_start(io["gates"].rearrange("l b d -> b l d"), gates[:]).then_inc(stored, 16)
                sp.wait_ge(stored, 16)

            @block.gpsimd
            def _(pool):
                pool.memset(ident[:], 0.0).then_inc(filled, 1)
                pool.memset(ones[:], 1.0).then_inc(filled, 1)
                pool.memset(eps[:], EPS).then_inc(filled, 1)
                pool.memset(one_b[:], 1.0).then_inc(filled, 1)
                pool.wait_ge(filled, 4)
                pool.affine_select(out=ident[:], in_=ident[:], compare_op=ALU.not_equal, fill=1.0, base=0,
                                   pattern=[[-1, P]], channel_multiplier=1).then_inc(diag_done, 1)

            @block.scalar
            def _(act):
                act.wait_ge(loaded, 48)
                act.activation(silu_c[:], cond_t[:], ACT.Silu).then_inc(silu_done, 1)

            @block.tensor
            def _(pe):
                pe.wait_ge(silu_done, 1)
                pe.wait_ge(weights_in, 16)
                pe.wait_ge(filled, 4)
                for l, name in enumerate(STYLE):
                    for part in range(2 * DH):
                        first = part if name in ("L0", "L2") else (part + DH) % (2 * DH)
                        c = COND_AT[name] + first * P
                        for k in range(KE):
                            last = pe.matmul(ps[:, l, part * B:(part + 1) * B], cond_w[:, k, c:c + P], silu_c[:, k, :],
                                             start=(k == 0), stop=(k == KE - 1))
                last.then_inc(mm_done, 1)
                for l, name in enumerate(("L1", "L3")):
                    c = COND_AT[name] + 2 * D
                    for k in range(KE):
                        pe.matmul(ps_gate[0:B, l, :], silu_c[:, k, :], cond_w[:, k, c:c + D], start=(k == 0), stop=False)
                    r = ROWS.index(name + "_gate_b")
                    last = pe.matmul(ps_gate[0:B, l, :], one_b[:], rows[:, r * D:(r + 1) * D], start=False, stop=True)
                last.then_inc(gate_mm, 1)

            @block.vector
            def _(dve):
                chain = Chain(dve, steps, 12, 0)
                dve.wait_ge(loaded, 48)
                dve.wait_ge(mm_done, 1)
                for l, name in enumerate(STYLE):
                    two = "2" if name in ("L0", "L2") else ""
                    bias = vecs[:, VEC_LAYOUT[name + "_scale_b"][0]:VEC_LAYOUT[name + "_scale_b"][0] + DH]
                    sbias = vecs[:, VEC_LAYOUT[name + "_shift_b"][0]:VEC_LAYOUT[name + "_shift_b"][0] + DH]
                    w, bb = vec(vecs, f"{name}_ln{two}_w"), vec(vecs, f"{name}_ln{two}_b")
                    v = ps[:, l, :].rearrange("p (q b) -> p q b", b=B)
                    for h in range(DH):
                        last = dve.tensor_scalar(raw[:, l, h, :], v[:, h, :], bias[:, h:h + 1], 1.0, ALU.add, ALU.add)
                    chain.link(last)
                    for h in range(DH):
                        dve.tensor_scalar(raw[:, l, DH + h, :], v[:, DH + h, :], sbias[:, h:h + 1], None, ALU.add)
                        dve.tensor_scalar(coef[:, l, 0, h, :], raw[:, l, h, :], w[:, h:h + 1], None, ALU.mult)
                        last = dve.tensor_scalar(bias2[:, l, h, :], raw[:, l, h, :], bb[:, h:h + 1], None, ALU.mult)
                    chain.link(last)
                    for h in range(DH):
                        last = dve.tensor_tensor(coef[:, l, 1, h, :], bias2[:, l, h, :], raw[:, l, DH + h, :], ALU.add)
                    chain.link(last)
                chain.end()
                dve.wait_ge(gate_mm, 1)
                dve.tensor_copy(gates[:], ps_gate[0:B, :, :]).then_inc(gate_out, 1)
        sems.clear("setup_clear")


def linear_attention(nc, io, keep):
    with ExitStack() as ctx:
        sb = lambda name, shape: ctx.enter_context(nc.sbuf_tensor("l0_" + name, shape, F32))
        sems = Semaphores(nc, ctx)
        sem = lambda name: sems("l0_" + name)
        pb = lambda name: ctx.enter_context(nc.psum_tensor("l0_" + name, [P, 2, T], F32))
        vecs, rows, ident, ones, eps, coef = (keep[k] for k in ("vecs", "rows", "ident", "ones", "eps", "coef"))
        w = sb("w", [P, DH, 4 * D])
        wq, wk, wv, wo = (w[:, :, i * D:(i + 1) * D] for i in range(4))
        mask_t = sb("mask_t", [P, B, TB])
        mask_row = sb("mask_row", [1, 2, T])
        mask_add = sb("mask_add", [1, 2, T])
        heads = sb("heads", [P, P])
        x_in = sb("x_in", [P, 2, TB, D])
        xn = sb("xn", [P, TB, D])
        xnT = sb("xnT", [P, DH, T])
        stats, moments, rstd = sb("stats", [P, TB, 6]), sb("moments", [P, TB, 2]), sb("rstd", [P, TB])
        stats2, moments2, rstd2 = sb("stats2", [P, TB, 6]), sb("moments2", [P, TB, 2]), sb("rstd2", [P, TB])
        q = sb("q", [P, TB * D])
        q_max, q_sum = sb("q_max", [P, TB * H0]), sb("q_sum", [P, TB * H0])
        k_exp = sb("k_exp", [P, DH, T])
        k_max, k_sum = sb("k_max", [P, DH]), sb("k_sum", [P, DH])
        k_tok = sb("k_tok", [P, TB, D])
        v = sb("v", [P, TB, D])
        qT = sb("qT", [P, DH, T])
        att = sb("att", [P, DH, P])
        yn = sb("yn", [P, TB, D])
        hT = sb("hT", [P, DH, T])
        res = sb("res", [P, 2, TB, D])
        ps_t, ps_q, ps_k, ps_v = pb("ps_t"), pb("ps_q"), pb("ps_k"), pb("ps_v")

        w_in, x_ld, mask_ld, heads_ok, stored = sem("w_in"), [sem("x_ld_even"), sem("x_ld_odd")], [sem("mask_ld_even"), sem("mask_ld_odd")], sem("heads_ok"), keep["x1_stored"]
        moments_ok, rstd_ok, xn_ok, xn_tr, xnT_ok, madd_ok = (
            sem("moments"), sem("rstd"), sem("xn"), sem("xn_tr"), sem("xnT"), sem("madd"))
        q_mm, k_mm, v_mm, q_sub, q_exp, q_ok, kmax_ok, kexp_ok, k_tr, ktok_ok, v_ok, rks_ok = (
            sem("q_mm"), sem("k_mm"), sem("v_mm"), sem("q_sub"), sem("q_exp"), sem("q_ok"), sem("kmax"), sem("kexp"),
            sem("k_tr"), sem("ktok"), sem("v_ok"), sem("rks"))
        att_mm, att_ok, q_tr, qT_ok, y_mm, m2_ok, rstd2_ok, yn_ok, yn_tr, hT_ok, o_mm, res_ok, a_steps, v_steps = (
            sem("att_mm"), sem("att_ok"), sem("q_tr"), sem("qT_ok"), sem("y_mm"), sem("m2"), sem("rstd2"), sem("yn"),
            sem("yn_tr"), sem("hT"), sem("o_mm"), sem("res"), sem("a_steps"), sem("v_steps"))

        def row(name):
            r = ROWS.index(name)
            return rows[:, r * D:(r + 1) * D]

        passed_v, res_free = sem("passed_v"), sem("res_free")

        with nc.Block("layer0") as block:
            @block.sync
            def _(sp):
                sp.dma_start(w[:], io["L0_w"]).then_inc(w_in, 16)
                sp.dma_start(mask_t[:], io["mask_t"]).then_inc(w_in, 16)
                with sp.Fori(0, B // 2) as pair:
                    for p in range(2):
                        b = pair * 2 + p
                        sp.wait_ge(res_ok, b + 1)
                        sp.dma_start(x_in[:, p, :, :], io["x"][bass.ds(b * T, T), :].rearrange("(k p) d -> p k d", p=P)).then_inc(x_ld[p], 16)
                        sp.dma_start(mask_row[:, p, :], io["mask_k"][bass.ds(b, 1), :]).then_inc(mask_ld[p], 16)
                for s in stored:
                    sp.wait_ge(s, 16 * (B // 2))

            @block.gpsimd
            def _(pool):
                pool.sem_inc(res_free, 2)
                pool.memset(heads[:], 0.0).then_inc(heads_ok, 1)
                pool.wait_ge(heads_ok, 1)
                for h in range(P // W0):
                    last = pool.memset(heads[h * W0:(h + 1) * W0, h * W0:(h + 1) * W0], 1.0)
                last.then_inc(heads_ok, 1)
                with pool.Fori(0, B // 2) as pair:
                    for p in range(2):
                        b = pair * 2 + p
                        pool.wait_ge(res_ok, b + 3)
                        pool.dma_start(io["x1"][bass.ds(b * T, T), :].rearrange("(k p) d -> p k d", p=P), res[:, p, :, :]).then_inc(stored[p], 16)
                        pool.wait_ge(stored[p], pair * 16 + 16)
                        pool.sem_inc(res_free, 1)

            @block.vector
            def _(dve):
                dve.sem_inc(res_ok, 2)
                dve.wait_ge(heads_ok, 2)
                with dve.Fori(0, B // 2) as pair:
                    for p in range(2):
                        b = pair * 2 + p
                        chain = Chain(dve, v_steps, 6, b)
                        dve.wait_ge(mask_ld[p], pair * 16 + 16)
                        dve.tensor_scalar(mask_add[:, p, :], mask_row[:, p, :], 1.0, MASKED, ALU.subtract, ALU.mult).then_inc(madd_ok, 1)
                        dve.wait_ge(x_ld[p], pair * 16 + 16)
                        for t in range(TB):
                            last = dve.bn_stats(stats[:, t, :], x_in[:, p, t, :])
                        chain.link(last)
                        dve.sem_inc(passed_v, 1)
                        for t in range(TB):
                            last = dve.bn_aggr(moments[:, t, :], stats[:, t, :])
                        last.then_inc(moments_ok, 1)
                        dve.wait_ge(rstd_ok, b + 1)
                        for t in range(TB):
                            last = dve.tensor_scalar(xn[:, t, :], x_in[:, p, t, :], moments[:, t, 0:1], rstd[:, t:t + 1],
                                                     ALU.subtract, ALU.mult)
                        last.then_inc(xn_ok, 1)
                        dve.wait_ge(q_mm, b + 1)
                        qv = ps_q[:].rearrange("p a (g c) -> p (a g) c", c=W0)
                        q3 = q[:].rearrange("p (g c) -> p g c", c=W0)
                        chain.link(dve.tensor_reduce(q_max[:], qv, AX.X, ALU.max))
                        dve.tensor_tensor(q3, qv, q_max[:].unsqueeze(2).to_broadcast([P, TB * H0, W0]), ALU.subtract).then_inc(q_sub, 1)
                        dve.wait_ge(k_mm, b + 1)
                        for h in range(DH):
                            last = dve.tensor_reduce(k_max[:, h:h + 1], ps_k[:, h, :], AX.X, ALU.max, negate=True)
                        last.then_inc(kmax_ok, 1)
                        dve.wait_ge(q_exp, b + 1)
                        chain.link(dve.tensor_reduce(q_sum[:], q3, AX.X, ALU.add))
                        chain.link(dve.reciprocal(q_sum[:], q_sum[:]))
                        dve.tensor_tensor(q3, q3, q_sum[:].unsqueeze(2).to_broadcast([P, TB * H0, W0]), ALU.mult).then_inc(q_ok, 1)
                        dve.wait_ge(kexp_ok, b + 1)
                        chain.link(dve.reciprocal(k_sum[:], k_sum[:]))
                        dve.wait_ge(att_mm, b + 1)
                        for h in range(DH):
                            last = dve.scalar_tensor_tensor(att[:, h, :], ps_q[:, h, 0:P], k_sum[:, h:h + 1], heads[:], ALU.mult, ALU.mult)
                        last.then_inc(att_ok, 1)
                        dve.wait_ge(y_mm, b + 1)
                        yv = ps_v[:].rearrange("p a (k d) -> p (a k) d", d=D)
                        for t in range(TB):
                            last = dve.bn_stats(stats2[:, t, :], yv[:, t, :])
                        chain.link(last)
                        dve.sem_inc(passed_v, 1)
                        for t in range(TB):
                            last = dve.bn_aggr(moments2[:, t, :], stats2[:, t, :])
                        last.then_inc(m2_ok, 1)
                        dve.wait_ge(rstd2_ok, b + 1)
                        for t in range(TB):
                            last = dve.tensor_scalar(yn[:, t, :], yv[:, t, :], moments2[:, t, 0:1], rstd2[:, t:t + 1],
                                                     ALU.subtract, ALU.mult)
                        last.then_inc(yn_ok, 1)
                        dve.wait_ge(o_mm, b + 1)
                        dve.wait_ge(res_free, b + 1)
                        dve.tensor_tensor(res[:, p, :, :].rearrange("p k d -> p (k d)"), ps_k[:].rearrange("p a c -> p (a c)"),
                                          x_in[:, p, :, :].rearrange("p k d -> p (k d)"), ALU.add).then_inc(res_ok, 1)
                        chain.end()

            @block.scalar
            def _(act):
                act.sem_inc(hT_ok, 1)
                act.wait_ge(w_in, 32)
                with act.Fori(0, B // 2) as pair:
                    for p in range(2):
                        b = pair * 2 + p
                        chain = Chain(act, a_steps, 2, b)
                        act.wait_ge(moments_ok, b + 1)
                        chain.link(act.activation(rstd[:], moments[:, :, 1], ACT.Ln, bias=eps[:]))
                        act.activation(rstd[:], rstd[:], ACT.Exp, scale=-0.5).then_inc(rstd_ok, 1)
                        act.wait_ge(xn_tr, b + 1)
                        for h in range(DH):
                            last = act.activation(xnT[:, h, :], ps_t[:, h, :], ACT.Identity, scale=vec(vecs, "L0_ln_w")[:, h:h + 1],
                                                  bias=vec(vecs, "L0_ln_b")[:, h:h + 1])
                        last.then_inc(xnT_ok, 1)
                        act.wait_ge(q_sub, b + 1)
                        act.activation(q[:], q[:], ACT.Exp).then_inc(q_exp, 1)
                        act.wait_ge(kmax_ok, b + 1)
                        for h in range(DH):
                            last = act.activation(k_exp[:, h, :], ps_k[:, h, :], ACT.Exp, bias=k_max[:, h:h + 1], accum_out=k_sum[:, h:h + 1])
                        last.then_inc(kexp_ok, 1)
                        act.wait_ge(v_mm, b + 1)
                        vv = ps_v[:].rearrange("p a (k d) -> p (a k) d", d=D)
                        for t in range(TB):
                            last = act.activation(v[:, t, :], vv[:, t, :], ACT.Copy, scale=mask_t[:, bass.ds(b, 1), t])
                        last.then_inc(v_ok, 1)
                        act.wait_ge(k_tr, b + 1)
                        act.activation(k_tok[:].rearrange("p k d -> p (k d)"), ps_t[:].rearrange("p a c -> p (a c)"), ACT.Copy).then_inc(ktok_ok, 1)
                        act.wait_ge(q_tr, b + 1)
                        act.activation(qT[:], ps_t[:], ACT.Copy).then_inc(qT_ok, 1)
                        act.wait_ge(m2_ok, b + 1)
                        chain.link(act.activation(rstd2[:], moments2[:, :, 1], ACT.Ln, bias=eps[:]))
                        act.activation(rstd2[:], rstd2[:], ACT.Exp, scale=-0.5).then_inc(rstd2_ok, 1)
                        act.wait_ge(yn_tr, b + 1)
                        for h in range(DH):
                            last = act.activation(hT[:, h, :], ps_t[:, h, :], ACT.Silu, scale=coef[:, 0, 0, h, bass.ds(b, 1)],
                                                  bias=coef[:, 0, 1, h, bass.ds(b, 1)])
                        last.then_inc(hT_ok, 1)
                        chain.end()

            @block.tensor
            def _(pe):
                pe.wait_ge(w_in, 32)
                with pe.Fori(0, B // 2) as pair:
                    for p in range(2):
                        b = pair * 2 + p

                        def transposed(src):
                            for h in range(DH):
                                for t in range(TB):
                                    last = pe.transpose(ps_t[:, h, t * P:(t + 1) * P], src[:, t, h * P:(h + 1) * P], ident[:])
                            return last

                        pe.wait_ge(xn_ok, b + 1)
                        pe.wait_ge(hT_ok, b + 1)
                        transposed(xn).then_inc(xn_tr, 1)
                        pe.wait_ge(xnT_ok, b + 1)
                        qv = ps_q[:].rearrange("p a (k d) -> p (a k) d", d=D)
                        vv = ps_v[:].rearrange("p a (k d) -> p (a k) d", d=D)
                        ov = ps_k[:].rearrange("p a (k d) -> p (a k) d", d=D)

                        def project(dst, src, weight, bias):
                            for t in range(TB):
                                for k in range(DH):
                                    pe.matmul(dst[:, t, :], src[:, k, t * P:(t + 1) * P], weight[:, k, :], start=(k == 0), stop=False)
                                last = pe.matmul(dst[:, t, :], ones[0:1, 0:P], bias, start=False, stop=True)
                            return last

                        project(qv, xnT, wq, row("L0_bq")).then_inc(q_mm, 1)
                        pe.wait_ge(madd_ok, b + 1)
                        pe.wait_ge(res_ok, b + 2)
                        for h in range(DH):
                            for k in range(DH):
                                pe.matmul(ps_k[:, h, :], wk[:, k, h * P:(h + 1) * P], xnT[:, k, :], start=(k == 0), stop=False)
                            pe.matmul(ps_k[:, h, :], row("L0_bk")[:, h * P:(h + 1) * P], ones[0:1, :], start=False, stop=False)
                            last = pe.matmul(ps_k[:, h, :], ones[0:1, 0:P], mask_add[:, p, :], start=False, stop=True)
                        last.then_inc(k_mm, 1)
                        project(vv, xnT, wv, row("L0_bv")).then_inc(v_mm, 1)
                        pe.wait_ge(kexp_ok, b + 1)
                        for t in range(TB):
                            for h in range(DH):
                                last = pe.transpose(ps_t[:].rearrange("p a (k d) -> p (a k) d", d=D)[:, t, h * P:(h + 1) * P],
                                                    k_exp[:, h, t * P:(t + 1) * P], ident[:])
                        last.then_inc(k_tr, 1)
                        pe.wait_ge(ktok_ok, b + 1)
                        pe.wait_ge(v_ok, b + 1)
                        pe.wait_ge(q_sub, b + 1)
                        for h in range(DH):
                            for t in range(TB):
                                last = pe.matmul(ps_q[:, h, 0:P], k_tok[:, t, h * P:(h + 1) * P], v[:, t, h * P:(h + 1) * P],
                                                 start=(t == 0), stop=(t == TB - 1))
                        last.then_inc(att_mm, 1)
                        pe.wait_ge(q_ok, b + 1)
                        transposed(q[:].rearrange("p (k d) -> p k d", d=D)).then_inc(q_tr, 1)
                        pe.wait_ge(qT_ok, b + 1)
                        pe.wait_ge(att_ok, b + 1)
                        for t in range(TB):
                            for h in range(DH):
                                last = pe.matmul(vv[:, t, h * P:(h + 1) * P], qT[:, h, t * P:(t + 1) * P], att[:, h, :], start=True, stop=True)
                        last.then_inc(y_mm, 1)
                        pe.wait_ge(yn_ok, b + 1)
                        transposed(yn).then_inc(yn_tr, 1)
                        pe.wait_ge(hT_ok, b + 2)
                        project(ov, hT, wo, row("L0_b_out")).then_inc(o_mm, 1)
        sems.clear("layer0_clear")


UNITS = N * JB
DA_RING, DBU_RING, H_RING, HC_RING = 4, 3, 4, 4
CREDIT = 8
C_GROUP = 4
C_LOADS = N // C_GROUP
OUT_PARTS = TB // 2
PREP_V = 1 + JB * (TAPS - 1)


def dbu_slot(s):
    return s % DBU_RING


def dbu_back(s):
    if s >= DBU_RING:
        return DBU_RING
    return next(d for d in range(1, UNITS + 1) if d > s and dbu_slot(s - d + UNITS) == dbu_slot(s))


def mamba(nc, io, keep, layer, src, dst, gathered):
    pre = f"l{layer}_"
    L = f"L{layer}"
    li = STYLE.index(L)
    with ExitStack() as ctx:
        sb = lambda name, shape, dt=F32: ctx.enter_context(nc.sbuf_tensor(pre + name, shape, dt))
        sems = Semaphores(nc, ctx)
        sem = lambda name: sems(pre + name)
        vecs, ident, eps, coef = (keep[k] for k in ("vecs", "ident", "eps", "coef"))
        w_in, w_x, w_dt, w_out = sb("w_in", [P, DH, 2 * DI]), sb("w_x", [P, JB, XD]), sb("w_dt", [R, DI]), sb("w_out", [P, JB, D])
        gate = sb("gate", [P, B, D])
        a_neg = sb("a_neg", [P, JB * N])
        x_in = sb("x_in", [P, TB, D])
        stats, moments, rstd = sb("stats", [P, TB, 6]), sb("moments", [P, TB, 2]), sb("rstd", [P, TB])
        modT = sb("modT", [P, DH, T])
        conv_in = sb("conv_in", [P, JB, T + TAPS - 1])
        work = sb("work", [P, JB, T])
        u = sb("u", [P, 2, JB, T])
        z = sb("z", [P, 2, JB, T])
        x_dbl = sb("x_dbl", [XD, 2, T])
        dt_in = conv_in[:, :, TAPS - 1:]
        dt = sb("dt", [P, 2, JB, T])
        duT = sb("duT", [P, 2, TB, DI])
        b_tok = sb("b_tok", [P, 2, TB, N])
        c_all = sb("c_all", [P, 2, C_GROUP, T])
        dub = sb("dub", [P, 2, TB, DI])
        dA = sb("dA", [P, DA_RING, T])
        h = sb("h", [P, H_RING, T])
        hc = sb("hc", [P, HC_RING, T])
        y = sb("y", [P, JB, T])
        og = sb("og", [P, 2, 2, D])
        res = sb("res", [P, TB, D])
        x_loads = TB if gathered else 1
        res_steps = 1 if gathered else OUT_PARTS
        idx = idx_x = y_rows = None
        if gathered:
            idx = sb("idx", [P, TB], I32)
            idx_x = sb("idx_x", [P, TB], I32)
            y_rows = sb("y_rows", [P, TB, D])
        ps_y = ctx.enter_context(nc.psum_tensor(pre + "ps_y", [P, JB, T], F32))
        ps_dbu = ctx.enter_context(nc.psum_tensor(pre + "ps_dbu", [P, DBU_RING, T], F32))
        misc = ctx.enter_context(nc.psum_tensor(pre + "misc", [P, T], F32))

        w_ld, a_exp_ok, pad_ok, x_ld, idx_ld, idx_ok = sem("w_ld"), sem("a_exp"), sem("pad"), sem("x_ld"), sem("idx_ld"), sem("idx_ok")
        mom_ok, rstd_ok, xn_ok, xn_tr, mod_ok = sem("mom"), sem("rstd"), sem("xn"), sem("xn_tr"), sem("mod")
        in_mm, xc_ok, conv_ok, z_ok, u_ok, xd_mm, xd_ok, b_tr, b_ok = (
            sem("in_mm"), sem("xc"), sem("conv"), sem("z"), sem("u"), sem("xd_mm"), sem("xd"), sem("b_tr"), sem("b"))
        dt_mm, dti_ok, clip_ok, ln_ok, dt_ok, du_ok, duT_tr, duT_ok = (
            sem("dt_mm"), sem("dti"), sem("clip"), sem("ln"), sem("dt"), sem("du"), sem("duT_tr"), sem("duT"))
        c_st, c_ld = sem("c_st"), [sem("c_ld0"), sem("c_ld1")]
        dub_ok, da_ok, dbu_ok, scan_ok, hc_ok, sum_ok = (
            sem("dub"), sem("da"), sem("dbu"), sem("scan"), sem("hc"), sem("sum"))
        y_ok, yg_ok, out_mm, og_ok, res_ld, res_ok, stored, y_st, yr_ld = (
            sem("y"), sem("yg"), sem("out_mm"), sem("og"), sem("res_ld"), sem("res"), sem("stored"), sem("y_st"), sem("yr_ld"))
        prep_v, prep_a, a_ok = sem("prep_v"), sem("prep_a"), sem("a_ok")

        def rows_of(ap, b):
            return ap[bass.ds(b * T, T), :].rearrange("(k p) d -> p k d", p=P)

        y_dram = (io["y_even"], io["y_odd"])

        def first(b):
            return isinstance(b, int) and b == 0

        def early(b):
            return isinstance(b, int) and b < 2

        def batches(eng, body):
            body(0, 0, False, True)
            with eng.Fori(0, (B - 2) // 2) as pair:
                body(pair * 2 + 1, 1, True, True)
                body(pair * 2 + 2, 0, True, True)
            body(B - 1, (B - 1) % 2, True, False)

        passed_v, passed_p = sem("passed_v"), sem("passed_p")

        with nc.Block(f"layer{layer}") as block:
            @block.sync
            def _(sp):
                for tile, name in ((w_in, "w_in"), (w_x, "w_x"), (w_dt, "w_dt"), (w_out, "w_out")):
                    sp.dma_start(tile[:], io[f"{L}_{name}"]).then_inc(w_ld, 16)
                sp.dma_start(gate[:].rearrange("p b d -> p (b d)"),
                             io["gates"][(0 if layer == 1 else 1):(1 if layer == 1 else 2), :, :].rearrange("l b d -> l (b d)").to_broadcast([P, B * D])).then_inc(w_ld, 16)
                if gathered:
                    sp.dma_start(idx_x[:], io["idx"]).then_inc(idx_ld, 16)
                    sp.dma_start(idx[:], io["idx"]).then_inc(idx_ld, 16)

                def load_x(b):
                    if not gathered:
                        if not first(b):
                            sp.wait_ge(xn_tr, b * DH)
                        sp.dma_start(x_in[:], rows_of(src, b)).then_inc(x_ld, 16)

                def c_out(b, p):
                    sp.wait_ge(xd_ok, b + 1)
                    sp.dma_start(io["c_rows"][p, :, :], x_dbl[R + N:XD, p, :]).then_inc(c_st, 16)

                def c_load(b, p, g):
                    if not (g < 2 and first(b)):
                        sp.wait_ge(hc_ok, b * UNITS + (g - 1) * C_GROUP * JB + CREDIT)
                    sp.dma_start(c_all[:, g % 2, :, :].rearrange("p n t -> p (n t)"),
                                 io["c_rows"][p, g * C_GROUP:(g + 1) * C_GROUP, :].rearrange("(o n) t -> o (n t)", o=1).to_broadcast([P, C_GROUP * T])
                                 ).then_inc(c_ld[g % 2], 16)

                def res_load(b):
                    sp.wait_ge(stored, b * 16 + 16)
                    sp.dma_start(res[:], rows_of(src, b)).then_inc(res_ld, 16)

                def out(b):
                    sp.wait_ge(res_ok, b * res_steps + res_steps + CREDIT)
                    sp.dma_start(rows_of(dst, b), res[:]).then_inc(stored, 16)

                def body(b, p, has_post, has_prep):
                    if has_prep:
                        load_x(b + 1)
                    if has_post:
                        res_load(b - 1)
                        if gathered:
                            for tp in range(OUT_PARTS):
                                y_store(b - 1, 1 - p, tp)
                    c_load(b, p, 2)
                    if has_post:
                        out(b - 1)
                    c_load(b, p, 3)
                    if has_prep:
                        c_out(b + 1, 1 - p)
                        sp.wait_ge(c_st, b * 16 + 32)
                        c_load(b + 1, 1 - p, 0)
                        c_load(b + 1, 1 - p, 1)

                def y_store(b, p, tp):
                    sp.wait_ge(og_ok, b * OUT_PARTS + tp + 1)
                    sp.dma_start(y_dram[p][tp * 2 * P:(tp + 1) * 2 * P, :].rearrange("(k p) d -> p k d", p=P), og[:, tp, :, :]).then_inc(y_st, 16)

                sp.sem_inc(stored, 16)
                sp.sem_inc(y_st, 16)
                load_x(0)
                c_out(0, 0)
                sp.wait_ge(c_st, 16)
                c_load(0, 0, 0)
                c_load(0, 0, 1)
                batches(sp, body)
                res_load(B - 1)
                if gathered:
                    for tp in range(OUT_PARTS):
                        y_store(B - 1, (B - 1) % 2, tp)
                out(B - 1)
                sp.wait_ge(stored, 16 * B + 16)

            @block.scalar
            def _(act):
                act.activation(a_neg[:], vec(vecs, L + "_A_log"), ACT.Exp).then_inc(a_exp_ok, 1)
                act.wait_ge(a_ok, 1)

                def ln_rstd(b):
                    chain = Chain(act, prep_a, 2, b)
                    act.wait_ge(mom_ok, b + 1)
                    chain.link(act.activation(rstd[:], moments[:, :, 1], ACT.Ln, bias=eps[:]))
                    act.activation(rstd[:], rstd[:], ACT.Exp, scale=-0.5).then_inc(rstd_ok, 1)
                    return chain

                def mod(b, half):
                    act.wait_ge(xn_tr, b * DH + half + 1)
                    act.activation(modT[:, half, :], misc[:], ACT.Identity, scale=coef[:, li, 0, half, bass.ds(b, 1)],
                                   bias=coef[:, li, 1, half, bass.ds(b, 1)]).then_inc(mod_ok, 1)

                def x_part(b, j):
                    act.wait_ge(in_mm, b * 2 * JB + j + 1)
                    act.activation(conv_in[:, j, TAPS - 1:], misc[:], ACT.Copy).then_inc(xc_ok, 1)

                def z_part(b, p, j):
                    act.wait_ge(in_mm, b * 2 * JB + JB + j + 1)
                    if j == 0:
                        if not early(b):
                            act.wait_ge(yg_ok, b * JB - JB)
                    act.activation(z[:, p, j, :], misc[:], ACT.Copy).then_inc(z_ok, 1)

                def silus(b, p):
                    act.wait_ge(conv_ok, b * JB + JB)
                    act.activation(u[:, p, :, :], work[:], ACT.Silu).then_inc(u_ok, 1)
                    act.wait_ge(z_ok, b * JB + JB)
                    act.activation(z[:, p, :, :], z[:, p, :, :], ACT.Silu).then_inc(u_ok, 1)

                def xd(b, p):
                    act.wait_ge(xd_mm, b + 1)
                    if not early(b):
                        act.wait_ge(c_st, b * 16 - 16)
                    act.activation(x_dbl[:, p, :], misc[0:XD, :], ACT.Copy).then_inc(xd_ok, 1)

                def dt_raw(b, j):
                    act.wait_ge(dt_mm, b * JB + j + 1)
                    act.activation(dt_in[:, j, :], misc[:], ACT.Identity, bias=vec(vecs, L + "_dt_b")[:, j:j + 1]).then_inc(dti_ok, 1)

                def softplus(b):
                    act.wait_ge(clip_ok, b + 1)
                    act.activation(work[:], work[:], ACT.Exp).then_inc(prep_a, 1)
                    act.wait_ge(prep_a, b * 2 + 2)
                    act.activation(work[:], work[:], ACT.Ln, bias=1.0).then_inc(ln_ok, 1)

                def du_tok(b, p, t):
                    act.wait_ge(duT_tr, b * TB + t + 1)
                    act.activation(duT[:, p, t, :], misc[:], ACT.Copy).then_inc(duT_ok, 1)

                def prep_step(s, b, p):
                    if s == 8: ln_rstd(b)
                    if s in (13, 15): mod(b, (s - 13) // 2)
                    if s in (18, 20, 22, 24): x_part(b, (s - 18) // 2)
                    if s in (26, 28, 30, 32): z_part(b, p, (s - 26) // 2)
                    if s == 33: silus(b, p)
                    if s == 36: xd(b, p)
                    if s in (41, 43, 45, 47): dt_raw(b, (s - 41) // 2)
                    if s == 50: softplus(b)
                    if s in (55, 57, 59, 61): du_tok(b, p, (s - 55) // 2)

                def body(b, p, has_post, has_prep):
                    for n in range(N):
                        if n == 0:
                            act.wait_ge(duT_ok, b * TB + TB)
                            act.wait_ge(b_ok, b + 1)
                        act.wait_ge(dbu_ok, b * UNITS + (n - 1) * JB + CREDIT)
                        for t in range(TB):
                            last = act.activation(dub[:, n % 2, t, :], duT[:, p, t, :], ACT.Copy, scale=b_tok[:, p, t, n:n + 1])
                        last.then_inc(dub_ok, 1)
                        for j in range(JB):
                            s = n * JB + j
                            if s == 0:
                                act.wait_ge(dt_ok, b + 1)
                            act.wait_ge(scan_ok, b * UNITS + s + 1 - DA_RING + CREDIT)
                            act.activation(dA[:, s % DA_RING, :], dt[:, p, j, :], ACT.Exp, scale=a_neg[:, j * N + n:j * N + n + 1]).then_inc(da_ok, 1)
                            if has_prep:
                                prep_step(s, b + 1, 1 - p)

                for s in range(UNITS):
                    prep_step(s, 0, 0)
                batches(act, body)

            @block.vector
            def _(dve):
                dve.memset(conv_in[:, :, 0:TAPS - 1], 0.0).then_inc(pad_ok, 1)
                dve.sem_inc(scan_ok, CREDIT)
                dve.wait_ge(pad_ok, 1)
                dve.wait_ge(w_ld, 16 * 5)
                dve.wait_ge(a_exp_ok, 1)
                dve.tensor_scalar(a_neg[:], a_neg[:], -1.0, None, ALU.mult).then_inc(a_ok, 1)

                def ln_stats(b):
                    dve.wait_ge(x_ld, (b + 1) * 16 * x_loads)
                    for t in range(TB):
                        last = dve.bn_stats(stats[:, t, :], x_in[:, t, :])
                    last.then_inc(prep_v, 1)
                    dve.wait_ge(prep_v, b * PREP_V + 1)
                    dve.sem_inc(passed_v, 1)
                    for t in range(TB):
                        last = dve.bn_aggr(moments[:, t, :], stats[:, t, :])
                    last.then_inc(mom_ok, 1)

                def ln_apply(b):
                    dve.wait_ge(rstd_ok, b + 1)
                    for t in range(TB):
                        last = dve.tensor_scalar(x_in[:, t, :], x_in[:, t, :], moments[:, t, 0:1], rstd[:, t:t + 1], ALU.subtract, ALU.mult)
                    last.then_inc(xn_ok, 1)

                def conv(b, j):
                    dve.wait_ge(xc_ok, b * JB + j + 1)
                    if j == 0 and not first(b):
                        dve.wait_ge(dt_ok, b)
                    wcol = VEC_LAYOUT[L + "_conv_w"][0] + j * TAPS
                    dve.tensor_scalar(work[:, j, :], conv_in[:, j, 0:T], vecs[:, wcol:wcol + 1],
                                      vec(vecs, L + "_conv_b")[:, j:j + 1], ALU.mult, ALU.add).then_inc(prep_v, 1)
                    for k in range(1, TAPS):
                        dve.wait_ge(prep_v, b * PREP_V + 1 + j * (TAPS - 1) + k)
                        last = dve.scalar_tensor_tensor(work[:, j, :], conv_in[:, j, k:k + T], vecs[:, wcol + k:wcol + k + 1], work[:, j, :],
                                                        ALU.mult, ALU.add)
                        last.then_inc(prep_v if k < TAPS - 1 else conv_ok, 1)

                def b_copy(b, p):
                    dve.wait_ge(b_tr, b + 1)
                    dve.tensor_copy(b_tok[:, p, :, :], misc[:, 0:TB * XD].rearrange("p (t c) -> p t c", c=XD)[:, :, R:R + N]).then_inc(b_ok, 1)

                def clip(b):
                    dve.wait_ge(dti_ok, b * JB + JB)
                    dve.wait_ge(u_ok, b * 2 + 1)
                    dve.tensor_scalar(work[:], dt_in, 30.0, None, ALU.min).then_inc(clip_ok, 1)

                def dt_du(b, p):
                    dve.wait_ge(ln_ok, b + 1)
                    dve.tensor_tensor(dt[:, p, :, :], dt_in, work[:], ALU.max).then_inc(dt_ok, 1)
                    dve.wait_ge(dt_ok, b + 1)
                    dve.tensor_tensor(dt_in, dt[:, p, :, :], u[:, p, :, :], ALU.mult).then_inc(du_ok, 1)

                def y_skip(b, p):
                    for j in range(JB):
                        dve.wait_ge(sum_ok, b * UNITS + UNITS - JB + j + 1 + CREDIT)
                        if j == 0:
                            dve.wait_ge(out_mm, b * OUT_PARTS + 1)
                        dve.scalar_tensor_tensor(y[:, j, :], u[:, p, j, :], vec(vecs, L + "_D")[:, j:j + 1], ps_y[:, j, :], ALU.mult, ALU.add).then_inc(y_ok, 1)

                def out_gate(b, tp):
                    dve.wait_ge(out_mm, b * OUT_PARTS + tp + 2)
                    if gathered:
                        dve.wait_ge(y_st, b * OUT_PARTS * 16 + 16)
                    else:
                        dve.wait_ge(res_ok, b * OUT_PARTS + CREDIT)
                    dve.tensor_tensor(og[:, tp, :, :], misc[:].rearrange("p (k d) -> p k d", d=D),
                                      gate[:, bass.ds(b, 1), :].to_broadcast([P, 2, D]), ALU.mult).then_inc(og_ok, 1)

                def prep_step(s, b, p):
                    if s == 6: ln_stats(b)
                    if s == 10: ln_apply(b)
                    if s in (19, 21, 23, 25): conv(b, (s - 19) // 2)
                    if s == 39: b_copy(b, p)
                    if s == 49: clip(b)
                    if s == 52: dt_du(b, p)

                def post_step(s, b, p):
                    if s == 0: y_skip(b, p)
                    if s in (7, 11): out_gate(b, (s - 7) // 4)

                def body(b, p, has_post, has_prep):
                    for s in range(UNITS):
                        if has_post:
                            post_step(s, b - 1, 1 - p)
                        dve.wait_ge(da_ok, b * UNITS + s + 1)
                        dve.wait_ge(dbu_ok, b * UNITS + s + 1 + CREDIT)
                        dve.wait_ge(hc_ok, b * UNITS + s + 1 - H_RING + CREDIT)
                        dve.tensor_tensor_scan(h[:, s % H_RING, :], dA[:, s % DA_RING, :], ps_dbu[:, dbu_slot(s), :],
                                               0.0, ALU.mult, ALU.add).then_inc(scan_ok, 1)
                        if has_prep:
                            prep_step(s, b + 1, 1 - p)

                for s in range(UNITS):
                    prep_step(s, 0, 0)
                batches(dve, body)
                for s in range(12):
                    post_step(s, B - 1, (B - 1) % 2)

            @block.gpsimd
            def _(pool):
                pool.sem_inc(hc_ok, CREDIT)
                pool.sem_inc(res_ok, CREDIT)
                if gathered:
                    pool.wait_ge(idx_ld, 32)

                def gather_x(b):
                    if not first(b):
                        pool.wait_ge(xn_tr, b * DH)
                        pool.sem_inc(passed_p, 1)
                        pool.tensor_scalar(idx_x[:], idx_x[:], float(T), None, ALU.add).then_inc(idx_ok, 1)
                        pool.wait_ge(idx_ok, b)
                        pool.sem_inc(passed_p, 1)
                    for t in range(TB):
                        pool.indirect_dma_start(x_in[:, t, :], None, src[:, :], bass.IndirectOffsetOnAxis(ap=idx_x[:, t:t + 1], axis=0)).then_inc(x_ld, 16)

                def silu_gate(b, p):
                    pool.wait_ge(u_ok, b * 2 + 2)
                    for j in range(JB):
                        pool.wait_ge(y_ok, b * JB + j + 1)
                        pool.tensor_tensor(y[:, j, :], y[:, j, :], z[:, p, j, :], ALU.mult).then_inc(yg_ok, 1)

                def residual(b, tp):
                    pool.wait_ge(og_ok, b * OUT_PARTS + tp + 1)
                    if tp == 0:
                        pool.wait_ge(res_ld, b * 16 + 16)
                    pool.tensor_tensor(res[:, 2 * tp:2 * tp + 2, :], res[:, 2 * tp:2 * tp + 2, :], og[:, tp, :, :], ALU.add).then_inc(res_ok, 1)

                def gather_y(b, p):
                    pool.wait_ge(y_st, b * OUT_PARTS * 16 + OUT_PARTS * 16 + 16)
                    pool.wait_ge(res_ok, b + CREDIT)
                    pool.sem_inc(passed_p, 1)
                    for t in range(TB):
                        pool.indirect_dma_start(y_rows[:, t, :], None, y_dram[p], bass.IndirectOffsetOnAxis(ap=idx[:, t:t + 1], axis=0)).then_inc(yr_ld, 16)

                def residual_rows(b):
                    pool.wait_ge(yr_ld, (b + 1) * 16 * TB)
                    pool.wait_ge(res_ld, b * 16 + 16)
                    pool.tensor_tensor(res[:], res[:], y_rows[:], ALU.add).then_inc(res_ok, 1)

                def body(b, p, has_post, has_prep):
                    for s in range(UNITS):
                        if gathered and has_prep and s == 0: gather_x(b + 1)
                        if gathered and has_post and s == 18: gather_y(b - 1, 1 - p)
                        if gathered and has_post and s == 26: residual_rows(b - 1)
                        if has_post:
                            if s == 2: silu_gate(b - 1, 1 - p)
                            if not gathered and s in (9, 13): residual(b - 1, (s - 9) // 4)
                        n, j = s // JB, s % JB
                        if s % (C_GROUP * JB) == 0:
                            g = n // C_GROUP
                            pool.wait_ge(c_ld[g % 2], b * 32 + (g // 2) * 16 + 16)
                        pool.wait_ge(scan_ok, b * UNITS + s + 1 + CREDIT)
                        pool.wait_ge(sum_ok, b * UNITS + s + 1 - HC_RING + CREDIT)
                        pool.tensor_tensor(hc[:, s % HC_RING, :], h[:, s % H_RING, :], c_all[:, (n // C_GROUP) % 2, n % C_GROUP, :], ALU.mult).then_inc(hc_ok, 1)

                if gathered:
                    gather_x(0)
                batches(pool, body)
                silu_gate(B - 1, (B - 1) % 2)
                if gathered:
                    gather_y(B - 1, (B - 1) % 2)
                    residual_rows(B - 1)
                else:
                    for tp in range(OUT_PARTS):
                        residual(B - 1, tp)

            @block.tensor
            def _(pe):
                pe.wait_ge(w_ld, 16 * 5)
                pe.sem_inc(dbu_ok, CREDIT)
                pe.sem_inc(sum_ok, CREDIT)
                pe.sem_inc(out_mm, 1)

                def xn_half(b, half, after_post):
                    pe.wait_ge(xn_ok, b + 1)
                    if half:
                        pe.wait_ge(mod_ok, b * DH + 1)
                    elif after_post:
                        pe.wait_ge(og_ok, b * OUT_PARTS - OUT_PARTS)
                    elif not first(b):
                        pe.wait_ge(duT_ok, b * TB)
                    for t in range(TB):
                        last = pe.transpose(misc[:, t * P:(t + 1) * P], x_in[:, t, half * P:(half + 1) * P], ident[:])
                    last.then_inc(xn_tr, 1)

                def in_proj(b, e):
                    if e == 0:
                        pe.wait_ge(mod_ok, b * DH + DH)
                    elif e <= JB:
                        pe.wait_ge(xc_ok, b * JB + e)
                    else:
                        pe.wait_ge(z_ok, b * JB + e - JB)
                    for k in range(DH):
                        last = pe.matmul(misc[:], w_in[:, k, e * P:(e + 1) * P], modT[:, k, :], start=(k == 0), stop=(k == DH - 1))
                    last.then_inc(in_mm, 1)

                def x_proj(b, p):
                    pe.wait_ge(u_ok, b * 2 + 1)
                    pe.wait_ge(z_ok, b * JB + JB)
                    for k in range(JB):
                        last = pe.matmul(misc[0:XD, :], w_x[:, k, :], u[:, p, k, :], start=(k == 0), stop=(k == JB - 1))
                    last.then_inc(xd_mm, 1)

                def b_turn(b, p):
                    pe.wait_ge(xd_ok, b + 1)
                    for t in range(TB):
                        last = pe.transpose(misc[:, t * XD:(t + 1) * XD], x_dbl[:, p, t * P:(t + 1) * P], ident[0:XD, 0:XD])
                    last.then_inc(b_tr, 1)

                def dt_proj(b, p, j):
                    if j == 0:
                        pe.wait_ge(b_ok, b + 1)
                    else:
                        pe.wait_ge(dti_ok, b * JB + j)
                    pe.matmul(misc[:], w_dt[:, j * P:(j + 1) * P], x_dbl[0:R, p, :], start=True, stop=True).then_inc(dt_mm, 1)

                def du_turn(b, t):
                    pe.wait_ge(du_ok, b + 1)
                    if t == 0:
                        pe.wait_ge(dti_ok, b * JB + JB)
                    else:
                        pe.wait_ge(duT_ok, b * TB + t)
                    for j in range(JB):
                        last = pe.transpose(misc[:, j * P:(j + 1) * P], dt_in[:, j, t * P:(t + 1) * P], ident[:])
                    last.then_inc(duT_tr, 1)

                def out_proj(b, tp):
                    pe.wait_ge(yg_ok, b * JB + JB)
                    if tp == 0:
                        if not (isinstance(b, int) and b == B - 1):
                            pe.wait_ge(duT_ok, b * TB + 2 * TB)
                    else:
                        pe.wait_ge(og_ok, b * OUT_PARTS + tp)
                    for i in range(2):
                        t = 2 * tp + i
                        for k in range(JB):
                            last = pe.matmul(misc[:, i * D:(i + 1) * D], y[:, k, t * P:(t + 1) * P], w_out[:, k, :], start=(k == 0), stop=(k == JB - 1))
                    last.then_inc(out_mm, 1)

                def prep_step(s, b, p, after_post):
                    if s in (12, 14): xn_half(b, (s - 12) // 2, after_post)
                    if s in (17, 19, 21, 23): in_proj(b, (s - 17) // 2)
                    if s in (25, 27, 29, 31): in_proj(b, JB + (s - 25) // 2)
                    if s == 35: x_proj(b, p)
                    if s == 38: b_turn(b, p)
                    if s in (40, 42, 44, 46): dt_proj(b, p, (s - 40) // 2)
                    if s in (54, 56, 58, 60): du_turn(b, (s - 54) // 2)

                def add_unit(b, s, has_post):
                    n, j = s // JB, s % JB
                    if n == 0 and has_post:
                        pe.wait_ge(y_ok, b * JB - JB + j + 1)
                    pe.wait_ge(hc_ok, b * UNITS + s + 1 + CREDIT)
                    pe.matmul(ps_y[:, j, :], ident[:], hc[:, s % HC_RING, :], start=(n == 0), stop=(n == N - 1), skip_group_check=True).then_inc(sum_ok, 1)

                LAG = 3

                def body(b, p, has_post, has_prep):
                    for s in range(UNITS):
                        n, j = s // JB, s % JB
                        if j == 0:
                            pe.wait_ge(dub_ok, b * N + n + 1)
                        pe.wait_ge(scan_ok, b * UNITS + s + 1 - dbu_back(s) + CREDIT)
                        for t in range(TB):
                            last = pe.transpose(ps_dbu[:, dbu_slot(s), t * P:(t + 1) * P], dub[:, n % 2, t, j * P:(j + 1) * P], ident[:])
                        last.then_inc(dbu_ok, 1)
                        if s >= LAG:
                            add_unit(b, s - LAG, has_post)
                        if has_post and s in (6, 10):
                            out_proj(b - 1, (s - 6) // 4)
                        if has_prep:
                            prep_step(s, b + 1, 1 - p, has_post)
                    for s in range(UNITS - LAG, UNITS):
                        add_unit(b, s, has_post)

                for s in range(UNITS):
                    prep_step(s, 0, 0, False)
                batches(pe, body)
                for tp in range(OUT_PARTS):
                    out_proj(B - 1, tp)
        sems.clear(f"layer{layer}_clear")


PAIRS = H2 // 2
GROUPS = 4
GH = H2 // GROUPS
RING = 3
Q_PARTS = (0, 0, 1, 1, 0, 2)
K_PARTS = (0, 1, 0, 1, 2, 0)
MASK_AT = len(Q_PARTS) * W2
MAX_AT = MASK_AT + 3
STACK = MAX_AT + 3
HALF_USES = PAIRS * TB // 2


def softmax_attention(nc, io, keep):
    with ExitStack() as ctx:
        sb = lambda name, shape, dt=F32: ctx.enter_context(nc.sbuf_tensor("l2_" + name, shape, dt))
        sems = Semaphores(nc, ctx)
        sem = lambda name: sems("l2_" + name)
        vecs, rows, ident, ones, eps, coef = (keep[k] for k in ("vecs", "rows", "ident", "ones", "eps", "coef"))
        w = sb("w", [P, DH, 4 * D])
        wq, wk, wv, wo = (w[:, :, i * D:(i + 1) * D] for i in range(4))
        mask_t = sb("mask_t", [P, B, TB])
        mask_all, mask_add = sb("mask_all", [B, T]), sb("mask_add", [B, T])
        mask_parts = sb("mask_parts", [B, 3, T], BF16)
        x_in = sb("x_in", [P, TB, D])
        xnT = sb("xnT", [P, DH, T])
        stats, moments, rstd = sb("stats", [P, TB, 6]), sb("moments", [P, TB, 2]), sb("rstd", [P, TB])
        stats2, moments2, rstd2 = sb("stats2", [P, TB, 6]), sb("moments2", [P, TB, 2]), sb("rstd2", [P, TB])
        parts = sb("parts", [P, 2, 3, DH, T], BF16)
        rest = sb("rest", [P, 2, DH, T])
        qs, ks = sb("qs", [STACK, 2, H2, T], BF16), sb("ks", [STACK, 2, H2, T], BF16)
        v = sb("v", [P, 2, TB, H2, W2 + 1])
        q_max = sb("q_max", [P, GROUPS, GH, TB])
        m_parts = sb("m_parts", [GH * TB, GROUPS, 3, P], BF16)
        m_rest = sb("m_rest", [GH * TB, GROUPS, P])
        probs = sb("probs", [P, 2, 2, TB, T])
        inv_sum = sb("inv_sum", [P, 2, TB])
        y = sb("y", [P, 2, TB, D])
        hT = sb("hT", [P, DH, T])
        res = sb("res", [P, TB, D])
        ring = ctx.enter_context(nc.psum_tensor("l2_ring", [P, RING, 2, T], F32))
        ps_y = ctx.enter_context(nc.psum_tensor("l2_ps_y", [P, T], F32))
        misc = ctx.enter_context(nc.psum_tensor("l2_misc", [P, T], F32))

        w_ld, fill_ok, mask_ok, mask_p1, mask_p2, mask_p3, mask_st = (
            sem("w_ld"), sem("fill"), sem("mask"), sem("mask_p1"), sem("mask_p2"), sem("mask_p3"), sem("mask_st"))
        x_ld, mom_ok, rstd_ok, xn_ok, xn_tr, xnT_ok = sem("x_ld"), sem("mom"), sem("rstd"), sem("xn"), sem("xn_tr"), sem("xnT")
        qk_mm, p1_ok, rest_ok, p2_ok, p3_ok, parts_st, stack_ld = (
            sem("qk_mm"), sem("p1"), sem("rest"), sem("p2"), sem("p3"), sem("parts_st"), sem("stack_ld"))
        v_mm, v_ok = sem("v_mm"), sem("v")
        s_mm, smax_ok, m_tr, m1_ok, mr_ok, m2p_ok, m3_ok, exp_mm, exp_ok, pv_ok, y_ok, inv_ok = (
            sem("s_mm"), sem("smax"), sem("m_tr"), sem("m1"), sem("mr"), sem("m2p"), sem("m3"), sem("exp_mm"), sem("exp"), sem("pv"),
            sem("y"), sem("inv"))
        m_ld = [sem(f"m_ld{g}") for g in range(GROUPS)]
        st2_ok, mom2_ok, rstd2_ok, yn_ok, yn_tr, hT_ok, o_mm, res_ld, res_ok, stored = (
            sem("st2"), sem("mom2"), sem("rstd2"), sem("yn"), sem("yn_tr"), sem("hT"), sem("o_mm"), sem("res_ld"), sem("res"), sem("stored"))
        st_ok, ln_a, ln_b, passed = sem("st"), sem("ln_a"), sem("ln_b"), sem("passed")
        OUT = TB // 2

        def row(name):
            r = ROWS.index(name)
            return rows[:, r * D:(r + 1) * D]

        def rows_of(ap, b):
            return ap[bass.ds(b * T, T), :].rearrange("(k p) d -> p k d", p=P)

        y_bank = ps_y[:, 0:2 * TB * (W2 + 1)].rearrange("p (h t c) -> p h t c", h=2, c=W2 + 1)

        def first(b):
            return isinstance(b, int) and b == 0

        def early(b):
            return isinstance(b, int) and b < 2

        def batches(body):
            def one(eng):
                body(0, 0, False, True, True)
                with eng.Fori(0, 2) as two:
                    body(two * 2 + 1, 1, True, True, True)
                    body(two * 2 + 2, 0, True, True, True)
                body(B - 3, (B - 3) % 2, True, True, True)
                body(B - 2, (B - 2) % 2, True, True, False)
                body(B - 1, (B - 1) % 2, True, False, False)
            return one

        with nc.Block("layer2") as block:
            @block.sync
            def _(sp):
                sp.dma_start(w[:], io["L2_w"]).then_inc(w_ld, 16)
                sp.dma_start(mask_t[:], io["mask2_t"]).then_inc(w_ld, 16)
                sp.dma_start(mask_all[:], io["mask2_k"]).then_inc(w_ld, 16)
                sp.sem_inc(stored, 16)

                def load_x(b):
                    if not first(b):
                        sp.wait_ge(xn_tr, b * DH)
                    sp.dma_start(x_in[:], rows_of(io["x2"], b)).then_inc(x_ld, 16)

                def parts_out(b, p):
                    sp.wait_ge(p3_ok, b * 2 * DH + 2 * DH)
                    for i in range(2):
                        for a in range(3):
                            sp.dma_start(io["parts"][p, i, a, :, :].rearrange("(g p) t -> p g t", p=P), parts[:, i, a, :, :]).then_inc(parts_st, 16)

                def stack(b, p):
                    sp.wait_ge(parts_st, b * 96 + 96)
                    if not early(b):
                        sp.wait_ge(exp_ok, (b - 1) * PAIRS * TB + RING)
                    for i, (dst, order) in enumerate(((qs, Q_PARTS), (ks, K_PARTS))):
                        for s, a in enumerate(order):
                            sp.dma_start(dst[s * W2:(s + 1) * W2, p, :, :], io["parts"][p, i, a, :, :].rearrange("(h c) t -> c h t", c=W2)).then_inc(stack_ld, 16)
                    sp.dma_start(ks[MASK_AT:MASK_AT + 3, p, :, :], io["mask_parts"][bass.ds(b, 1), :, :].rearrange("b a t -> a b t").to_broadcast([3, H2, T])).then_inc(stack_ld, 16)

                def max_out(b, p, g):
                    sp.wait_ge(m3_ok, b * GROUPS + g + 1)
                    for a in range(3):
                        sp.dma_start(qs[MAX_AT + a:MAX_AT + a + 1, p, g * GH:(g + 1) * GH, :].rearrange("o h (t n) -> o (h t) n", n=P),
                                     m_parts[:, g, a, :]).then_inc(m_ld[g], 16)

                def res_load(b):
                    sp.wait_ge(stored, b * 16 + 16)
                    sp.dma_start(res[:], rows_of(io["x2"], b)).then_inc(res_ld, 16)

                def out(b):
                    sp.wait_ge(res_ok, b * OUT + OUT)
                    sp.dma_start(rows_of(io["x3"], b), res[:]).then_inc(stored, 16)

                @batches
                def run(b, p, has_post, has_next, has_after):
                    if has_after:
                        load_x(b + 2)
                    if has_post:
                        res_load(b - 1)
                    max_out(b, p, 1)
                    if has_next:
                        stack(b + 1, 1 - p)
                    max_out(b, p, 2)
                    if has_post:
                        out(b - 1)
                    max_out(b, p, 3)
                    if has_next:
                        max_out(b + 1, 1 - p, 0)
                    if has_after:
                        parts_out(b + 2, p)

                load_x(0)
                sp.wait_ge(mask_p3, 1)
                sp.dma_start(io["mask_parts"], mask_parts[:]).then_inc(mask_st, 16)
                sp.wait_ge(mask_st, 16)
                parts_out(0, 0)
                sp.wait_ge(fill_ok, 4)
                stack(0, 0)
                load_x(1)
                max_out(0, 0, 0)
                parts_out(1, 1)
                run(sp)
                res_load(B - 1)
                out(B - 1)
                sp.wait_ge(stored, 16 * B + 16)

            @block.gpsimd
            def _(pool):
                pool.memset(qs[MASK_AT:STACK, :, :, :], 1.0).then_inc(fill_ok, 1)
                pool.wait_ge(fill_ok, 1)
                pool.memset(ks[MASK_AT:STACK, :, :, :], -1.0).then_inc(fill_ok, 1)
                for p in range(2):
                    pool.wait_ge(fill_ok, 2 + p)
                    pool.memset(v[:, p, :, :, W2], 1.0).then_inc(fill_ok, 1)

            @block.vector
            def _(dve):
                dve.sem_inc(smax_ok, RING)
                dve.sem_inc(y_ok, 1)
                dve.wait_ge(fill_ok, 4)
                dve.wait_ge(w_ld, 48)
                dve.tensor_scalar(mask_add[:], mask_all[:], 1.0, MASKED, ALU.subtract, ALU.mult).then_inc(mask_ok, 1)
                dve.wait_ge(mask_ok, 1)
                dve.tensor_copy(mask_parts[:, 0, :], mask_add[:]).then_inc(mask_p1, 1)
                dve.wait_ge(mask_p1, 1)
                dve.tensor_tensor(mask_add[:], mask_add[:], mask_parts[:, 0, :], ALU.subtract).then_inc(mask_ok, 1)
                dve.wait_ge(mask_ok, 2)
                dve.tensor_copy(mask_parts[:, 1, :], mask_add[:]).then_inc(mask_p2, 1)
                dve.wait_ge(mask_p2, 1)
                dve.tensor_tensor(mask_parts[:, 2, :], mask_add[:], mask_parts[:, 1, :], ALU.subtract).then_inc(mask_p3, 1)

                def ln_stats(b):
                    dve.wait_ge(x_ld, b * 16 + 16)
                    for t in range(TB):
                        last = dve.bn_stats(stats[:, t, :], x_in[:, t, :])
                    last.then_inc(st_ok, 1)
                    dve.wait_ge(st_ok, b + 1)
                    dve.sem_inc(passed, 1)
                    for t in range(TB):
                        last = dve.bn_aggr(moments[:, t, :], stats[:, t, :])
                    last.then_inc(mom_ok, 1)

                def ln_apply(b):
                    dve.wait_ge(rstd_ok, b + 1)
                    for t in range(TB):
                        last = dve.tensor_scalar(x_in[:, t, :], x_in[:, t, :], moments[:, t, 0:1], rstd[:, t:t + 1], ALU.subtract, ALU.mult)
                    last.then_inc(xn_ok, 1)

                def split(b, i, g):
                    n = b * 2 * DH + i * DH + g + 1
                    bias = vec(vecs, "L2_q_bias" if i == 0 else "L2_k_bias")[:, g:g + 1]
                    dve.wait_ge(p1_ok, n)
                    dve.scalar_tensor_tensor(rest[:, i, g, :], misc[:], bias, parts[:, i, 0, g, :], ALU.add, ALU.subtract).then_inc(rest_ok, 1)
                    dve.wait_ge(rest_ok, n)
                    dve.tensor_copy(parts[:, i, 1, g, :], rest[:, i, g, :]).then_inc(p2_ok, 1)
                    dve.wait_ge(p2_ok, n)
                    dve.tensor_tensor(parts[:, i, 2, g, :], rest[:, i, g, :], parts[:, i, 1, g, :], ALU.subtract).then_inc(p3_ok, 1)

                def max_parts(b, g):
                    n = b * GROUPS + g + 1
                    dve.wait_ge(m_tr, n)
                    if not first(b):
                        dve.wait_ge(m_ld[g], b * 48)
                    ps = misc[0:GH * TB, 0:P]
                    dve.tensor_copy(m_parts[:, g, 0, :], ps).then_inc(m1_ok, 1)
                    dve.wait_ge(m1_ok, n)
                    dve.tensor_tensor(m_rest[:, g, :], ps, m_parts[:, g, 0, :], ALU.subtract).then_inc(mr_ok, 1)
                    dve.wait_ge(mr_ok, n)
                    dve.tensor_copy(m_parts[:, g, 1, :], m_rest[:, g, :]).then_inc(m2p_ok, 1)
                    dve.wait_ge(m2p_ok, n)
                    dve.tensor_tensor(m_parts[:, g, 2, :], m_rest[:, g, :], m_parts[:, g, 1, :], ALU.subtract).then_inc(m3_ok, 1)

                def maximum(b, u, slot):
                    pair, t = u // TB, u % TB
                    dve.wait_ge(s_mm, b * PAIRS * TB + u + 1)
                    if u % (2 * TB) == 0 and not first(b):
                        dve.wait_ge(m_tr, (b - 1) * GROUPS + pair // 2 + 1)
                    i = 2 * (pair % 2)
                    dve.tensor_reduce(q_max[:, pair // 2, i:i + 2, t], ring[:, slot, :, :], AX.X, ALU.max).then_inc(smax_ok, 1)

                def quotient(b, p, pair):
                    n = b * PAIRS + pair + 1
                    dve.wait_ge(pv_ok, n)
                    if pair == 0 and not early(b):
                        dve.wait_ge(yn_ok, b - 1)
                    dve.reciprocal(inv_sum[:], y_bank[:, :, :, W2]).then_inc(inv_ok, 1)
                    dve.wait_ge(inv_ok, n)
                    for i in range(2):
                        c = (2 * pair + i) * W2
                        last = dve.tensor_tensor(y[:, p, :, c:c + W2], y_bank[:, i, :, 0:W2],
                                                 inv_sum[:, i, :].unsqueeze(2).to_broadcast([P, TB, W2]), ALU.mult)
                    last.then_inc(y_ok, 1)

                def ln2_stats(b, p):
                    dve.wait_ge(y_ok, b * PAIRS + PAIRS + 1)
                    for t in range(TB):
                        last = dve.bn_stats(stats2[:, t, :], y[:, p, t, :])
                    last.then_inc(st2_ok, 1)
                    dve.wait_ge(st2_ok, b + 1)
                    dve.sem_inc(passed, 1)
                    for t in range(TB):
                        last = dve.bn_aggr(moments2[:, t, :], stats2[:, t, :])
                    last.then_inc(mom2_ok, 1)

                def ln2_apply(b, p):
                    dve.wait_ge(rstd2_ok, b + 1)
                    for t in range(TB):
                        last = dve.tensor_scalar(y[:, p, t, :], y[:, p, t, :], moments2[:, t, 0:1], rstd2[:, t:t + 1], ALU.subtract, ALU.mult)
                    last.then_inc(yn_ok, 1)

                def result(b, t):
                    dve.wait_ge(o_mm, b * OUT + t + 1)
                    dve.wait_ge(res_ld, b * 16 + 16)
                    dve.tensor_tensor(res[:, 2 * t:2 * t + 2, :], misc[:].rearrange("p (k d) -> p k d", d=D), res[:, 2 * t:2 * t + 2, :], ALU.add).then_inc(res_ok, 1)

                @batches
                def run(b, p, has_post, has_next, has_after):
                    n = 0
                    for i in range(2 * HALF_USES):
                        n += 1
                        if i < HALF_USES:
                            maximum(b, HALF_USES + i, n % RING)
                            n += 1
                        elif has_next:
                            maximum(b + 1, i - HALF_USES, n % RING)
                            n += 1
                        if i % TB == 3 and i > TB: quotient(b, p, i // TB - 1)
                        if i == 2: max_parts(b, 1)
                        if has_post:
                            if i == 3: quotient(b - 1, 1 - p, PAIRS - 1)
                            if i == 4: ln2_stats(b - 1, 1 - p)
                            if i == 6: ln2_apply(b - 1, 1 - p)
                            if i in (13, 14): result(b - 1, i - 13)
                        if i == 10: max_parts(b, 2)
                        if i == 18: max_parts(b, 3)
                        if has_after:
                            if i == 10: ln_stats(b + 2)
                            if i == 12: ln_apply(b + 2)
                            if i in (20, 22): split(b + 2, 0, (i - 20) // 2)
                            if i == 24: split(b + 2, 1, 0)
                            if i == 28: split(b + 2, 1, 1)
                        if i == 26 and has_next: max_parts(b + 1, 0)

                def stage_a(b):
                    ln_stats(b)
                    ln_apply(b)
                    for i in range(2):
                        for g in range(DH):
                            split(b, i, g)

                stage_a(0)
                for u in range(HALF_USES):
                    maximum(0, u, u % RING)
                    if u == 10:
                        max_parts(0, 0)
                stage_a(1)
                run(dve)
                quotient(B - 1, (B - 1) % 2, PAIRS - 1)
                ln2_stats(B - 1, (B - 1) % 2)
                ln2_apply(B - 1, (B - 1) % 2)
                for t in range(OUT):
                    result(B - 1, t)

            @block.scalar
            def _(act):
                act.wait_ge(w_ld, 48)
                act.wait_ge(fill_ok, 4)
                act.sem_inc(exp_ok, RING)

                def ln_rstd(b, mom, mom_sem, out, step, ok):
                    act.wait_ge(mom_sem, b + 1)
                    act.activation(out[:], mom[:, :, 1], ACT.Ln, bias=eps[:]).then_inc(step, 1)
                    act.wait_ge(step, b + 1)
                    act.activation(out[:], out[:], ACT.Exp, scale=-0.5).then_inc(ok, 1)

                def xnT_half(b, h):
                    act.wait_ge(xn_tr, b * DH + h + 1)
                    act.activation(xnT[:, h, :], misc[:], ACT.Identity, scale=vec(vecs, "L2_ln_w")[:, h:h + 1],
                                   bias=vec(vecs, "L2_ln_b")[:, h:h + 1]).then_inc(xnT_ok, 1)

                def first_part(b, i, g):
                    act.wait_ge(qk_mm, b * 2 * DH + i * DH + g + 1)
                    if i == 0 and g == 0 and not first(b):
                        act.wait_ge(parts_st, b * 96)
                    act.activation(parts[:, i, 0, g, :], misc[:], ACT.Identity, bias=vec(vecs, "L2_q_bias" if i == 0 else "L2_k_bias")[:, g:g + 1]).then_inc(p1_ok, 1)

                def v_part(b, p, h):
                    act.wait_ge(v_mm, b * OUT + h + 1)
                    if h == 0 and not early(b):
                        act.wait_ge(pv_ok, (b - 1) * PAIRS)
                    for t in (2 * h, 2 * h + 1):
                        last = act.activation(v[:, p, t, :, 0:W2], misc[:, (t % 2) * D:(t % 2 + 1) * D].rearrange("p (h c) -> p h c", c=W2), ACT.Copy,
                                              scale=mask_t[:, bass.ds(b, 1), t])
                    last.then_inc(v_ok, 1)

                def silu_half(b, h):
                    act.wait_ge(yn_tr, b * DH + h + 1)
                    act.activation(hT[:, h, :], misc[:], ACT.Silu, scale=coef[:, 2, 0, h, bass.ds(b, 1)],
                                   bias=coef[:, 2, 1, h, bass.ds(b, 1)]).then_inc(hT_ok, 1)

                @batches
                def run(b, p, has_post, has_next, has_after):
                    n = 0
                    for i in range(2 * HALF_USES):
                        pair, t = i // TB, i % TB
                        act.wait_ge(exp_mm, b * PAIRS * TB + i + 1)
                        if t == 0 and not (first(b) and pair < 2):
                            act.wait_ge(pv_ok, b * PAIRS + pair - 1)
                        act.activation(probs[:, pair % 2, :, t, :], ring[:, n % RING, :, :], ACT.Exp).then_inc(exp_ok, 1)
                        n += 2 if i < HALF_USES or has_next else 1
                        if has_next and i in (4, 6): v_part(b + 1, 1 - p, (i - 4) // 2)
                        if has_post:
                            if i == 5: ln_rstd(b - 1, moments2, mom2_ok, rstd2, ln_b, rstd2_ok)
                            if i in (9, 11): silu_half(b - 1, (i - 9) // 2)
                        if has_after:
                            if i == 11: ln_rstd(b + 2, moments, mom_ok, rstd, ln_a, rstd_ok)
                            if i in (16, 17): xnT_half(b + 2, i - 16)
                            if i in (19, 21): first_part(b + 2, 0, (i - 19) // 2)
                            if i == 23: first_part(b + 2, 1, 0)
                            if i == 27: first_part(b + 2, 1, 1)

                def stage_a(b):
                    ln_rstd(b, moments, mom_ok, rstd, ln_a, rstd_ok)
                    for h in range(DH):
                        xnT_half(b, h)
                    for i in range(2):
                        for g in range(DH):
                            first_part(b, i, g)

                stage_a(0)
                for h in range(OUT):
                    v_part(0, 0, h)
                stage_a(1)
                run(act)
                ln_rstd(B - 1, moments2, mom2_ok, rstd2, ln_b, rstd2_ok)
                for h in range(DH):
                    silu_half(B - 1, h)

            @block.tensor
            def _(pe):
                pe.wait_ge(w_ld, 48)
                pe.wait_ge(fill_ok, 4)
                reader = [None]

                def take(ok, value):
                    if reader[0]:
                        pe.wait_ge(*reader[0])
                    reader[0] = (ok, value)

                def xn_half(b, h):
                    pe.wait_ge(xn_ok, b + 1)
                    take(xnT_ok, b * DH + h + 1)
                    for t in range(TB):
                        last = pe.transpose(misc[:, t * P:(t + 1) * P], x_in[:, t, h * P:(h + 1) * P], ident[:])
                    last.then_inc(xn_tr, 1)

                def project(b, i, g):
                    pe.wait_ge(xnT_ok, b * DH + DH)
                    take(rest_ok, b * 2 * DH + i * DH + g + 1)
                    weight = wq if i == 0 else wk
                    for k in range(DH):
                        last = pe.matmul(misc[:], weight[:, k, g * P:(g + 1) * P], xnT[:, k, :], start=(k == 0), stop=(k == DH - 1))
                    last.then_inc(qk_mm, 1)

                def tokens(src, weight, bias, h):
                    for t in (2 * h, 2 * h + 1):
                        o = misc[:, (t % 2) * D:(t % 2 + 1) * D]
                        for k in range(DH):
                            pe.matmul(o, src[:, k, t * P:(t + 1) * P], weight[:, k, :], start=(k == 0), stop=False)
                        last = pe.matmul(o, ones[0:1, 0:P], row(bias), start=False, stop=True)
                    return last

                def v_rows(b, h):
                    take(v_ok, b * OUT + h + 1)
                    tokens(xnT, wv, "L2_bv", h).then_inc(v_mm, 1)

                def max_rows(b, g):
                    pe.wait_ge(smax_ok, b * PAIRS * TB + (g + 1) * 2 * TB + RING)
                    take(mr_ok, b * GROUPS + g + 1)
                    pe.transpose(misc[0:GH * TB, 0:P], q_max[:, g, :, :].rearrange("p h t -> p (h t)"), ident[:]).then_inc(m_tr, 1)

                def yn_half(b, p, h):
                    pe.wait_ge(yn_ok, b + 1)
                    take(hT_ok, b * DH + h + 1)
                    for t in range(TB):
                        last = pe.transpose(misc[:, t * P:(t + 1) * P], y[:, p, t, h * P:(h + 1) * P], ident[:])
                    last.then_inc(yn_tr, 1)

                def project_out(b, h):
                    pe.wait_ge(hT_ok, b * DH + DH)
                    take(res_ok, b * OUT + h + 1)
                    tokens(hT, wo, "L2_b_out", h).then_inc(o_mm, 1)

                def times_v(b, p, pair):
                    pe.wait_ge(exp_ok, b * PAIRS * TB + (pair + 1) * TB + RING)
                    pe.wait_ge(v_ok, b * OUT + OUT)
                    pe.wait_ge(y_ok, b * PAIRS + pair + 1)
                    for i in range(2):
                        for t in range(TB):
                            for m in range(TB):
                                last = pe.matmul(y_bank[:, i, t, :], probs[:, pair % 2, i, m, t * P:(t + 1) * P], v[:, p, m, 2 * pair + i, :],
                                                 start=(m == 0), stop=(m == TB - 1))
                    last.then_inc(pv_ok, 1)

                def max_scores(b, p, u, slot):
                    pair, t = u // TB, u % TB
                    if u == 0:
                        pe.wait_ge(stack_ld, (b + 1) * 16 * 13)
                    for i in range(2):
                        hd = 2 * pair + i
                        last = pe.matmul(ring[:, slot, i, :], qs[0:MAX_AT, p, hd, t * P:(t + 1) * P], ks[0:MAX_AT, p, hd, :], start=True, stop=True)
                    last.then_inc(s_mm, 1)

                def exp_scores(b, p, u, slot):
                    pair, t = u // TB, u % TB
                    if u % (2 * TB) == 0:
                        pe.wait_ge(m_ld[pair // 2], b * 48 + 48)
                    for i in range(2):
                        hd = 2 * pair + i
                        last = pe.matmul(ring[:, slot, i, :], ks[:, p, hd, t * P:(t + 1) * P], qs[:, p, hd, :], start=True, stop=True)
                    last.then_inc(exp_mm, 1)

                @batches
                def run(b, p, has_post, has_next, has_after):
                    U = PAIRS * TB
                    uses = []

                    def slot_free(n):
                        if n >= RING:
                            pe.wait_ge(*uses[n - RING])
                        else:
                            pe.wait_ge(exp_ok, b * U + RING)
                            pe.wait_ge(smax_ok, b * U + HALF_USES + RING)

                    if has_after and not first(b):
                        reader[0] = (rest_ok, b * 2 * DH + 4 * DH)
                    for i in range(U):
                        slot_free(len(uses))
                        exp_scores(b, p, i, len(uses) % RING)
                        uses.append((exp_ok, b * U + i + 1 + RING))
                        if i < HALF_USES or has_next:
                            bb, u = (b, HALF_USES + i) if i < HALF_USES else (b + 1, i - HALF_USES)
                            slot_free(len(uses))
                            max_scores(bb, p if i < HALF_USES else 1 - p, u, len(uses) % RING)
                            uses.append((smax_ok, bb * U + u + 1 + RING))
                        if i % TB == 1:
                            if i > TB:
                                times_v(b, p, i // TB - 1)
                            elif has_post:
                                times_v(b - 1, 1 - p, PAIRS - 1)
                        if i == 1: max_rows(b, 1)
                        if has_next and i in (3, 5): v_rows(b + 1, (i - 3) // 2)
                        if has_post and i in (8, 10): yn_half(b - 1, 1 - p, (i - 8) // 2)
                        if i == 9: max_rows(b, 2)
                        if has_post and i in (12, 13): project_out(b - 1, i - 12)
                        if has_after and i in (15, 16): xn_half(b + 2, i - 15)
                        if i == 17: max_rows(b, 3)
                        if has_after:
                            if i in (18, 20): project(b + 2, 0, (i - 18) // 2)
                            if i == 22: project(b + 2, 1, 0)
                            if i == 26: project(b + 2, 1, 1)
                        if has_next and i == 25: max_rows(b + 1, 0)

                def stage_a(b):
                    for h in range(DH):
                        xn_half(b, h)
                    for i in range(2):
                        for g in range(DH):
                            project(b, i, g)

                stage_a(0)
                for h in range(OUT):
                    v_rows(0, h)
                for u in range(HALF_USES):
                    if u >= RING:
                        pe.wait_ge(smax_ok, u + 1)
                    max_scores(0, 0, u, u % RING)
                    if u == 9:
                        max_rows(0, 0)
                stage_a(1)
                run(pe)
                times_v(B - 1, (B - 1) % 2, PAIRS - 1)
                for h in range(DH):
                    yn_half(B - 1, (B - 1) % 2, h)
                for h in range(OUT):
                    project_out(B - 1, h)
        sems.clear("layer2_clear")


def build(nc, io):
    with ExitStack() as ctx:
        sb = lambda name, shape: ctx.enter_context(nc.sbuf_tensor(name, shape, F32))
        keep = {
            "vecs": sb("vecs", [P, NVEC]),
            "rows": sb("rows", [1, len(ROWS) * D]),
            "ident": sb("ident", [P, P]),
            "ones": sb("ones", [1, T]),
            "eps": sb("eps", [P, 1]),
            "coef": sb("coef", [P, 4, 2, DH, B]),
            "x1_stored": [ctx.enter_context(nc.semaphore(f"x1_stored_{p}")) for p in ("even", "odd")],
        }
        setup_block(nc, io, keep)
        linear_attention(nc, io, keep)
        mamba(nc, io, keep, 1, io["x1"], io["x2"], False)
        softmax_attention(nc, io, keep)
        mamba(nc, io, keep, 3, io["x3"], io["out"], True)


def _halves(a, n):
    return np.ascontiguousarray(np.asarray(a).reshape(n, P).T)


def _blocks(a):
    a = np.asarray(a)
    return np.ascontiguousarray(a.reshape(-1, P, a.shape[1]).transpose(1, 0, 2))


def _layout(i):
    f = {k: np.asarray(v) for k, v in i.items()}
    vecs = np.zeros((P, NVEC), np.float32)

    def put(name, a):
        c, n = VEC_LAYOUT[name]
        vecs[:, c:c + n] = a

    for l, ln, ln2, eb in (("L0", "ln", "ln2", "b_emb"), ("L2", "norm", "sb_norm", "emb_b")):
        put(l + "_ln_w", _halves(f[f"{l}_cond_{ln}_w"], DH))
        put(l + "_ln_b", _halves(f[f"{l}_cond_{ln}_b"], DH))
        put(l + "_ln2_w", _halves(f[f"{l}_cond_{ln2}_w"], DH))
        put(l + "_ln2_b", _halves(f[f"{l}_cond_{ln2}_b"], DH))
        put(l + "_scale_b", _halves(f[f"{l}_cond_{eb}"][:D], DH))
        put(l + "_shift_b", _halves(f[f"{l}_cond_{eb}"][D:], DH))
    for name in ("q", "k"):
        put(f"L2_{name}_bias", _halves(f[f"L2_cond_{name}_b"], DH))
    m = {1: ("ln_g", "ln_b", "ada_b", "dt_proj_b"), 3: ("gamma", "beta", "b_ada", "b_dt")}
    for l, (g, bb, ab, db) in m.items():
        c = f"L{l}_cond_"
        put(f"L{l}_ln_w", _halves(f[c + g], DH))
        put(f"L{l}_ln_b", _halves(f[c + bb], DH))
        put(f"L{l}_shift_b", _halves(f[c + ab][:D], DH))
        put(f"L{l}_scale_b", _halves(f[c + ab][D:2 * D], DH))
        put(f"L{l}_conv_b", _halves(f[c + "conv_b"], JB))
        put(f"L{l}_dt_b", _halves(f[c + db], JB))
        put(f"L{l}_D", _halves(f[c + "D_param"], JB))
        put(f"L{l}_conv_w", _blocks(f[c + "conv_w"].reshape(DI, TAPS)).reshape(P, JB * TAPS))
        put(f"L{l}_A_log", _blocks(f[c + "A_log"]).reshape(P, JB * N))
    rows = np.concatenate([f["L0_cond_bq"], f["L0_cond_bk"], f["L0_cond_bv"], f["L0_cond_b_out"], f["L2_cond_v_b"],
                           f["L2_cond_out_b"], f["L1_cond_ada_b"][2 * D:], f["L3_cond_b_ada"][2 * D:]])[None, :]
    cond_w = np.concatenate([f["L0_cond_W_emb"], f["L2_cond_emb_w"], f["L1_cond_ada_w"].T, f["L3_cond_W_ada"]], axis=1)
    out = {
        "x": f["x"].reshape(B * T, D),
        "cond_t": _blocks(f["cond_2048"].T),
        "cond_w": _blocks(cond_w),
        "vecs": vecs,
        "rows": rows,
        "mask_k": f["mask_BxSx1_fk1"].reshape(B, T),
        "mask_t": np.ascontiguousarray(f["mask_BxSx1_fk1"].reshape(B, TB, P).transpose(2, 0, 1)),
        "L0_w": _blocks(np.concatenate([f["L0_cond_Wq"], f["L0_cond_Wk"], f["L0_cond_Wv"], f["L0_cond_W_out"]], axis=1)),
    }
    out["L2_w"] = _blocks(np.concatenate([f[f"L2_cond_{n}_w"] for n in ("q", "k", "v", "out")], axis=1))
    out["mask2_k"] = f["mask_BxS_ff1"]
    out["mask2_t"] = np.ascontiguousarray(f["mask_BxS_ff1"].reshape(B, TB, P).transpose(2, 0, 1))
    for l, names, t in (("L1", ("in_proj_w", "x_proj_w", "dt_proj_w", "out_proj_w"), True), ("L3", ("W_in", "W_xp", "W_dt", "W_out"), False)):
        w = [f[f"{l}_cond_{n}"] for n in names]
        w = [a.T for a in w] if t else w
        out[l + "_w_in"], out[l + "_w_x"], out[l + "_w_dt"], out[l + "_w_out"] = _blocks(w[0]), _blocks(w[1]), w[2], _blocks(w[3])
    out["idx"] = np.ascontiguousarray(f["itok_S_0_1023"].reshape(TB, P).T)
    return {k: np.ascontiguousarray(v) for k, v in out.items()}


def kernel(**inputs):
    import concourse.bacc as _bacc
    from concourse.bass_utils import run_bass_kernel_spmd as _run

    nc = _bacc.Bacc("TRN2", target_bir_lowering=False, num_devices=1)
    arrays, io = {}, {}
    for name, a in _layout(inputs).items():
        arrays[f"in_{name}"] = a
        io[name] = nc.dram_tensor(f"in_{name}", a.shape, mybir.dt.from_np(a.dtype), kind="ExternalInput").ap()
    io["out"] = nc.dram_tensor("out_0_dram", (B * T, D), F32, kind="ExternalOutput").ap()
    for name in ("x1", "x2", "x3"):
        io[name] = nc.dram_tensor(name + "_dram", (B * T, D), F32).ap()
    for name in ("y_even", "y_odd"):
        io[name] = nc.dram_tensor(name + "_dram", (T, D), F32).ap()
    io["parts"] = nc.dram_tensor("parts_dram", (2, 2, 3, D, T), BF16).ap()
    io["mask_parts"] = nc.dram_tensor("mask_parts_dram", (B, 3, T), BF16).ap()
    io["gates"] = nc.dram_tensor("gates_dram", (2, B, D), F32).ap()
    io["c_rows"] = nc.dram_tensor("c_rows_dram", (2, N, T), F32).ap()
    build(nc, io)
    r = _run(nc, [arrays], core_ids=[0])
    return r.results[0]["out_0_dram"].reshape(B, T, D)
```

```python
from contextlib import ExitStack

import numpy as np

import concourse.bass as bass
from concourse import mybir

F32 = mybir.dt.float32
I32 = mybir.dt.int32
BF16 = mybir.dt.bfloat16
ALU = mybir.AluOpType
ACT = mybir.ActivationFunctionType
AX = mybir.AxisListType

P = 128
B, T, D = 8, 512, 256
TB = T // P
DH = D // P
TE = 512
KE = TE // P
H0 = 8
W0 = D // H0
H2 = 16
W2 = D // H2
DI = 512
JB = DI // P
N = 16
R = 64
XD = R + 2 * N
TAPS = 4
EPS = 1e-5
MASKED = 1000000.0

VEC_LAYOUT = {}
_at = 0
for _name, _n in (
    [("L0_ln_w", DH), ("L0_ln_b", DH), ("L0_ln2_w", DH), ("L0_ln2_b", DH), ("L0_scale_b", DH), ("L0_shift_b", DH),
     ("L2_ln_w", DH), ("L2_ln_b", DH), ("L2_ln2_w", DH), ("L2_ln2_b", DH), ("L2_scale_b", DH), ("L2_shift_b", DH),
     ("L2_q_bias", DH), ("L2_k_bias", DH)]
    + [(f"L{l}_{n}", c) for l in (1, 3) for n, c in (
        ("ln_w", DH), ("ln_b", DH), ("shift_b", DH), ("scale_b", DH), ("conv_b", JB), ("dt_b", JB),
        ("D", JB), ("conv_w", JB * TAPS), ("A_log", JB * N))]
):
    VEC_LAYOUT[_name] = (_at, _n)
    _at += _n
NVEC = _at
ROWS = ["L0_bq", "L0_bk", "L0_bv", "L0_b_out", "L2_bv", "L2_b_out", "L1_gate_b", "L3_gate_b"]
COND_AT = {"L0": 0, "L2": 2 * D, "L1": 4 * D, "L3": 7 * D}
COND_W = 10 * D
STYLE = ("L0", "L1", "L2", "L3")


def vec(tile, name):
    a, n = VEC_LAYOUT[name]
    return tile[:, a:a + n]


class Chain:

    def __init__(self, eng, sem, per, b):
        self.eng, self.sem, self.per, self.base, self.n = eng, sem, per, b * per, 0

    def link(self, ins):
        ins.then_inc(self.sem, 1)
        self.n += 1
        self.eng.wait_ge(self.sem, self.base + self.n)

    def end(self):
        assert self.n == self.per, (self.n, self.per)


class Semaphores:

    def __init__(self, nc, ctx):
        self.nc, self.ctx, self.all = nc, ctx, []

    def __call__(self, name):
        self.all.append(self.ctx.enter_context(self.nc.semaphore(name)))
        return self.all[-1]

    def clear(self, name):
        with self.nc.Block(name) as block:
            @block.sync
            def _(sp):
                for s in self.all:
                    sp.sem_clear(s)


def setup_block(nc, io, keep):
    with ExitStack() as ctx:
        sb = lambda name, shape: ctx.enter_context(nc.sbuf_tensor(name, shape, F32))
        sems = Semaphores(nc, ctx)
        sem = lambda name: sems(name)
        cond_w = sb("su_cond_w", [P, KE, COND_W])
        cond_t = sb("su_cond_t", [P, KE, B])
        silu_c = sb("su_silu_c", [P, KE, B])
        raw = sb("su_raw", [P, 4, 2 * DH, B])
        one_b = sb("su_one_b", [1, B])
        gates = sb("su_gates", [B, 2, D])
        bias2 = sb("su_bias2", [P, 4, 2 * DH, B])
        ps = ctx.enter_context(nc.psum_tensor("su_ps", [P, 4, 2 * DH * B], F32))
        ps_gate = ctx.enter_context(nc.psum_tensor("su_ps_gate", [P, 2, D], F32))
        vecs, ident, ones, eps, coef = (keep[k] for k in ("vecs", "ident", "ones", "eps", "coef"))
        rows = sb("su_rows", [1, len(ROWS) * D])
        loaded, weights_in, filled, diag_done = sem("su_loaded"), sem("su_weights_in"), sem("su_filled"), sem("su_diag")
        silu_done, mm_done, gate_mm, gate_out, stored, steps = (
            sem("su_silu"), sem("su_mm"), sem("su_gate_mm"), sem("su_gate_out"), sem("su_stored"), sem("su_steps"))

        with nc.Block("setup") as block:
            @block.sync
            def _(sp):
                sp.dma_start(cond_t[:], io["cond_t"]).then_inc(loaded, 16)
                sp.dma_start(vecs[:], io["vecs"]).then_inc(loaded, 16)
                sp.dma_start(rows[:], io["rows"]).then_inc(loaded, 16)
                sp.dma_start(cond_w[:], io["cond_w"]).then_inc(weights_in, 16)
                sp.wait_ge(gate_out, 1)
                sp.dma_start(io["gates"].rearrange("l b d -> b l d"), gates[:]).then_inc(stored, 16)
                sp.wait_ge(stored, 16)

            @block.gpsimd
            def _(pool):
                pool.memset(ident[:], 0.0).then_inc(filled, 1)
                pool.memset(ones[:], 1.0).then_inc(filled, 1)
                pool.memset(eps[:], EPS).then_inc(filled, 1)
                pool.memset(one_b[:], 1.0).then_inc(filled, 1)
                pool.wait_ge(filled, 4)
                pool.affine_select(out=ident[:], in_=ident[:], compare_op=ALU.not_equal, fill=1.0, base=0,
                                   pattern=[[-1, P]], channel_multiplier=1).then_inc(diag_done, 1)

            @block.scalar
            def _(act):
                act.wait_ge(loaded, 48)
                act.activation(silu_c[:], cond_t[:], ACT.Silu).then_inc(silu_done, 1)

            @block.tensor
            def _(pe):
                pe.wait_ge(silu_done, 1)
                pe.wait_ge(weights_in, 16)
                pe.wait_ge(filled, 4)
                for l, name in enumerate(STYLE):
                    for part in range(2 * DH):
                        first = part if name in ("L0", "L2") else (part + DH) % (2 * DH)
                        c = COND_AT[name] + first * P
                        for k in range(KE):
                            last = pe.matmul(ps[:, l, part * B:(part + 1) * B], cond_w[:, k, c:c + P], silu_c[:, k, :],
                                             start=(k == 0), stop=(k == KE - 1))
                last.then_inc(mm_done, 1)
                for l, name in enumerate(("L1", "L3")):
                    c = COND_AT[name] + 2 * D
                    for k in range(KE):
                        pe.matmul(ps_gate[0:B, l, :], silu_c[:, k, :], cond_w[:, k, c:c + D], start=(k == 0), stop=False)
                    r = ROWS.index(name + "_gate_b")
                    last = pe.matmul(ps_gate[0:B, l, :], one_b[:], rows[:, r * D:(r + 1) * D], start=False, stop=True)
                last.then_inc(gate_mm, 1)

            @block.vector
            def _(dve):
                chain = Chain(dve, steps, 12, 0)
                dve.wait_ge(loaded, 48)
                dve.wait_ge(mm_done, 1)
                for l, name in enumerate(STYLE):
                    two = "2" if name in ("L0", "L2") else ""
                    bias = vecs[:, VEC_LAYOUT[name + "_scale_b"][0]:VEC_LAYOUT[name + "_scale_b"][0] + DH]
                    sbias = vecs[:, VEC_LAYOUT[name + "_shift_b"][0]:VEC_LAYOUT[name + "_shift_b"][0] + DH]
                    w, bb = vec(vecs, f"{name}_ln{two}_w"), vec(vecs, f"{name}_ln{two}_b")
                    v = ps[:, l, :].rearrange("p (q b) -> p q b", b=B)
                    for h in range(DH):
                        last = dve.tensor_scalar(raw[:, l, h, :], v[:, h, :], bias[:, h:h + 1], 1.0, ALU.add, ALU.add)
                    chain.link(last)
                    for h in range(DH):
                        dve.tensor_scalar(raw[:, l, DH + h, :], v[:, DH + h, :], sbias[:, h:h + 1], None, ALU.add)
                        dve.tensor_scalar(coef[:, l, 0, h, :], raw[:, l, h, :], w[:, h:h + 1], None, ALU.mult)
                        last = dve.tensor_scalar(bias2[:, l, h, :], raw[:, l, h, :], bb[:, h:h + 1], None, ALU.mult)
                    chain.link(last)
                    for h in range(DH):
                        last = dve.tensor_tensor(coef[:, l, 1, h, :], bias2[:, l, h, :], raw[:, l, DH + h, :], ALU.add)
                    chain.link(last)
                chain.end()
                dve.wait_ge(gate_mm, 1)
                dve.tensor_copy(gates[:], ps_gate[0:B, :, :]).then_inc(gate_out, 1)
        sems.clear("setup_clear")


def linear_attention(nc, io, keep):
    with ExitStack() as ctx:
        sb = lambda name, shape: ctx.enter_context(nc.sbuf_tensor("l0_" + name, shape, F32))
        sems = Semaphores(nc, ctx)
        sem = lambda name: sems("l0_" + name)
        pb = lambda name: ctx.enter_context(nc.psum_tensor("l0_" + name, [P, 2, T], F32))
        vecs, ident, ones, eps, coef = (keep[k] for k in ("vecs", "ident", "ones", "eps", "coef"))
        rows = sb("rows", [1, len(ROWS) * D])
        w = sb("w", [P, DH, 4 * D])
        wq, wk, wv, wo = (w[:, :, i * D:(i + 1) * D] for i in range(4))
        mask_t = sb("mask_t", [P, B, TB])
        mask_row = sb("mask_row", [1, 2, T])
        mask_add = sb("mask_add", [1, 2, T])
        heads = sb("heads", [P, P])
        x_in = sb("x_in", [P, 2, TB, D])
        xn = sb("xn", [P, TB, D])
        xnT = sb("xnT", [P, DH, T])
        stats, moments, rstd = sb("stats", [P, TB, 6]), sb("moments", [P, TB, 2]), sb("rstd", [P, TB])
        stats2, moments2, rstd2 = sb("stats2", [P, TB, 6]), sb("moments2", [P, TB, 2]), sb("rstd2", [P, TB])
        q = sb("q", [P, TB * D])
        q_max, q_sum = sb("q_max", [P, TB * H0]), sb("q_sum", [P, TB * H0])
        k_exp = sb("k_exp", [P, DH, T])
        k_max, k_sum = sb("k_max", [P, DH]), sb("k_sum", [P, DH])
        k_tok = sb("k_tok", [P, TB, D])
        v = sb("v", [P, TB, D])
        qT = sb("qT", [P, DH, T])
        att = sb("att", [P, DH, P])
        yn = sb("yn", [P, TB, D])
        hT = sb("hT", [P, DH, T])
        res = sb("res", [P, 2, TB, D])
        ps_t, ps_q, ps_k, ps_v = pb("ps_t"), pb("ps_q"), pb("ps_k"), pb("ps_v")

        w_in, x_ld, mask_ld, heads_ok, stored = sem("w_in"), [sem("x_ld_even"), sem("x_ld_odd")], [sem("mask_ld_even"), sem("mask_ld_odd")], sem("heads_ok"), keep["x1_stored"]
        moments_ok, rstd_ok, xn_ok, xn_tr, xnT_ok, madd_ok = (
            sem("moments"), sem("rstd"), sem("xn"), sem("xn_tr"), sem("xnT"), sem("madd"))
        q_mm, k_mm, v_mm, q_sub, q_exp, q_ok, kmax_ok, kexp_ok, k_tr, ktok_ok, v_ok, rks_ok = (
            sem("q_mm"), sem("k_mm"), sem("v_mm"), sem("q_sub"), sem("q_exp"), sem("q_ok"), sem("kmax"), sem("kexp"),
            sem("k_tr"), sem("ktok"), sem("v_ok"), sem("rks"))
        att_mm, att_ok, q_tr, qT_ok, y_mm, m2_ok, rstd2_ok, yn_ok, yn_tr, hT_ok, o_mm, res_ok, a_steps, v_steps = (
            sem("att_mm"), sem("att_ok"), sem("q_tr"), sem("qT_ok"), sem("y_mm"), sem("m2"), sem("rstd2"), sem("yn"),
            sem("yn_tr"), sem("hT"), sem("o_mm"), sem("res"), sem("a_steps"), sem("v_steps"))

        def row(name):
            r = ROWS.index(name)
            return rows[:, r * D:(r + 1) * D]

        passed_v, res_free = sem("passed_v"), sem("res_free")

        with nc.Block("layer0") as block:
            @block.sync
            def _(sp):
                sp.dma_start(w[:], io["L0_w"]).then_inc(w_in, 16)
                sp.dma_start(mask_t[:], io["mask_t"]).then_inc(w_in, 16)
                sp.dma_start(rows[:], io["rows"]).then_inc(w_in, 16)
                with sp.Fori(0, B // 2) as pair:
                    for p in range(2):
                        b = pair * 2 + p
                        sp.wait_ge(res_ok, b + 1)
                        sp.dma_start(x_in[:, p, :, :], io["x"][bass.ds(b * T, T), :].rearrange("(k p) d -> p k d", p=P)).then_inc(x_ld[p], 16)
                        sp.dma_start(mask_row[:, p, :], io["mask_k"][bass.ds(b, 1), :]).then_inc(mask_ld[p], 16)
                for s in stored:
                    sp.wait_ge(s, 16 * (B // 2))

            @block.gpsimd
            def _(pool):
                pool.sem_inc(res_free, 2)
                pool.memset(heads[:], 0.0).then_inc(heads_ok, 1)
                pool.wait_ge(heads_ok, 1)
                for h in range(P // W0):
                    last = pool.memset(heads[h * W0:(h + 1) * W0, h * W0:(h + 1) * W0], 1.0)
                last.then_inc(heads_ok, 1)
                with pool.Fori(0, B // 2) as pair:
                    for p in range(2):
                        b = pair * 2 + p
                        pool.wait_ge(res_ok, b + 3)
                        pool.dma_start(io["x1"][bass.ds(b * T, T), :].rearrange("(k p) d -> p k d", p=P), res[:, p, :, :]).then_inc(stored[p], 16)
                        pool.wait_ge(stored[p], pair * 16 + 16)
                        pool.sem_inc(res_free, 1)

            @block.vector
            def _(dve):
                dve.sem_inc(res_ok, 2)
                dve.wait_ge(heads_ok, 2)
                with dve.Fori(0, B // 2) as pair:
                    for p in range(2):
                        b = pair * 2 + p
                        chain = Chain(dve, v_steps, 6, b)
                        dve.wait_ge(mask_ld[p], pair * 16 + 16)
                        dve.tensor_scalar(mask_add[:, p, :], mask_row[:, p, :], 1.0, MASKED, ALU.subtract, ALU.mult).then_inc(madd_ok, 1)
                        dve.wait_ge(x_ld[p], pair * 16 + 16)
                        for t in range(TB):
                            last = dve.bn_stats(stats[:, t, :], x_in[:, p, t, :])
                        chain.link(last)
                        dve.sem_inc(passed_v, 1)
                        for t in range(TB):
                            last = dve.bn_aggr(moments[:, t, :], stats[:, t, :])
                        last.then_inc(moments_ok, 1)
                        dve.wait_ge(rstd_ok, b + 1)
                        for t in range(TB):
                            last = dve.tensor_scalar(xn[:, t, :], x_in[:, p, t, :], moments[:, t, 0:1], rstd[:, t:t + 1],
                                                     ALU.subtract, ALU.mult)
                        last.then_inc(xn_ok, 1)
                        dve.wait_ge(q_mm, b + 1)
                        qv = ps_q[:].rearrange("p a (g c) -> p (a g) c", c=W0)
                        q3 = q[:].rearrange("p (g c) -> p g c", c=W0)
                        chain.link(dve.tensor_reduce(q_max[:], qv, AX.X, ALU.max))
                        dve.tensor_tensor(q3, qv, q_max[:].unsqueeze(2).to_broadcast([P, TB * H0, W0]), ALU.subtract).then_inc(q_sub, 1)
                        dve.wait_ge(k_mm, b + 1)
                        for h in range(DH):
                            last = dve.tensor_reduce(k_max[:, h:h + 1], ps_k[:, h, :], AX.X, ALU.max, negate=True)
                        last.then_inc(kmax_ok, 1)
                        dve.wait_ge(q_exp, b + 1)
                        chain.link(dve.tensor_reduce(q_sum[:], q3, AX.X, ALU.add))
                        chain.link(dve.reciprocal(q_sum[:], q_sum[:]))
                        dve.tensor_tensor(q3, q3, q_sum[:].unsqueeze(2).to_broadcast([P, TB * H0, W0]), ALU.mult).then_inc(q_ok, 1)
                        dve.wait_ge(kexp_ok, b + 1)
                        chain.link(dve.reciprocal(k_sum[:], k_sum[:]))
                        dve.wait_ge(att_mm, b + 1)
                        for h in range(DH):
                            last = dve.scalar_tensor_tensor(att[:, h, :], ps_q[:, h, 0:P], k_sum[:, h:h + 1], heads[:], ALU.mult, ALU.mult)
                        last.then_inc(att_ok, 1)
                        dve.wait_ge(y_mm, b + 1)
                        yv = ps_v[:].rearrange("p a (k d) -> p (a k) d", d=D)
                        for t in range(TB):
                            last = dve.bn_stats(stats2[:, t, :], yv[:, t, :])
                        chain.link(last)
                        dve.sem_inc(passed_v, 1)
                        for t in range(TB):
                            last = dve.bn_aggr(moments2[:, t, :], stats2[:, t, :])
                        last.then_inc(m2_ok, 1)
                        dve.wait_ge(rstd2_ok, b + 1)
                        for t in range(TB):
                            last = dve.tensor_scalar(yn[:, t, :], yv[:, t, :], moments2[:, t, 0:1], rstd2[:, t:t + 1],
                                                     ALU.subtract, ALU.mult)
                        last.then_inc(yn_ok, 1)
                        dve.wait_ge(o_mm, b + 1)
                        dve.wait_ge(res_free, b + 1)
                        dve.tensor_tensor(res[:, p, :, :].rearrange("p k d -> p (k d)"), ps_k[:].rearrange("p a c -> p (a c)"),
                                          x_in[:, p, :, :].rearrange("p k d -> p (k d)"), ALU.add).then_inc(res_ok, 1)
                        chain.end()

            @block.scalar
            def _(act):
                act.sem_inc(hT_ok, 1)
                act.wait_ge(w_in, 48)
                act.preload_act_table_set(EXP_LN)
                with act.Fori(0, B // 2) as pair:
                    for p in range(2):
                        b = pair * 2 + p
                        chain = Chain(act, a_steps, 2, b)
                        act.wait_ge(moments_ok, b + 1)
                        chain.link(act.activation(rstd[:], moments[:, :, 1], ACT.Ln, bias=eps[:]))
                        act.activation(rstd[:], rstd[:], ACT.Exp, scale=-0.5).then_inc(rstd_ok, 1)
                        act.wait_ge(xn_tr, b + 1)
                        for h in range(DH):
                            last = act.activation(xnT[:, h, :], ps_t[:, h, :], ACT.Identity, scale=vec(vecs, "L0_ln_w")[:, h:h + 1],
                                                  bias=vec(vecs, "L0_ln_b")[:, h:h + 1])
                        last.then_inc(xnT_ok, 1)
                        act.wait_ge(q_sub, b + 1)
                        act.activation(q[:], q[:], ACT.Exp).then_inc(q_exp, 1)
                        act.wait_ge(kmax_ok, b + 1)
                        for h in range(DH):
                            last = act.activation(k_exp[:, h, :], ps_k[:, h, :], ACT.Exp, bias=k_max[:, h:h + 1], accum_out=k_sum[:, h:h + 1])
                        last.then_inc(kexp_ok, 1)
                        act.wait_ge(v_mm, b + 1)
                        vv = ps_v[:].rearrange("p a (k d) -> p (a k) d", d=D)
                        for t in range(TB):
                            last = act.activation(v[:, t, :], vv[:, t, :], ACT.Copy, scale=mask_t[:, bass.ds(b, 1), t])
                        last.then_inc(v_ok, 1)
                        act.wait_ge(k_tr, b + 1)
                        act.activation(k_tok[:].rearrange("p k d -> p (k d)"), ps_t[:].rearrange("p a c -> p (a c)"), ACT.Copy).then_inc(ktok_ok, 1)
                        act.wait_ge(q_tr, b + 1)
                        act.activation(qT[:], ps_t[:], ACT.Copy).then_inc(qT_ok, 1)
                        act.wait_ge(m2_ok, b + 1)
                        chain.link(act.activation(rstd2[:], moments2[:, :, 1], ACT.Ln, bias=eps[:]))
                        act.activation(rstd2[:], rstd2[:], ACT.Exp, scale=-0.5).then_inc(rstd2_ok, 1)
                        act.wait_ge(yn_tr, b + 1)
                        for h in range(DH):
                            last = act.activation(hT[:, h, :], ps_t[:, h, :], ACT.Silu, scale=coef[:, 0, 0, h, bass.ds(b, 1)],
                                                  bias=coef[:, 0, 1, h, bass.ds(b, 1)])
                        last.then_inc(hT_ok, 1)
                        act.preload_act_table_set(EXP_LN)
                        chain.end()

            @block.tensor
            def _(pe):
                pe.wait_ge(w_in, 48)
                with pe.Fori(0, B // 2) as pair:
                    for p in range(2):
                        b = pair * 2 + p

                        def transposed(src):
                            for h in range(DH):
                                for t in range(TB):
                                    last = pe.transpose(ps_t[:, h, t * P:(t + 1) * P], src[:, t, h * P:(h + 1) * P], ident[:])
                            return last

                        pe.wait_ge(xn_ok, b + 1)
                        pe.wait_ge(hT_ok, b + 1)
                        transposed(xn).then_inc(xn_tr, 1)
                        pe.wait_ge(xnT_ok, b + 1)
                        qv = ps_q[:].rearrange("p a (k d) -> p (a k) d", d=D)
                        vv = ps_v[:].rearrange("p a (k d) -> p (a k) d", d=D)
                        ov = ps_k[:].rearrange("p a (k d) -> p (a k) d", d=D)

                        def project(dst, src, weight, bias):
                            for t in range(TB):
                                for k in range(DH):
                                    pe.matmul(dst[:, t, :], src[:, k, t * P:(t + 1) * P], weight[:, k, :], start=(k == 0), stop=False)
                                last = pe.matmul(dst[:, t, :], ones[0:1, 0:P], bias, start=False, stop=True)
                            return last

                        project(qv, xnT, wq, row("L0_bq")).then_inc(q_mm, 1)
                        pe.wait_ge(madd_ok, b + 1)
                        pe.wait_ge(res_ok, b + 2)
                        for h in range(DH):
                            for k in range(DH):
                                pe.matmul(ps_k[:, h, :], wk[:, k, h * P:(h + 1) * P], xnT[:, k, :], start=(k == 0), stop=False)
                            pe.matmul(ps_k[:, h, :], row("L0_bk")[:, h * P:(h + 1) * P], ones[0:1, :], start=False, stop=False)
                            last = pe.matmul(ps_k[:, h, :], ones[0:1, 0:P], mask_add[:, p, :], start=False, stop=True)
                        last.then_inc(k_mm, 1)
                        project(vv, xnT, wv, row("L0_bv")).then_inc(v_mm, 1)
                        pe.wait_ge(kexp_ok, b + 1)
                        for t in range(TB):
                            for h in range(DH):
                                last = pe.transpose(ps_t[:].rearrange("p a (k d) -> p (a k) d", d=D)[:, t, h * P:(h + 1) * P],
                                                    k_exp[:, h, t * P:(t + 1) * P], ident[:])
                        last.then_inc(k_tr, 1)
                        pe.wait_ge(ktok_ok, b + 1)
                        pe.wait_ge(v_ok, b + 1)
                        pe.wait_ge(q_sub, b + 1)
                        for h in range(DH):
                            for t in range(TB):
                                last = pe.matmul(ps_q[:, h, 0:P], k_tok[:, t, h * P:(h + 1) * P], v[:, t, h * P:(h + 1) * P],
                                                 start=(t == 0), stop=(t == TB - 1))
                        last.then_inc(att_mm, 1)
                        pe.wait_ge(q_ok, b + 1)
                        transposed(q[:].rearrange("p (k d) -> p k d", d=D)).then_inc(q_tr, 1)
                        pe.wait_ge(qT_ok, b + 1)
                        pe.wait_ge(att_ok, b + 1)
                        for t in range(TB):
                            for h in range(DH):
                                last = pe.matmul(vv[:, t, h * P:(h + 1) * P], qT[:, h, t * P:(t + 1) * P], att[:, h, :], start=True, stop=True)
                        last.then_inc(y_mm, 1)
                        pe.wait_ge(yn_ok, b + 1)
                        transposed(yn).then_inc(yn_tr, 1)
                        pe.wait_ge(hT_ok, b + 2)
                        project(ov, hT, wo, row("L0_b_out")).then_inc(o_mm, 1)
        sems.clear("layer0_clear")


UNITS = N * JB
DA_RING, DBU_RING = 4, 3
PAIRED = UNITS // 2
ADD_LAG, SUM_LAG = 2, 4
EXP_LN = "natural_log_exp_and_others"
CREDIT = 8
C_GROUP = 4
C_LOADS = N // C_GROUP
OUT_PARTS = TB // 2
PREP_V = 1 + JB * (TAPS - 1)


def dbu_slot(s):
    return s % DBU_RING


def dbu_back(s):
    if s >= DBU_RING:
        return DBU_RING
    return next(d for d in range(1, UNITS + 1) if d > s and dbu_slot(s - d + UNITS) == dbu_slot(s))


def h_slot(s):
    n, j = s // JB, s % JB
    return 2 * JB + j if n % 2 else n // 2 % 2 * JB + j


def pair_of(s):
    return s // (2 * JB) * JB + s % JB, s - JB


def mamba(nc, io, keep, layer, src, dst, gathered):
    pre = f"l{layer}_"
    L = f"L{layer}"
    li = STYLE.index(L)
    with ExitStack() as ctx:
        sb = lambda name, shape, dt=F32: ctx.enter_context(nc.sbuf_tensor(pre + name, shape, dt))
        sems = Semaphores(nc, ctx)
        sem = lambda name: sems(pre + name)
        vecs, ident, eps, coef = (keep[k] for k in ("vecs", "ident", "eps", "coef"))
        w_in, w_x, w_dt, w_out = sb("w_in", [P, DH, 2 * DI]), sb("w_x", [P, JB, XD]), sb("w_dt", [R, DI]), sb("w_out", [P, JB, D])
        gate = sb("gate", [P, B, D])
        a_neg = sb("a_neg", [P, JB * N])
        x_in = sb("x_in", [P, TB, D])
        stats, moments, rstd = sb("stats", [P, TB, 6]), sb("moments", [P, TB, 2]), sb("rstd", [P, TB])
        modT = sb("modT", [P, DH, T])
        conv_in = sb("conv_in", [P, JB, T + TAPS - 1])
        work = sb("work", [P, JB, T])
        u = sb("u", [P, 2, JB, T])
        z = sb("z", [P, 2, JB, T])
        x_dbl = sb("x_dbl", [XD, 2, T])
        dt_in = conv_in[:, :, TAPS - 1:]
        dt = sb("dt", [P, 2, JB, T])
        duT = sb("duT", [P, 2, TB, DI])
        b_tok = sb("b_tok", [P, 2, TB, N])
        c_all = sb("c_all", [P, 2, C_GROUP, T])
        dub = sb("dub", [P, 2, TB, DI])
        dA = sb("dA", [P, DA_RING, T])
        h = sb("h", [P, 3 * JB, T])
        y = sb("y", [P, JB, T])
        og = sb("og", [P, 2, 2, D])
        res = sb("res", [P, TB, D])
        x_loads = TB if gathered else 1
        res_steps = 1 if gathered else OUT_PARTS
        idx = idx_x = y_rows = None
        if gathered:
            idx = sb("idx", [P, TB], I32)
            idx_x = sb("idx_x", [P, TB], I32)
            y_rows = sb("y_rows", [P, TB, D])
        ps_y = ctx.enter_context(nc.psum_tensor(pre + "ps_y", [P, JB, T], F32))
        ps_dbu = ctx.enter_context(nc.psum_tensor(pre + "ps_dbu", [P, DBU_RING, T], F32))
        misc = ctx.enter_context(nc.psum_tensor(pre + "misc", [P, T], F32))

        w_ld, a_exp_ok, pad_ok, x_ld, idx_ld, idx_ok = sem("w_ld"), sem("a_exp"), sem("pad"), sem("x_ld"), sem("idx_ld"), sem("idx_ok")
        mom_ok, rstd_ok, xn_ok, xn_tr, mod_ok = sem("mom"), sem("rstd"), sem("xn"), sem("xn_tr"), sem("mod")
        in_mm, xc_ok, conv_ok, z_ok, u_ok, xd_mm, xd_ok, b_tr, b_ok = (
            sem("in_mm"), sem("xc"), sem("conv"), sem("z"), sem("u"), sem("xd_mm"), sem("xd"), sem("b_tr"), sem("b"))
        dt_mm, dti_ok, clip_ok, ln_ok, dt_ok, du_ok, duT_tr, duT_ok = (
            sem("dt_mm"), sem("dti"), sem("clip"), sem("ln"), sem("dt"), sem("du"), sem("duT_tr"), sem("duT"))
        c_st, c_ld = sem("c_st"), [sem("c_ld0"), sem("c_ld1")]
        dub_ok, da_ok, dbu_ok, scan_ok, hc_ok, add_ok, sum_ok = (
            sem("dub"), sem("da"), sem("dbu"), sem("scan"), sem("hc"), sem("add"), sem("sum"))
        y_ok, yg_ok, out_mm, og_ok, res_ld, res_ok, stored, y_st, yr_ld = (
            sem("y"), sem("yg"), sem("out_mm"), sem("og"), sem("res_ld"), sem("res"), sem("stored"), sem("y_st"), sem("yr_ld"))
        prep_v, prep_a, a_ok = sem("prep_v"), sem("prep_a"), sem("a_ok")

        def rows_of(ap, b):
            return ap[bass.ds(b * T, T), :].rearrange("(k p) d -> p k d", p=P)

        y_dram = (io["y_even"], io["y_odd"])

        def first(b):
            return isinstance(b, int) and b == 0

        def early(b):
            return isinstance(b, int) and b < 2

        def batches(eng, body):
            body(0, 0, False, True)
            with eng.Fori(0, (B - 2) // 2) as pair:
                body(pair * 2 + 1, 1, True, True)
                body(pair * 2 + 2, 0, True, True)
            body(B - 1, (B - 1) % 2, True, False)

        passed_v, passed_p = sem("passed_v"), sem("passed_p")

        with nc.Block(f"layer{layer}") as block:
            @block.sync
            def _(sp):
                for tile, name in ((w_in, "w_in"), (w_x, "w_x"), (w_dt, "w_dt"), (w_out, "w_out")):
                    sp.dma_start(tile[:], io[f"{L}_{name}"]).then_inc(w_ld, 16)
                sp.dma_start(gate[:].rearrange("p b d -> p (b d)"),
                             io["gates"][(0 if layer == 1 else 1):(1 if layer == 1 else 2), :, :].rearrange("l b d -> l (b d)").to_broadcast([P, B * D])).then_inc(w_ld, 16)
                if gathered:
                    sp.dma_start(idx_x[:], io["idx"]).then_inc(idx_ld, 16)
                    sp.dma_start(idx[:], io["idx"]).then_inc(idx_ld, 16)

                def load_x(b):
                    if not gathered:
                        if not first(b):
                            sp.wait_ge(xn_tr, b * DH)
                        sp.dma_start(x_in[:], rows_of(src, b)).then_inc(x_ld, 16)

                def c_out(b, p):
                    sp.wait_ge(xd_ok, b + 1)
                    sp.dma_start(io["c_rows"][p, :, :], x_dbl[R + N:XD, p, :]).then_inc(c_st, 16)

                def c_load(b, p, g):
                    if not (g < 2 and first(b)):
                        sp.wait_ge(hc_ok, b * UNITS + (g - 1) * C_GROUP * JB + CREDIT)
                    sp.dma_start(c_all[:, g % 2, :, :].rearrange("p n t -> p (n t)"),
                                 io["c_rows"][p, g * C_GROUP:(g + 1) * C_GROUP, :].rearrange("(o n) t -> o (n t)", o=1).to_broadcast([P, C_GROUP * T])
                                 ).then_inc(c_ld[g % 2], 16)

                def res_load(b):
                    sp.wait_ge(stored, b * 16 + 16)
                    sp.dma_start(res[:], rows_of(src, b)).then_inc(res_ld, 16)

                def out(b):
                    sp.wait_ge(res_ok, b * res_steps + res_steps + CREDIT)
                    sp.dma_start(rows_of(dst, b), res[:]).then_inc(stored, 16)

                def body(b, p, has_post, has_prep):
                    if has_prep:
                        load_x(b + 1)
                    if has_post:
                        res_load(b - 1)
                        if gathered:
                            for tp in range(OUT_PARTS):
                                y_store(b - 1, 1 - p, tp)
                    c_load(b, p, 2)
                    if has_post:
                        out(b - 1)
                    c_load(b, p, 3)
                    if has_prep:
                        c_out(b + 1, 1 - p)
                        sp.wait_ge(c_st, b * 16 + 32)
                        c_load(b + 1, 1 - p, 0)
                        c_load(b + 1, 1 - p, 1)

                def y_store(b, p, tp):
                    sp.wait_ge(og_ok, b * OUT_PARTS + tp + 1)
                    sp.dma_start(y_dram[p][tp * 2 * P:(tp + 1) * 2 * P, :].rearrange("(k p) d -> p k d", p=P), og[:, tp, :, :]).then_inc(y_st, 16)

                sp.sem_inc(stored, 16)
                sp.sem_inc(y_st, 16)
                load_x(0)
                c_out(0, 0)
                sp.wait_ge(c_st, 16)
                c_load(0, 0, 0)
                c_load(0, 0, 1)
                batches(sp, body)
                res_load(B - 1)
                if gathered:
                    for tp in range(OUT_PARTS):
                        y_store(B - 1, (B - 1) % 2, tp)
                out(B - 1)
                sp.wait_ge(stored, 16 * B + 16)

            @block.scalar
            def _(act):
                act.preload_act_table_set(EXP_LN)
                act.activation(a_neg[:], vec(vecs, L + "_A_log"), ACT.Exp).then_inc(a_exp_ok, 1)
                act.wait_ge(a_ok, 1)

                def ln_rstd(b):
                    chain = Chain(act, prep_a, 2, b)
                    act.wait_ge(mom_ok, b + 1)
                    chain.link(act.activation(rstd[:], moments[:, :, 1], ACT.Ln, bias=eps[:]))
                    act.activation(rstd[:], rstd[:], ACT.Exp, scale=-0.5).then_inc(rstd_ok, 1)
                    return chain

                def mod(b, half):
                    act.wait_ge(xn_tr, b * DH + half + 1)
                    act.activation(modT[:, half, :], misc[:], ACT.Identity, scale=coef[:, li, 0, half, bass.ds(b, 1)],
                                   bias=coef[:, li, 1, half, bass.ds(b, 1)]).then_inc(mod_ok, 1)

                def x_part(b, j):
                    act.wait_ge(in_mm, b * 2 * JB + j + 1)
                    act.activation(conv_in[:, j, TAPS - 1:], misc[:], ACT.Copy).then_inc(xc_ok, 1)

                def z_part(b, p, j):
                    act.wait_ge(in_mm, b * 2 * JB + JB + j + 1)
                    if j == 0:
                        if not early(b):
                            act.wait_ge(yg_ok, b * JB - JB)
                    act.activation(z[:, p, j, :], misc[:], ACT.Copy).then_inc(z_ok, 1)

                def silus(b, p):
                    act.wait_ge(conv_ok, b * JB + JB)
                    act.activation(u[:, p, :, :], work[:], ACT.Silu).then_inc(u_ok, 1)
                    act.wait_ge(z_ok, b * JB + JB)
                    act.activation(z[:, p, :, :], z[:, p, :, :], ACT.Silu).then_inc(u_ok, 1)
                    act.preload_act_table_set(EXP_LN)

                def xd(b, p):
                    act.wait_ge(xd_mm, b + 1)
                    if not early(b):
                        act.wait_ge(c_st, b * 16 - 16)
                    act.activation(x_dbl[:, p, :], misc[0:XD, :], ACT.Copy).then_inc(xd_ok, 1)

                def dt_raw(b, j):
                    act.wait_ge(dt_mm, b * JB + j + 1)
                    act.activation(dt_in[:, j, :], misc[:], ACT.Identity, bias=vec(vecs, L + "_dt_b")[:, j:j + 1]).then_inc(dti_ok, 1)

                def softplus(b):
                    act.wait_ge(clip_ok, b + 1)
                    act.activation(work[:], work[:], ACT.Exp).then_inc(prep_a, 1)
                    act.wait_ge(prep_a, b * 2 + 2)
                    act.activation(work[:], work[:], ACT.Ln, bias=1.0).then_inc(ln_ok, 1)

                def du_tok(b, p, t):
                    act.wait_ge(duT_tr, b * TB + t + 1)
                    act.activation(duT[:, p, t, :], misc[:], ACT.Copy).then_inc(duT_ok, 1)

                def prep_step(s, b, p):
                    if s == 8: ln_rstd(b)
                    if s in (15, 17): mod(b, (s - 15) // 2)
                    if s in (20, 22, 24, 26): x_part(b, (s - 20) // 2)
                    if s in (28, 30, 32, 34): z_part(b, p, (s - 28) // 2)
                    if s == 35: silus(b, p)
                    if s == 38: xd(b, p)
                    if s in (43, 45, 47, 49): dt_raw(b, (s - 43) // 2)
                    if s == 52: softplus(b)
                    if s in (57, 59, 61, 63): du_tok(b, p, (s - 57) // 2)

                def scale_rows(p, n, t):
                    return act.activation(dub[:, n % 2, t, :], duT[:, p, t, :], ACT.Copy, scale=b_tok[:, p, t, n:n + 1])

                def body(b, p, has_post, has_prep):
                    act.wait_ge(duT_ok, b * TB + TB)
                    act.wait_ge(b_ok, b + 1)
                    act.wait_ge(dbu_ok, b * UNITS - JB + CREDIT)
                    for t in range(TB):
                        last = scale_rows(p, 0, t)
                    last.then_inc(dub_ok, 1)
                    act.wait_ge(dt_ok, b + 1)
                    for s in range(UNITS):
                        n, j = s // JB, s % JB
                        act.wait_ge(scan_ok, b * UNITS + s + 1 - DA_RING + CREDIT)
                        act.activation(dA[:, s % DA_RING, :], dt[:, p, j, :], ACT.Exp, scale=a_neg[:, j * N + n:j * N + n + 1]).then_inc(da_ok, 1)
                        if n + 1 < N:
                            if j == 0:
                                act.wait_ge(dbu_ok, b * UNITS + n * JB + CREDIT)
                            last = scale_rows(p, n + 1, j)
                            if j == TB - 1:
                                last.then_inc(dub_ok, 1)
                        if has_prep:
                            prep_step(s, b + 1, 1 - p)

                for s in range(UNITS):
                    prep_step(s, 0, 0)
                batches(act, body)

            @block.vector
            def _(dve):
                dve.memset(conv_in[:, :, 0:TAPS - 1], 0.0).then_inc(pad_ok, 1)
                dve.sem_inc(scan_ok, CREDIT)
                dve.sem_inc(add_ok, CREDIT)
                dve.wait_ge(pad_ok, 1)
                dve.wait_ge(w_ld, 16 * 5)
                dve.wait_ge(a_exp_ok, 1)
                dve.tensor_scalar(a_neg[:], a_neg[:], -1.0, None, ALU.mult).then_inc(a_ok, 1)

                def ln_stats(b):
                    dve.wait_ge(x_ld, (b + 1) * 16 * x_loads)
                    for t in range(TB):
                        last = dve.bn_stats(stats[:, t, :], x_in[:, t, :])
                    last.then_inc(prep_v, 1)
                    dve.wait_ge(prep_v, b * PREP_V + 1)
                    dve.sem_inc(passed_v, 1)
                    for t in range(TB):
                        last = dve.bn_aggr(moments[:, t, :], stats[:, t, :])
                    last.then_inc(mom_ok, 1)

                def ln_apply(b):
                    dve.wait_ge(rstd_ok, b + 1)
                    for t in range(TB):
                        last = dve.tensor_scalar(x_in[:, t, :], x_in[:, t, :], moments[:, t, 0:1], rstd[:, t:t + 1], ALU.subtract, ALU.mult)
                    last.then_inc(xn_ok, 1)

                def conv(b, j):
                    dve.wait_ge(xc_ok, b * JB + j + 1)
                    if j == 0 and not first(b):
                        dve.wait_ge(dt_ok, b)
                    wcol = VEC_LAYOUT[L + "_conv_w"][0] + j * TAPS
                    dve.tensor_scalar(work[:, j, :], conv_in[:, j, 0:T], vecs[:, wcol:wcol + 1],
                                      vec(vecs, L + "_conv_b")[:, j:j + 1], ALU.mult, ALU.add).then_inc(prep_v, 1)
                    for k in range(1, TAPS):
                        dve.wait_ge(prep_v, b * PREP_V + 1 + j * (TAPS - 1) + k)
                        last = dve.scalar_tensor_tensor(work[:, j, :], conv_in[:, j, k:k + T], vecs[:, wcol + k:wcol + k + 1], work[:, j, :],
                                                        ALU.mult, ALU.add)
                        last.then_inc(prep_v if k < TAPS - 1 else conv_ok, 1)

                def b_copy(b, p):
                    dve.wait_ge(b_tr, b + 1)
                    dve.tensor_copy(b_tok[:, p, :, :], misc[:, 0:TB * XD].rearrange("p (t c) -> p t c", c=XD)[:, :, R:R + N]).then_inc(b_ok, 1)

                def clip(b):
                    dve.wait_ge(dti_ok, b * JB + JB)
                    dve.wait_ge(u_ok, b * 2 + 1)
                    dve.tensor_scalar(work[:], dt_in, 30.0, None, ALU.min).then_inc(clip_ok, 1)

                def dt_du(b, p):
                    dve.wait_ge(ln_ok, b + 1)
                    dve.tensor_tensor(dt[:, p, :, :], dt_in, work[:], ALU.max).then_inc(dt_ok, 1)
                    dve.wait_ge(dt_ok, b + 1)
                    dve.tensor_tensor(dt_in, dt[:, p, :, :], u[:, p, :, :], ALU.mult).then_inc(du_ok, 1)

                def y_skip(b, p, j):
                    dve.wait_ge(sum_ok, b * PAIRED + PAIRED - JB + j + 1 + CREDIT)
                    if j == 0:
                        dve.wait_ge(out_mm, b * OUT_PARTS + 1)
                    dve.scalar_tensor_tensor(y[:, j, :], u[:, p, j, :], vec(vecs, L + "_D")[:, j:j + 1], ps_y[:, j, :], ALU.mult, ALU.add).then_inc(y_ok, 1)

                def add_states(b, s):
                    if s // JB % 2:
                        q, s0 = pair_of(s)
                        dve.wait_ge(hc_ok, b * UNITS + s + 1 + CREDIT)
                        dve.tensor_tensor(h[:, h_slot(s0), :], h[:, h_slot(s0), :], h[:, h_slot(s), :], ALU.add).then_inc(add_ok, 1)

                def out_gate(b, tp):
                    dve.wait_ge(out_mm, b * OUT_PARTS + tp + 2)
                    if gathered:
                        dve.wait_ge(y_st, b * OUT_PARTS * 16 + 16)
                    else:
                        dve.wait_ge(res_ok, b * OUT_PARTS + CREDIT)
                    dve.tensor_tensor(og[:, tp, :, :], misc[:].rearrange("p (k d) -> p k d", d=D),
                                      gate[:, bass.ds(b, 1), :].to_broadcast([P, 2, D]), ALU.mult).then_inc(og_ok, 1)

                def prep_step(s, b, p):
                    if s == 6: ln_stats(b)
                    if s == 10: ln_apply(b)
                    if s in (21, 23, 25, 27): conv(b, (s - 21) // 2)
                    if s == 41: b_copy(b, p)
                    if s == 51: clip(b)
                    if s == 54: dt_du(b, p)

                def post_step(s, b, p):
                    if s < ADD_LAG: add_states(b, UNITS - ADD_LAG + s)
                    if s in (4, 5, 6, 7): y_skip(b, p, s - 4)
                    if s in (12, 14): out_gate(b, (s - 12) // 2)

                def body(b, p, has_post, has_prep):
                    for s in range(UNITS):
                        if has_post:
                            post_step(s, b - 1, 1 - p)
                        dve.wait_ge(da_ok, b * UNITS + s + 1)
                        dve.wait_ge(dbu_ok, b * UNITS + s + 1 + CREDIT)
                        if s // JB % 2:
                            dve.wait_ge(add_ok, b * PAIRED + pair_of(s)[0] - JB + 1 + CREDIT)
                        else:
                            dve.wait_ge(sum_ok, b * PAIRED + pair_of(s + JB)[0] - 2 * JB + 1 + CREDIT)
                        dve.tensor_tensor_scan(h[:, h_slot(s), :], dA[:, s % DA_RING, :], ps_dbu[:, dbu_slot(s), :],
                                               0.0, ALU.mult, ALU.add).then_inc(scan_ok, 1)
                        if s >= ADD_LAG:
                            add_states(b, s - ADD_LAG)
                        if has_prep:
                            prep_step(s, b + 1, 1 - p)

                for s in range(UNITS):
                    prep_step(s, 0, 0)
                batches(dve, body)
                for s in range(16):
                    post_step(s, B - 1, (B - 1) % 2)

            @block.gpsimd
            def _(pool):
                pool.sem_inc(hc_ok, CREDIT)
                pool.sem_inc(res_ok, CREDIT)
                if gathered:
                    pool.wait_ge(idx_ld, 32)

                def gather_x(b):
                    if not first(b):
                        pool.wait_ge(xn_tr, b * DH)
                        pool.sem_inc(passed_p, 1)
                        pool.tensor_scalar(idx_x[:], idx_x[:], float(T), None, ALU.add).then_inc(idx_ok, 1)
                        pool.wait_ge(idx_ok, b)
                        pool.sem_inc(passed_p, 1)
                    for t in range(TB):
                        pool.indirect_dma_start(x_in[:, t, :], None, src[:, :], bass.IndirectOffsetOnAxis(ap=idx_x[:, t:t + 1], axis=0)).then_inc(x_ld, 16)

                def silu_gate(b, p, j):
                    if j == 0:
                        pool.wait_ge(u_ok, b * 2 + 2)
                    pool.wait_ge(y_ok, b * JB + j + 1)
                    pool.tensor_tensor(y[:, j, :], y[:, j, :], z[:, p, j, :], ALU.mult).then_inc(yg_ok, 1)

                def residual(b, tp):
                    pool.wait_ge(og_ok, b * OUT_PARTS + tp + 1)
                    if tp == 0:
                        pool.wait_ge(res_ld, b * 16 + 16)
                    pool.tensor_tensor(res[:, 2 * tp:2 * tp + 2, :], res[:, 2 * tp:2 * tp + 2, :], og[:, tp, :, :], ALU.add).then_inc(res_ok, 1)

                def gather_y(b, p):
                    pool.wait_ge(y_st, b * OUT_PARTS * 16 + OUT_PARTS * 16 + 16)
                    pool.wait_ge(res_ok, b + CREDIT)
                    pool.sem_inc(passed_p, 1)
                    for t in range(TB):
                        pool.indirect_dma_start(y_rows[:, t, :], None, y_dram[p], bass.IndirectOffsetOnAxis(ap=idx[:, t:t + 1], axis=0)).then_inc(yr_ld, 16)

                def residual_rows(b):
                    pool.wait_ge(yr_ld, (b + 1) * 16 * TB)
                    pool.wait_ge(res_ld, b * 16 + 16)
                    pool.tensor_tensor(res[:], res[:], y_rows[:], ALU.add).then_inc(res_ok, 1)

                def body(b, p, has_post, has_prep):
                    for s in range(UNITS):
                        if gathered and has_prep and s == 0: gather_x(b + 1)
                        if gathered and has_post and s == 18: gather_y(b - 1, 1 - p)
                        if gathered and has_post and s == 26: residual_rows(b - 1)
                        if has_post:
                            if s in (6, 7, 8, 9): silu_gate(b - 1, 1 - p, s - 6)
                            if not gathered and s in (13, 15): residual(b - 1, (s - 13) // 2)
                        n, j = s // JB, s % JB
                        if s % (C_GROUP * JB) == 0:
                            g = n // C_GROUP
                            pool.wait_ge(c_ld[g % 2], b * 32 + (g // 2) * 16 + 16)
                        pool.wait_ge(scan_ok, b * UNITS + s + 1 + CREDIT)
                        pool.tensor_tensor(h[:, h_slot(s), :], h[:, h_slot(s), :], c_all[:, (n // C_GROUP) % 2, n % C_GROUP, :], ALU.mult).then_inc(hc_ok, 1)

                if gathered:
                    gather_x(0)
                batches(pool, body)
                for j in range(JB):
                    silu_gate(B - 1, (B - 1) % 2, j)
                if gathered:
                    gather_y(B - 1, (B - 1) % 2)
                    residual_rows(B - 1)
                else:
                    for tp in range(OUT_PARTS):
                        residual(B - 1, tp)

            @block.tensor
            def _(pe):
                pe.wait_ge(w_ld, 16 * 5)
                pe.sem_inc(dbu_ok, CREDIT)
                pe.sem_inc(sum_ok, CREDIT)
                pe.sem_inc(out_mm, 1)

                def xn_half(b, half, after_post):
                    pe.wait_ge(xn_ok, b + 1)
                    if half:
                        pe.wait_ge(mod_ok, b * DH + 1)
                    elif after_post:
                        pe.wait_ge(og_ok, b * OUT_PARTS - OUT_PARTS)
                    elif not first(b):
                        pe.wait_ge(duT_ok, b * TB)
                    for t in range(TB):
                        last = pe.transpose(misc[:, t * P:(t + 1) * P], x_in[:, t, half * P:(half + 1) * P], ident[:])
                    last.then_inc(xn_tr, 1)

                def in_proj(b, e):
                    if e == 0:
                        pe.wait_ge(mod_ok, b * DH + DH)
                    elif e <= JB:
                        pe.wait_ge(xc_ok, b * JB + e)
                    else:
                        pe.wait_ge(z_ok, b * JB + e - JB)
                    for k in range(DH):
                        last = pe.matmul(misc[:], w_in[:, k, e * P:(e + 1) * P], modT[:, k, :], start=(k == 0), stop=(k == DH - 1))
                    last.then_inc(in_mm, 1)

                def x_proj(b, p):
                    pe.wait_ge(u_ok, b * 2 + 1)
                    pe.wait_ge(z_ok, b * JB + JB)
                    for k in range(JB):
                        last = pe.matmul(misc[0:XD, :], w_x[:, k, :], u[:, p, k, :], start=(k == 0), stop=(k == JB - 1))
                    last.then_inc(xd_mm, 1)

                def b_turn(b, p):
                    pe.wait_ge(xd_ok, b + 1)
                    for t in range(TB):
                        last = pe.transpose(misc[:, t * XD:(t + 1) * XD], x_dbl[:, p, t * P:(t + 1) * P], ident[0:XD, 0:XD])
                    last.then_inc(b_tr, 1)

                def dt_proj(b, p, j):
                    if j == 0:
                        pe.wait_ge(b_ok, b + 1)
                    else:
                        pe.wait_ge(dti_ok, b * JB + j)
                    pe.matmul(misc[:], w_dt[:, j * P:(j + 1) * P], x_dbl[0:R, p, :], start=True, stop=True).then_inc(dt_mm, 1)

                def du_turn(b, t):
                    pe.wait_ge(du_ok, b + 1)
                    if t == 0:
                        pe.wait_ge(dti_ok, b * JB + JB)
                    else:
                        pe.wait_ge(duT_ok, b * TB + t)
                    for j in range(JB):
                        last = pe.transpose(misc[:, j * P:(j + 1) * P], dt_in[:, j, t * P:(t + 1) * P], ident[:])
                    last.then_inc(duT_tr, 1)

                def out_proj(b, tp):
                    pe.wait_ge(yg_ok, b * JB + JB)
                    if tp == 0:
                        if not (isinstance(b, int) and b == B - 1):
                            pe.wait_ge(duT_ok, b * TB + 2 * TB)
                    else:
                        pe.wait_ge(og_ok, b * OUT_PARTS + tp)
                    for i in range(2):
                        t = 2 * tp + i
                        for k in range(JB):
                            last = pe.matmul(misc[:, i * D:(i + 1) * D], y[:, k, t * P:(t + 1) * P], w_out[:, k, :], start=(k == 0), stop=(k == JB - 1))
                    last.then_inc(out_mm, 1)

                def prep_step(s, b, p, after_post):
                    if s in (14, 16): xn_half(b, (s - 14) // 2, after_post)
                    if s in (19, 21, 23, 25): in_proj(b, (s - 19) // 2)
                    if s in (27, 29, 31, 33): in_proj(b, JB + (s - 27) // 2)
                    if s == 37: x_proj(b, p)
                    if s == 40: b_turn(b, p)
                    if s in (42, 44, 46, 48): dt_proj(b, p, (s - 42) // 2)
                    if s in (56, 58, 60, 62): du_turn(b, (s - 56) // 2)

                def sum_states(b, s):
                    n, j = s // JB, s % JB
                    if n % 2:
                        q, s0 = pair_of(s)
                        if q < JB and not first(b):
                            pe.wait_ge(y_ok, b * JB - JB + j + 1)
                        pe.wait_ge(add_ok, b * PAIRED + q + 1 + CREDIT)
                        pe.matmul(ps_y[:, j, :], ident[:], h[:, h_slot(s0), :], start=(q < JB), stop=(n == N - 1), skip_group_check=True).then_inc(sum_ok, 1)

                def body(b, p, has_post, has_prep):
                    for s in range(UNITS):
                        n, j = s // JB, s % JB
                        if s >= SUM_LAG:
                            sum_states(b, s - SUM_LAG)
                        elif has_post:
                            sum_states(b - 1, UNITS - SUM_LAG + s)
                        if j == 0:
                            pe.wait_ge(dub_ok, b * N + n + 1)
                        pe.wait_ge(scan_ok, b * UNITS + s + 1 - dbu_back(s) + CREDIT)
                        for t in range(TB):
                            last = pe.transpose(ps_dbu[:, dbu_slot(s), t * P:(t + 1) * P], dub[:, n % 2, t, j * P:(j + 1) * P], ident[:])
                        last.then_inc(dbu_ok, 1)
                        if has_post and s in (11, 13):
                            out_proj(b - 1, (s - 11) // 2)
                        if has_prep:
                            prep_step(s, b + 1, 1 - p, has_post)

                for s in range(UNITS):
                    prep_step(s, 0, 0, False)
                batches(pe, body)
                for s in range(UNITS - SUM_LAG, UNITS):
                    sum_states(B - 1, s)
                for tp in range(OUT_PARTS):
                    out_proj(B - 1, tp)
        sems.clear(f"layer{layer}_clear")


PAIRS = H2 // 2
GROUPS = 4
GH = H2 // GROUPS
GU = 2 * TB
V_COLS = P // GH
RING = 2
Q_PARTS = (0, 0, 1, 1, 0, 2)
K_PARTS = (0, 1, 0, 1, 2, 0)
MASK_AT = len(Q_PARTS) * W2
MAX_AT = MASK_AT + 3
STACK = MAX_AT + 3
HALF_USES = PAIRS * TB // 2


def softmax_attention(nc, io, keep):
    with ExitStack() as ctx:
        sb = lambda name, shape, dt=F32: ctx.enter_context(nc.sbuf_tensor("l2_" + name, shape, dt))
        sems = Semaphores(nc, ctx)
        sem = lambda name: sems("l2_" + name)
        vecs, ident, ones, eps, coef = (keep[k] for k in ("vecs", "ident", "ones", "eps", "coef"))
        rows = sb("rows", [1, len(ROWS) * D])
        w = sb("w", [P, DH, 4 * D])
        wq, wk, wv, wo = (w[:, :, i * D:(i + 1) * D] for i in range(4))
        mask_t = sb("mask_t", [P, B, TB])
        mask_parts = sb("mask_parts", [B, 3, T], BF16)
        x_in = sb("x_in", [P, TB, D])
        xnT = sb("xnT", [P, DH, T])
        stats, moments, rstd = sb("stats", [P, TB, 6]), sb("moments", [P, TB, 2]), sb("rstd", [P, TB])
        stats2, moments2, rstd2 = sb("stats2", [P, TB, 6]), sb("moments2", [P, TB, 2]), sb("rstd2", [P, TB])
        parts = sb("parts", [P, 2, 3, DH, T], BF16)
        rest = sb("rest", [P, T])
        qs, ks = sb("qs", [STACK, 2, H2, T], BF16), sb("ks", [STACK, 2, H2, T], BF16)
        v = sb("v", [P, 2, TB, H2, V_COLS])
        q_max = sb("q_max", [P, GROUPS, GH, TB])
        m_parts = sb("m_parts", [GH * TB, GROUPS, 3, P], BF16)
        m_rest = sb("m_rest", [GH * TB, P])
        probs = sb("probs", [P, 2 * GH // 2, 2, TB, T])
        mask_all, mask_add = probs[0:B, 0, 0, 0, :], probs[0:B, 0, 0, 1, :]
        yT = sb("yT", [P, T])
        inv_sum = sb("inv_sum", [P, TB, GH])
        y = sb("y", [P, TB, D])
        hT = sb("hT", [P, DH, T])
        res = sb("res", [P, TB, D])
        ring = ctx.enter_context(nc.psum_tensor("l2_ring", [P, RING, 2, T], F32))
        ps_y = ctx.enter_context(nc.psum_tensor("l2_ps_y", [P, T], F32))
        ps_x, ps_s, ps_o = (ctx.enter_context(nc.psum_tensor("l2_" + name, [P, T], F32)) for name in ("ps_x", "ps_s", "ps_o"))

        w_ld, fill_ok, mask_ok, mask_p1, mask_p2, mask_p3, mask_st = (
            sem("w_ld"), sem("fill"), sem("mask"), sem("mask_p1"), sem("mask_p2"), sem("mask_p3"), sem("mask_st"))
        x_ld, mom_ok, rstd_ok, xn_ok, xn_tr, xnT_ok = sem("x_ld"), sem("mom"), sem("rstd"), sem("xn"), sem("xn_tr"), sem("xnT")
        qk_mm, p1_ok, rest_ok, p2_ok, p3_ok, parts_st, stack_ld = (
            sem("qk_mm"), sem("p1"), sem("rest"), sem("p2"), sem("p3"), sem("parts_st"), sem("stack_ld"))
        v_mm, v_ok = sem("v_mm"), sem("v")
        s_mm, smax_ok, m_tr, m1_ok, mr_ok, m2p_ok, m3_ok, exp_mm, exp_ok, pv_ok, yt_ok, y_tr, y_ok, inv_ok = (
            sem("s_mm"), sem("smax"), sem("m_tr"), sem("m1"), sem("mr"), sem("m2p"), sem("m3"), sem("exp_mm"), sem("exp"), sem("pv"),
            sem("yt"), sem("y_tr"), sem("y"), sem("inv"))
        m_ld = [sem(f"m_ld{g}") for g in range(GROUPS)]
        st2_ok, mom2_ok, rstd2_ok, yn_ok, yn_tr, hT_ok, o_mm, res_ld, res_ok, stored = (
            sem("st2"), sem("mom2"), sem("rstd2"), sem("yn"), sem("yn_tr"), sem("hT"), sem("o_mm"), sem("res_ld"), sem("res"), sem("stored"))
        st_ok, ln_a, ln_b, passed = sem("st"), sem("ln_a"), sem("ln_b"), sem("passed")
        OUT = TB // 2

        def row(name):
            r = ROWS.index(name)
            return rows[:, r * D:(r + 1) * D]

        def rows_of(ap, b):
            return ap[bass.ds(b * T, T), :].rearrange("(k p) d -> p k d", p=P)

        y_tok = ps_s[:].rearrange("p (t h c) -> p t h c", h=GH, c=V_COLS)

        def first(b):
            return isinstance(b, int) and b == 0

        def early(b):
            return isinstance(b, int) and b < 2

        def batches(body):
            def one(eng):
                body(0, 0, False, True, True)
                with eng.Fori(0, 2) as two:
                    body(two * 2 + 1, 1, True, True, True)
                    body(two * 2 + 2, 0, True, True, True)
                body(B - 3, (B - 3) % 2, True, True, True)
                body(B - 2, (B - 2) % 2, True, True, False)
                body(B - 1, (B - 1) % 2, True, False, False)
            return one

        with nc.Block("layer2") as block:
            @block.sync
            def _(sp):
                sp.dma_start(w[:], io["L2_w"]).then_inc(w_ld, 16)
                sp.dma_start(mask_t[:], io["mask2_t"]).then_inc(w_ld, 16)
                sp.dma_start(mask_all, io["mask2_k"]).then_inc(w_ld, 16)
                sp.dma_start(rows[:], io["rows"]).then_inc(w_ld, 16)
                sp.sem_inc(stored, 16)

                def load_x(b):
                    if not first(b):
                        sp.wait_ge(xn_tr, b * DH)
                    sp.dma_start(x_in[:], rows_of(io["x2"], b)).then_inc(x_ld, 16)

                def parts_out(b, p):
                    sp.wait_ge(p3_ok, b * 2 * DH + 2 * DH)
                    for i in range(2):
                        for a in range(3):
                            sp.dma_start(io["parts"][p, i, a, :, :].rearrange("(g p) t -> p g t", p=P), parts[:, i, a, :, :]).then_inc(parts_st, 16)

                def stack(b, p):
                    sp.wait_ge(parts_st, b * 96 + 96)
                    if not early(b):
                        sp.wait_ge(exp_ok, (b - 1) * PAIRS * TB + RING)
                    for i, (dst, order) in enumerate(((qs, Q_PARTS), (ks, K_PARTS))):
                        for s, a in enumerate(order):
                            sp.dma_start(dst[s * W2:(s + 1) * W2, p, :, :], io["parts"][p, i, a, :, :].rearrange("(h c) t -> c h t", c=W2)).then_inc(stack_ld, 16)
                    sp.dma_start(ks[MASK_AT:MASK_AT + 3, p, :, :], io["mask_parts"][bass.ds(b, 1), :, :].rearrange("b a t -> a b t").to_broadcast([3, H2, T])).then_inc(stack_ld, 16)

                def max_out(b, p, g):
                    sp.wait_ge(m3_ok, b * GROUPS + g + 1)
                    for a in range(3):
                        sp.dma_start(qs[MAX_AT + a:MAX_AT + a + 1, p, g * GH:(g + 1) * GH, :].rearrange("o h (t n) -> o (h t) n", n=P),
                                     m_parts[:, g, a, :]).then_inc(m_ld[g], 16)

                def res_load(b):
                    sp.wait_ge(stored, b * 16 + 16)
                    sp.dma_start(res[:], rows_of(io["x2"], b)).then_inc(res_ld, 16)

                def out(b):
                    sp.wait_ge(res_ok, b * OUT + OUT)
                    sp.dma_start(rows_of(io["x3"], b), res[:]).then_inc(stored, 16)

                @batches
                def run(b, p, has_post, has_next, has_after):
                    if has_after:
                        load_x(b + 2)
                    if has_post:
                        res_load(b - 1)
                    max_out(b, p, 1)
                    if has_next:
                        stack(b + 1, 1 - p)
                    max_out(b, p, 2)
                    if has_post:
                        out(b - 1)
                    max_out(b, p, 3)
                    if has_next:
                        max_out(b + 1, 1 - p, 0)
                    if has_after:
                        parts_out(b + 2, p)

                load_x(0)
                sp.wait_ge(mask_p3, 1)
                sp.dma_start(io["mask_parts"], mask_parts[:]).then_inc(mask_st, 16)
                sp.wait_ge(mask_st, 16)
                parts_out(0, 0)
                load_x(1)
                sp.wait_ge(fill_ok, 4)
                stack(0, 0)
                parts_out(1, 1)
                max_out(0, 0, 0)
                run(sp)
                res_load(B - 1)
                out(B - 1)
                sp.wait_ge(stored, 16 * B + 16)

            @block.gpsimd
            def _(pool):
                pool.memset(qs[MASK_AT:STACK, :, :, :], 1.0).then_inc(fill_ok, 1)
                pool.wait_ge(fill_ok, 1)
                pool.memset(ks[MASK_AT:STACK, :, :, :], -1.0).then_inc(fill_ok, 1)
                for p in range(2):
                    pool.wait_ge(fill_ok, 2 + p)
                    pool.memset(v[:, p, :, :, W2:V_COLS], 1.0).then_inc(fill_ok, 1)

            @block.vector
            def _(dve):
                dve.sem_inc(smax_ok, RING)
                dve.wait_ge(w_ld, 64)
                dve.tensor_scalar(mask_add, mask_all, 1.0, MASKED, ALU.subtract, ALU.mult).then_inc(mask_ok, 1)
                dve.wait_ge(mask_ok, 1)
                dve.tensor_copy(mask_parts[:, 0, :], mask_add).then_inc(mask_p1, 1)
                dve.wait_ge(mask_p1, 1)
                dve.tensor_tensor(mask_add, mask_add, mask_parts[:, 0, :], ALU.subtract).then_inc(mask_ok, 1)
                dve.wait_ge(mask_ok, 2)
                dve.tensor_copy(mask_parts[:, 1, :], mask_add).then_inc(mask_p2, 1)
                dve.wait_ge(mask_p2, 1)
                dve.tensor_tensor(mask_parts[:, 2, :], mask_add, mask_parts[:, 1, :], ALU.subtract).then_inc(mask_p3, 1)

                def ln_stats(b):
                    dve.wait_ge(x_ld, b * 16 + 16)
                    for t in range(TB):
                        last = dve.bn_stats(stats[:, t, :], x_in[:, t, :])
                    last.then_inc(st_ok, 1)
                    dve.wait_ge(st_ok, b + 1)
                    dve.sem_inc(passed, 1)
                    for t in range(TB):
                        last = dve.bn_aggr(moments[:, t, :], stats[:, t, :])
                    last.then_inc(mom_ok, 1)

                def ln_apply(b):
                    dve.wait_ge(rstd_ok, b + 1)
                    for t in range(TB):
                        last = dve.tensor_scalar(x_in[:, t, :], x_in[:, t, :], moments[:, t, 0:1], rstd[:, t:t + 1], ALU.subtract, ALU.mult)
                    last.then_inc(xn_ok, 1)

                def split(b, i, g):
                    n = b * 2 * DH + i * DH + g + 1
                    bias = vec(vecs, "L2_q_bias" if i == 0 else "L2_k_bias")[:, g:g + 1]
                    dve.wait_ge(p1_ok, n)
                    if not (first(b) and i + g == 0):
                        dve.wait_ge(p3_ok, n - 1)
                    dve.scalar_tensor_tensor(rest[:], ps_x[:], bias, parts[:, i, 0, g, :], ALU.add, ALU.subtract).then_inc(rest_ok, 1)
                    dve.wait_ge(rest_ok, n)
                    dve.tensor_copy(parts[:, i, 1, g, :], rest[:]).then_inc(p2_ok, 1)
                    dve.wait_ge(p2_ok, n)
                    dve.tensor_tensor(parts[:, i, 2, g, :], rest[:], parts[:, i, 1, g, :], ALU.subtract).then_inc(p3_ok, 1)

                def max_parts(b, g):
                    n = b * GROUPS + g + 1
                    dve.wait_ge(m_tr, n)
                    if not first(b):
                        dve.wait_ge(m_ld[g], b * 48)
                    ps = ps_s[0:GH * TB, 0:P]
                    dve.tensor_copy(m_parts[:, g, 0, :], ps).then_inc(m1_ok, 1)
                    dve.wait_ge(m1_ok, n)
                    if not (first(b) and g == 0):
                        dve.wait_ge(m3_ok, n - 1)
                    dve.tensor_tensor(m_rest[:], ps, m_parts[:, g, 0, :], ALU.subtract).then_inc(mr_ok, 1)
                    dve.wait_ge(mr_ok, n)
                    dve.tensor_copy(m_parts[:, g, 1, :], m_rest[:]).then_inc(m2p_ok, 1)
                    dve.wait_ge(m2p_ok, n)
                    dve.tensor_tensor(m_parts[:, g, 2, :], m_rest[:], m_parts[:, g, 1, :], ALU.subtract).then_inc(m3_ok, 1)

                def maximum(b, u, slot):
                    pair, t = u // TB, u % TB
                    dve.wait_ge(s_mm, b * PAIRS * TB + u + 1)
                    if u % (2 * TB) == 0 and not first(b):
                        dve.wait_ge(m_tr, (b - 1) * GROUPS + pair // 2 + 1)
                    i = 2 * (pair % 2)
                    dve.tensor_reduce(q_max[:, pair // 2, i:i + 2, t], ring[:, slot, :, :], AX.X, ALU.max).then_inc(smax_ok, 1)

                def products_out(b, g):
                    n = b * GROUPS + g
                    dve.wait_ge(pv_ok, n + 1)
                    if not (first(b) and g == 0):
                        dve.wait_ge(y_tr, n)
                    dve.tensor_copy(yT[:], ps_y[:]).then_inc(yt_ok, 1)

                def quotient(b, p, g):
                    n = b * GROUPS + g + 1
                    dve.wait_ge(y_tr, n)
                    if g == 0 and not first(b):
                        dve.wait_ge(yn_tr, b * DH)
                    dve.reciprocal(inv_sum[:], y_tok[:, :, :, W2]).then_inc(inv_ok, 1)
                    dve.wait_ge(inv_ok, n)
                    dve.tensor_tensor(y[:, :, g * GH * W2:(g + 1) * GH * W2].rearrange("p t (h c) -> p t h c", c=W2), y_tok[:, :, :, 0:W2],
                                      inv_sum[:].unsqueeze(3).to_broadcast([P, TB, GH, W2]), ALU.mult).then_inc(y_ok, 1)

                def ln2_stats(b, p):
                    dve.wait_ge(y_ok, b * GROUPS + GROUPS)
                    for t in range(TB):
                        last = dve.bn_stats(stats2[:, t, :], y[:, t, :])
                    last.then_inc(st2_ok, 1)
                    dve.wait_ge(st2_ok, b + 1)
                    dve.sem_inc(passed, 1)
                    for t in range(TB):
                        last = dve.bn_aggr(moments2[:, t, :], stats2[:, t, :])
                    last.then_inc(mom2_ok, 1)

                def ln2_apply(b, p):
                    dve.wait_ge(rstd2_ok, b + 1)
                    for t in range(TB):
                        last = dve.tensor_scalar(y[:, t, :], y[:, t, :], moments2[:, t, 0:1], rstd2[:, t:t + 1], ALU.subtract, ALU.mult)
                    last.then_inc(yn_ok, 1)

                def result(b, t):
                    dve.wait_ge(o_mm, b * OUT + t + 1)
                    dve.wait_ge(res_ld, b * 16 + 16)
                    dve.tensor_tensor(res[:, 2 * t:2 * t + 2, :], ps_o[:].rearrange("p (k d) -> p k d", d=D), res[:, 2 * t:2 * t + 2, :], ALU.add).then_inc(res_ok, 1)

                @batches
                def run(b, p, has_post, has_next, has_after):
                    n = 0
                    for i in range(2 * HALF_USES):
                        n += 1
                        if i < HALF_USES:
                            maximum(b, HALF_USES + i, n % RING)
                            n += 1
                        elif has_next:
                            maximum(b + 1, i - HALF_USES, n % RING)
                            n += 1
                        if i in (14, 22, 30): products_out(b, i // GU - 1)
                        if i in (15, 23, 31): quotient(b, p, i // GU - 1)
                        if i == 2: max_parts(b, 1)
                        if has_post:
                            if i == 6: products_out(b - 1, GROUPS - 1)
                            if i == 7: quotient(b - 1, 1 - p, GROUPS - 1)
                            if i == 8: ln2_stats(b - 1, 1 - p)
                            if i == 10: ln2_apply(b - 1, 1 - p)
                        if i == 10: max_parts(b, 2)
                        if has_post and i in (16, 17): result(b - 1, i - 16)
                        if i == 18: max_parts(b, 3)
                        if has_after:
                            if i == 12: ln_stats(b + 2)
                            if i == 15: ln_apply(b + 2)
                            if i in (20, 21): split(b + 2, 0, i - 20)
                            if i == 22: split(b + 2, 1, 0)
                            if i == 24: split(b + 2, 1, 1)
                        if i == 26 and has_next: max_parts(b + 1, 0)

                def stage_a(b):
                    ln_stats(b)
                    ln_apply(b)
                    for i in range(2):
                        for g in range(DH):
                            split(b, i, g)

                stage_a(0)
                stage_a(1)
                for u in range(HALF_USES):
                    maximum(0, u, u % RING)
                    if u == 10:
                        max_parts(0, 0)
                run(dve)
                products_out(B - 1, GROUPS - 1)
                quotient(B - 1, (B - 1) % 2, GROUPS - 1)
                ln2_stats(B - 1, (B - 1) % 2)
                ln2_apply(B - 1, (B - 1) % 2)
                for t in range(OUT):
                    result(B - 1, t)

            @block.scalar
            def _(act):
                act.wait_ge(w_ld, 64)
                act.preload_act_table_set(EXP_LN)
                act.sem_inc(exp_ok, RING)

                def ln_rstd(b, mom, mom_sem, out, step, ok):
                    act.wait_ge(mom_sem, b + 1)
                    act.activation(out[:], mom[:, :, 1], ACT.Ln, bias=eps[:]).then_inc(step, 1)
                    act.wait_ge(step, b + 1)
                    act.activation(out[:], out[:], ACT.Exp, scale=-0.5).then_inc(ok, 1)

                def xnT_half(b, h):
                    act.wait_ge(xn_tr, b * DH + h + 1)
                    act.activation(xnT[:, h, :], ps_x[:], ACT.Identity, scale=vec(vecs, "L2_ln_w")[:, h:h + 1],
                                   bias=vec(vecs, "L2_ln_b")[:, h:h + 1]).then_inc(xnT_ok, 1)

                def first_part(b, i, g):
                    act.wait_ge(qk_mm, b * 2 * DH + i * DH + g + 1)
                    if i == 0 and g == 0 and not first(b):
                        act.wait_ge(parts_st, b * 96)
                    act.activation(parts[:, i, 0, g, :], ps_x[:], ACT.Identity, bias=vec(vecs, "L2_q_bias" if i == 0 else "L2_k_bias")[:, g:g + 1]).then_inc(p1_ok, 1)

                def v_part(b, p, h):
                    act.wait_ge(v_mm, b * OUT + h + 1)
                    if h == 0 and not early(b):
                        act.wait_ge(pv_ok, (b - 1) * GROUPS)
                    for t in (2 * h, 2 * h + 1):
                        last = act.activation(v[:, p, t, :, 0:W2], ps_x[:, (t % 2) * D:(t % 2 + 1) * D].rearrange("p (h c) -> p h c", c=W2), ACT.Copy,
                                              scale=mask_t[:, bass.ds(b, 1), t])
                    last.then_inc(v_ok, 1)

                def silu_half(b, h):
                    act.wait_ge(yn_tr, b * DH + h + 1)
                    act.activation(hT[:, h, :], ps_o[:], ACT.Silu, scale=coef[:, 2, 0, h, bass.ds(b, 1)],
                                   bias=coef[:, 2, 1, h, bass.ds(b, 1)]).then_inc(hT_ok, 1)
                    if h == DH - 1:
                        act.preload_act_table_set(EXP_LN)

                @batches
                def run(b, p, has_post, has_next, has_after):
                    n = 0
                    for i in range(2 * HALF_USES):
                        pair, t = i // TB, i % TB
                        act.wait_ge(exp_mm, b * PAIRS * TB + i + 1)
                        if i % GU == 0 and not (first(b) and i < 2 * GU):
                            act.wait_ge(pv_ok, b * GROUPS + i // GU - 1)
                        act.activation(probs[:, pair % GH, :, t, :], ring[:, n % RING, :, :], ACT.Exp).then_inc(exp_ok, 1)
                        n += 2 if i < HALF_USES or has_next else 1
                        if has_next and i in (7, 8): v_part(b + 1, 1 - p, i - 7)
                        if has_post:
                            if i == 9: ln_rstd(b - 1, moments2, mom2_ok, rstd2, ln_b, rstd2_ok)
                            if i in (13, 14): silu_half(b - 1, i - 13)
                        if has_after:
                            if i == 14: ln_rstd(b + 2, moments, mom_ok, rstd, ln_a, rstd_ok)
                            if i in (17, 18): xnT_half(b + 2, i - 17)
                            if i in (20, 21): first_part(b + 2, 0, i - 20)
                            if i == 22: first_part(b + 2, 1, 0)
                            if i == 24: first_part(b + 2, 1, 1)

                def stage_a(b):
                    ln_rstd(b, moments, mom_ok, rstd, ln_a, rstd_ok)
                    for h in range(DH):
                        xnT_half(b, h)
                    for i in range(2):
                        for g in range(DH):
                            first_part(b, i, g)

                stage_a(0)
                act.wait_ge(fill_ok, 4)
                for h in range(OUT):
                    v_part(0, 0, h)
                stage_a(1)
                run(act)
                ln_rstd(B - 1, moments2, mom2_ok, rstd2, ln_b, rstd2_ok)
                for h in range(DH):
                    silu_half(B - 1, h)

            @block.tensor
            def _(pe):
                pe.wait_ge(w_ld, 64)
                reader = {}

                def take(bank, ok, value):
                    if bank.name in reader:
                        pe.wait_ge(*reader[bank.name])
                    reader[bank.name] = (ok, value)

                def xn_half(b, h):
                    pe.wait_ge(xn_ok, b + 1)
                    take(ps_x, xnT_ok, b * DH + h + 1)
                    for t in range(TB):
                        last = pe.transpose(ps_x[:, t * P:(t + 1) * P], x_in[:, t, h * P:(h + 1) * P], ident[:])
                    last.then_inc(xn_tr, 1)

                def project(b, i, g):
                    pe.wait_ge(xnT_ok, b * DH + DH)
                    take(ps_x, rest_ok, b * 2 * DH + i * DH + g + 1)
                    weight = wq if i == 0 else wk
                    for k in range(DH):
                        last = pe.matmul(ps_x[:], weight[:, k, g * P:(g + 1) * P], xnT[:, k, :], start=(k == 0), stop=(k == DH - 1))
                    last.then_inc(qk_mm, 1)

                def tokens(bank, src, weight, bias, h):
                    for t in (2 * h, 2 * h + 1):
                        o = bank[:, (t % 2) * D:(t % 2 + 1) * D]
                        for k in range(DH):
                            pe.matmul(o, src[:, k, t * P:(t + 1) * P], weight[:, k, :], start=(k == 0), stop=False)
                        last = pe.matmul(o, ones[0:1, 0:P], row(bias), start=False, stop=True)
                    return last

                def v_rows(b, h):
                    take(ps_x, v_ok, b * OUT + h + 1)
                    tokens(ps_x, xnT, wv, "L2_bv", h).then_inc(v_mm, 1)

                def max_rows(b, g):
                    pe.wait_ge(smax_ok, b * PAIRS * TB + (g + 1) * 2 * TB + RING)
                    take(ps_s, mr_ok, b * GROUPS + g + 1)
                    pe.transpose(ps_s[0:GH * TB, 0:P], q_max[:, g, :, :].rearrange("p h t -> p (h t)"), ident[:]).then_inc(m_tr, 1)

                def yn_half(b, p, h):
                    pe.wait_ge(yn_ok, b + 1)
                    take(ps_o, hT_ok, b * DH + h + 1)
                    for t in range(TB):
                        last = pe.transpose(ps_o[:, t * P:(t + 1) * P], y[:, t, h * P:(h + 1) * P], ident[:])
                    last.then_inc(yn_tr, 1)

                def project_out(b, h):
                    pe.wait_ge(hT_ok, b * DH + DH)
                    take(ps_o, res_ok, b * OUT + h + 1)
                    tokens(ps_o, hT, wo, "L2_b_out", h).then_inc(o_mm, 1)

                def times_v(b, p, g, m):
                    if m == 0:
                        pe.wait_ge(exp_ok, b * PAIRS * TB + (g + 1) * GU + RING)
                        pe.wait_ge(v_ok, b * OUT + OUT)
                        if not (first(b) and g == 0):
                            pe.wait_ge(yt_ok, b * GROUPS + g)
                    for i in range(GH):
                        last = pe.matmul(ps_y[i * V_COLS:(i + 1) * V_COLS, :], v[:, p, m, g * GH + i, :], probs[:, (2 * g + i // 2) % GH, i % 2, m, :],
                                         start=(m == 0), stop=(m == TB - 1))
                    if m == TB - 1:
                        last.then_inc(pv_ok, 1)

                def turn(b, g):
                    pe.wait_ge(yt_ok, b * GROUPS + g + 1)
                    take(ps_s, y_ok, b * GROUPS + g + 1)
                    for t in range(TB):
                        last = pe.transpose(ps_s[:, t * P:(t + 1) * P], yT[:, t * P:(t + 1) * P], ident[:])
                    last.then_inc(y_tr, 1)

                def max_scores(b, p, u, slot):
                    pair, t = u // TB, u % TB
                    if u == 0:
                        pe.wait_ge(stack_ld, (b + 1) * 16 * 13)
                    for i in range(2):
                        hd = 2 * pair + i
                        last = pe.matmul(ring[:, slot, i, :], qs[0:MAX_AT, p, hd, t * P:(t + 1) * P], ks[0:MAX_AT, p, hd, :], start=True, stop=True)
                    last.then_inc(s_mm, 1)

                def exp_scores(b, p, u, slot):
                    pair, t = u // TB, u % TB
                    if u % (2 * TB) == 0:
                        pe.wait_ge(m_ld[pair // 2], b * 48 + 48)
                    for i in range(2):
                        hd = 2 * pair + i
                        last = pe.matmul(ring[:, slot, i, :], ks[:, p, hd, t * P:(t + 1) * P], qs[:, p, hd, :], start=True, stop=True)
                    last.then_inc(exp_mm, 1)

                @batches
                def run(b, p, has_post, has_next, has_after):
                    U = PAIRS * TB
                    uses = []

                    def slot_free(n):
                        if n >= RING:
                            pe.wait_ge(*uses[n - RING])
                        else:
                            pe.wait_ge(exp_ok, b * U + RING)
                            pe.wait_ge(smax_ok, b * U + HALF_USES + RING)

                    if not first(b):
                        reader[ps_s.name] = (y_ok, b * GROUPS - 1)
                        if has_next:
                            reader[ps_x.name] = (rest_ok, b * 2 * DH + 4 * DH)
                    if has_post:
                        if early(b):
                            reader.pop(ps_o.name, None)
                        else:
                            reader[ps_o.name] = (res_ok, b * OUT - OUT)
                    for i in range(U):
                        slot_free(len(uses))
                        exp_scores(b, p, i, len(uses) % RING)
                        uses.append((exp_ok, b * U + i + 1 + RING))
                        if i < HALF_USES or has_next:
                            bb, u = (b, HALF_USES + i) if i < HALF_USES else (b + 1, i - HALF_USES)
                            slot_free(len(uses))
                            max_scores(bb, p if i < HALF_USES else 1 - p, u, len(uses) % RING)
                            uses.append((smax_ok, bb * U + u + 1 + RING))
                        if has_post and 2 <= i < 2 + TB: times_v(b - 1, 1 - p, GROUPS - 1, i - 2)
                        if i >= GU and 2 <= i % GU < 2 + TB: times_v(b, p, i // GU - 1, i % GU - 2)
                        if i == 1: max_rows(b, 1)
                        if has_post and i == 6: turn(b - 1, GROUPS - 1)
                        if has_next and i in (7, 8): v_rows(b + 1, i - 7)
                        if i == 9: max_rows(b, 2)
                        if has_post and i in (12, 13): yn_half(b - 1, 1 - p, i - 12)
                        if i in (14, 22, 30): turn(b, i // GU - 1)
                        if has_post and i in (15, 16): project_out(b - 1, i - 15)
                        if has_after and i == 17: xn_half(b + 2, 0)
                        if i == 17: max_rows(b, 3)
                        if has_after:
                            if i == 18: xn_half(b + 2, 1)
                            if i in (19, 20): project(b + 2, 0, i - 19)
                            if i == 21: project(b + 2, 1, 0)
                            if i == 23: project(b + 2, 1, 1)
                        if has_next and i == 25: max_rows(b + 1, 0)

                def stage_a(b):
                    for h in range(DH):
                        xn_half(b, h)
                    for i in range(2):
                        for g in range(DH):
                            project(b, i, g)

                stage_a(0)
                for h in range(OUT):
                    v_rows(0, h)
                stage_a(1)
                for u in range(HALF_USES):
                    if u >= RING:
                        pe.wait_ge(smax_ok, u + 1)
                    max_scores(0, 0, u, u % RING)
                    if u == 9:
                        max_rows(0, 0)
                run(pe)
                for m in range(TB):
                    times_v(B - 1, (B - 1) % 2, GROUPS - 1, m)
                turn(B - 1, GROUPS - 1)
                for h in range(DH):
                    yn_half(B - 1, (B - 1) % 2, h)
                for h in range(OUT):
                    project_out(B - 1, h)
        sems.clear("layer2_clear")


def build(nc, io):
    with ExitStack() as ctx:
        sb = lambda name, shape: ctx.enter_context(nc.sbuf_tensor(name, shape, F32))
        keep = {
            "vecs": sb("vecs", [P, NVEC]),
            "ident": sb("ident", [P, P]),
            "ones": sb("ones", [1, T]),
            "eps": sb("eps", [P, 1]),
            "coef": sb("coef", [P, 4, 2, DH, B]),
            "x1_stored": [ctx.enter_context(nc.semaphore(f"x1_stored_{p}")) for p in ("even", "odd")],
        }
        setup_block(nc, io, keep)
        linear_attention(nc, io, keep)
        mamba(nc, io, keep, 1, io["x1"], io["x2"], False)
        softmax_attention(nc, io, keep)
        mamba(nc, io, keep, 3, io["x3"], io["out"], True)


def _halves(a, n):
    return np.ascontiguousarray(np.asarray(a).reshape(n, P).T)


def _blocks(a):
    a = np.asarray(a)
    return np.ascontiguousarray(a.reshape(-1, P, a.shape[1]).transpose(1, 0, 2))


def _layout(i):
    f = {k: np.asarray(v) for k, v in i.items()}
    vecs = np.zeros((P, NVEC), np.float32)

    def put(name, a):
        c, n = VEC_LAYOUT[name]
        vecs[:, c:c + n] = a

    for l, ln, ln2, eb in (("L0", "ln", "ln2", "b_emb"), ("L2", "norm", "sb_norm", "emb_b")):
        put(l + "_ln_w", _halves(f[f"{l}_cond_{ln}_w"], DH))
        put(l + "_ln_b", _halves(f[f"{l}_cond_{ln}_b"], DH))
        put(l + "_ln2_w", _halves(f[f"{l}_cond_{ln2}_w"], DH))
        put(l + "_ln2_b", _halves(f[f"{l}_cond_{ln2}_b"], DH))
        put(l + "_scale_b", _halves(f[f"{l}_cond_{eb}"][:D], DH))
        put(l + "_shift_b", _halves(f[f"{l}_cond_{eb}"][D:], DH))
    for name in ("q", "k"):
        put(f"L2_{name}_bias", _halves(f[f"L2_cond_{name}_b"], DH))
    m = {1: ("ln_g", "ln_b", "ada_b", "dt_proj_b"), 3: ("gamma", "beta", "b_ada", "b_dt")}
    for l, (g, bb, ab, db) in m.items():
        c = f"L{l}_cond_"
        put(f"L{l}_ln_w", _halves(f[c + g], DH))
        put(f"L{l}_ln_b", _halves(f[c + bb], DH))
        put(f"L{l}_shift_b", _halves(f[c + ab][:D], DH))
        put(f"L{l}_scale_b", _halves(f[c + ab][D:2 * D], DH))
        put(f"L{l}_conv_b", _halves(f[c + "conv_b"], JB))
        put(f"L{l}_dt_b", _halves(f[c + db], JB))
        put(f"L{l}_D", _halves(f[c + "D_param"], JB))
        put(f"L{l}_conv_w", _blocks(f[c + "conv_w"].reshape(DI, TAPS)).reshape(P, JB * TAPS))
        put(f"L{l}_A_log", _blocks(f[c + "A_log"]).reshape(P, JB * N))
    rows = np.concatenate([f["L0_cond_bq"], f["L0_cond_bk"], f["L0_cond_bv"], f["L0_cond_b_out"], f["L2_cond_v_b"],
                           f["L2_cond_out_b"], f["L1_cond_ada_b"][2 * D:], f["L3_cond_b_ada"][2 * D:]])[None, :]
    cond_w = np.concatenate([f["L0_cond_W_emb"], f["L2_cond_emb_w"], f["L1_cond_ada_w"].T, f["L3_cond_W_ada"]], axis=1)
    out = {
        "x": f["x"].reshape(B * T, D),
        "cond_t": _blocks(f["cond_2048"].T),
        "cond_w": _blocks(cond_w),
        "vecs": vecs,
        "rows": rows,
        "mask_k": f["mask_BxSx1_fk1"].reshape(B, T),
        "mask_t": np.ascontiguousarray(f["mask_BxSx1_fk1"].reshape(B, TB, P).transpose(2, 0, 1)),
        "L0_w": _blocks(np.concatenate([f["L0_cond_Wq"], f["L0_cond_Wk"], f["L0_cond_Wv"], f["L0_cond_W_out"]], axis=1)),
    }
    out["L2_w"] = _blocks(np.concatenate([f[f"L2_cond_{n}_w"] for n in ("q", "k", "v", "out")], axis=1))
    out["mask2_k"] = f["mask_BxS_ff1"]
    out["mask2_t"] = np.ascontiguousarray(f["mask_BxS_ff1"].reshape(B, TB, P).transpose(2, 0, 1))
    for l, names, t in (("L1", ("in_proj_w", "x_proj_w", "dt_proj_w", "out_proj_w"), True), ("L3", ("W_in", "W_xp", "W_dt", "W_out"), False)):
        w = [f[f"{l}_cond_{n}"] for n in names]
        w = [a.T for a in w] if t else w
        out[l + "_w_in"], out[l + "_w_x"], out[l + "_w_dt"], out[l + "_w_out"] = _blocks(w[0]), _blocks(w[1]), w[2], _blocks(w[3])
    out["idx"] = np.ascontiguousarray(f["itok_S_0_1023"].reshape(TB, P).T)
    return {k: np.ascontiguousarray(v) for k, v in out.items()}


def kernel(**inputs):
    import concourse.bacc as _bacc
    from concourse.bass_utils import run_bass_kernel_spmd as _run

    nc = _bacc.Bacc("TRN2", target_bir_lowering=False, num_devices=1)
    arrays, io = {}, {}
    for name, a in _layout(inputs).items():
        arrays[f"in_{name}"] = a
        io[name] = nc.dram_tensor(f"in_{name}", a.shape, mybir.dt.from_np(a.dtype), kind="ExternalInput").ap()
    io["out"] = nc.dram_tensor("out_0_dram", (B * T, D), F32, kind="ExternalOutput").ap()
    for name in ("x1", "x2", "x3"):
        io[name] = nc.dram_tensor(name + "_dram", (B * T, D), F32).ap()
    for name in ("y_even", "y_odd"):
        io[name] = nc.dram_tensor(name + "_dram", (T, D), F32).ap()
    io["parts"] = nc.dram_tensor("parts_dram", (2, 2, 3, D, T), BF16).ap()
    io["mask_parts"] = nc.dram_tensor("mask_parts_dram", (B, 3, T), BF16).ap()
    io["gates"] = nc.dram_tensor("gates_dram", (2, B, D), F32).ap()
    io["c_rows"] = nc.dram_tensor("c_rows_dram", (2, N, T), F32).ap()
    build(nc, io)
    r = _run(nc, [arrays], core_ids=[0])
    return r.results[0]["out_0_dram"].reshape(B, T, D)
```
